# Optimizing a Trainium2 kernel written in Bass

```python
import numpy as np
import jax
import jax.numpy as jnp

def _softmax(x, axis=-1):
    return jax.nn.softmax(x, axis=axis)

def _gelu(x):
    return jax.nn.gelu(x, approximate=True)

def _silu(x):
    return jax.nn.silu(x)

def _sigmoid(x):
    return jax.nn.sigmoid(x)

def _layernorm(x, axis=-1, eps=1e-05):
    m = jnp.mean(x, axis=axis, keepdims=True)
    v = jnp.var(x, axis=axis, keepdims=True)
    return (x - m) / jnp.sqrt(v + eps)

def _scatter_add(tgt, idx, src, axis=0):
    return tgt.at[idx].add(src)

def _segment_sum(src, seg, n):
    return jax.ops.segment_sum(src, seg, n)
kernel_name = 'mk_seq_preln_d1_jaxref_r8_8495e8'

def setup_inputs(seed: int=0):
    np.random.seed(seed)
    _w = jnp.asarray

    def _L0_attn_setup():
        import jax, jax.numpy as jnp
        import numpy as np
        DIM = 256
        DT_RANK = 64
        DIM_INNER = 256
        D_STATE = 32
        B_SZ = 4
        L = 256

        def _selective_scan(u, delta, A, Bm, Cm, D_param):

            def step(h, inp):
                delta_t, B_t, C_t, u_t = inp
                dA = jnp.exp(delta_t[:, :, None] * A[None])
                dBu = (delta_t * u_t)[:, :, None] * B_t[:, None, :]
                h = dA * h + dBu
                y_t = jnp.einsum('bdn,bn->bd', h, C_t)
                return (h, y_t)
            b = u.shape[0]
            h0 = jnp.zeros((b, A.shape[0], A.shape[1]), dtype=u.dtype)
            xs = (jnp.moveaxis(delta, 1, 0), jnp.moveaxis(Bm, 1, 0), jnp.moveaxis(Cm, 1, 0), jnp.moveaxis(u, 1, 0))
            _, ys = jax.lax.scan(step, h0, xs)
            y = jnp.moveaxis(ys, 0, 1)
            return y + u * D_param[None, None, :]
        key = jax.random.key(seed)
        ks = jax.random.split(key, 6)
        x = jax.random.normal(ks[0], (B_SZ, L, DIM), dtype=jnp.float32)
        z = jax.random.normal(ks[1], (B_SZ, L, DIM_INNER), dtype=jnp.float32)
        W_bc = jax.random.normal(ks[2], (DT_RANK + 2 * D_STATE, DIM), dtype=jnp.float32) * DIM ** (-0.5)
        W_dt = jax.random.normal(ks[3], (DIM_INNER, DT_RANK), dtype=jnp.float32) * DT_RANK ** (-0.5)
        b_dt = jax.random.normal(ks[4], (DIM_INNER,), dtype=jnp.float32) * 0.1
        A_log = jnp.log(jnp.tile(jnp.arange(1, D_STATE + 1, dtype=jnp.float32), (DIM_INNER, 1)))
        D_param = jnp.ones((DIM_INNER,), dtype=jnp.float32)
        return {'x': x, 'z': z, 'W_bc': W_bc, 'W_dt': W_dt, 'b_dt': b_dt, 'A_log': A_log, 'D_param': D_param}
    _L0_attn_in = _L0_attn_setup()

    def _L0_ffn_setup():
        import jax, jax.numpy as jnp
        import numpy as np
        L, B, D = (256, 1, 256)
        H = 16
        DK, DV = (D // 2, D)
        HDK, HDV = (DK // H, DV // H)
        RATIO = 2
        BASE = 10000.0
        EPS = 1e-05

        def _apply_rotary(x, cos, sin):
            d2 = x.shape[-1] // 2
            x1, x2 = (x[..., :d2], x[..., d2:])
            return jnp.concatenate([x1 * cos - x2 * sin, x2 * cos + x1 * sin], axis=-1)
        key = jax.random.key(seed)
        ks = jax.random.split(key, 8)
        s = 0.02
        return {'x': jax.random.normal(ks[0], (L, B, D), jnp.float32), 'conv_w': jax.random.normal(ks[1], (D, 2), jnp.float32) * 0.5, 'Wq': jax.random.normal(ks[2], (D, DK), jnp.float32) * s, 'Wk': jax.random.normal(ks[3], (D, DK), jnp.float32) * s, 'Wv': jax.random.normal(ks[4], (D, DV), jnp.float32) * s, 'Wg': jax.random.normal(ks[5], (D, DV), jnp.float32) * s, 'router_w': jax.random.normal(ks[6], (H, HDV, RATIO), jnp.float32) * s, 'Wout': jax.random.normal(ks[7], (DV, D), jnp.float32) * s}
    _L0_ffn_in = _L0_ffn_setup()
    _d = {'L0_attn_x': _L0_attn_in['x'], 'L0_attn_z': _L0_attn_in['z'], 'L0_attn_W_bc': _L0_attn_in['W_bc'], 'L0_attn_W_dt': _L0_attn_in['W_dt'], 'L0_attn_b_dt': _L0_attn_in['b_dt'], 'L0_attn_A_log': _L0_attn_in['A_log'], 'L0_attn_D_param': _L0_attn_in['D_param'], 'L0_ffn_conv_w': _L0_ffn_in['conv_w'], 'L0_ffn_Wq': _L0_ffn_in['Wq'], 'L0_ffn_Wk': _L0_ffn_in['Wk'], 'L0_ffn_Wv': _L0_ffn_in['Wv'], 'L0_ffn_Wg': _L0_ffn_in['Wg'], 'L0_ffn_router_w': _L0_ffn_in['router_w'], 'L0_ffn_Wout': _L0_ffn_in['Wout']}
    _x0 = _d['L0_attn_x']
    _d['L0_attn_x'] = jax.random.normal(jax.random.fold_in(jax.random.key(seed), 1), (4, 1024, 256), dtype=_x0.dtype)
    del _x0
    return _d

def reference(L0_attn_x, L0_attn_z, L0_attn_W_bc, L0_attn_W_dt, L0_attn_b_dt, L0_attn_A_log, L0_attn_D_param, L0_ffn_conv_w, L0_ffn_Wq, L0_ffn_Wk, L0_ffn_Wv, L0_ffn_Wg, L0_ffn_router_w, L0_ffn_Wout):

    def _L0_attn_ref(x, z, W_bc, W_dt, b_dt, A_log, D_param):
        import jax, jax.numpy as jnp
        import numpy as np
        DIM = 256
        DT_RANK = 64
        DIM_INNER = 256
        D_STATE = 32
        B_SZ = 4
        L = 256

        def _selective_scan(u, delta, A, Bm, Cm, D_param):

            def step(h, inp):
                delta_t, B_t, C_t, u_t = inp
                dA = jnp.exp(delta_t[:, :, None] * A[None])
                dBu = (delta_t * u_t)[:, :, None] * B_t[:, None, :]
                h = dA * h + dBu
                y_t = jnp.einsum('bdn,bn->bd', h, C_t)
                return (h, y_t)
            b = u.shape[0]
            h0 = jnp.zeros((b, A.shape[0], A.shape[1]), dtype=u.dtype)
            xs = (jnp.moveaxis(delta, 1, 0), jnp.moveaxis(Bm, 1, 0), jnp.moveaxis(Cm, 1, 0), jnp.moveaxis(u, 1, 0))
            _, ys = jax.lax.scan(step, h0, xs)
            y = jnp.moveaxis(ys, 0, 1)
            return y + u * D_param[None, None, :]
        A = -jnp.exp(A_log)
        deltaBC = jnp.einsum('bld,od->blo', x, W_bc)
        dt_r = deltaBC[..., :DT_RANK]
        Bm = deltaBC[..., DT_RANK:DT_RANK + D_STATE]
        Cm = deltaBC[..., DT_RANK + D_STATE:]
        dt = jnp.einsum('blr,dr->bld', dt_r, W_dt)
        delta = jax.nn.softplus(dt + b_dt[None, None, :])
        y = _selective_scan(x, delta, A, Bm, Cm, D_param)
        return y

    def _L0_ffn_ref(x, conv_w, Wq, Wk, Wv, Wg, router_w, Wout):
        import jax, jax.numpy as jnp
        import numpy as np
        L, B, D = (256, 1, 256)
        H = 16
        DK, DV = (D // 2, D)
        HDK, HDV = (DK // H, DV // H)
        RATIO = 2
        BASE = 10000.0
        EPS = 1e-05

        def _apply_rotary(x, cos, sin):
            d2 = x.shape[-1] // 2
            x1, x2 = (x[..., :d2], x[..., d2:])
            return jnp.concatenate([x1 * cos - x2 * sin, x2 * cos + x1 * sin], axis=-1)
        x = jnp.transpose(x, (1, 0, 2))
        b, l, d = x.shape
        x_prev = jnp.pad(x, ((0, 0), (1, 0), (0, 0)))[:, :l]
        x = jax.nn.silu(x_prev * conv_w[:, 0] + x * conv_w[:, 1])
        q = jax.nn.silu(x @ Wq)
        k = x @ Wk
        v = x @ Wv
        g = x @ Wg
        q = q.reshape(b, l, H, HDK).transpose(0, 2, 1, 3)
        k = k.reshape(b, l, H, HDK).transpose(0, 2, 1, 3)
        v = v.reshape(b, l, H, HDV).transpose(0, 2, 1, 3)
        inv_freq = 1.0 / BASE ** (jnp.arange(0, HDK, 2, dtype=jnp.float32) / HDK)
        freqs = jnp.arange(l, dtype=jnp.float32)[:, None] * inv_freq[None, :]
        cos, sin = (jnp.cos(freqs), jnp.sin(freqs))
        q = _apply_rotary(q, cos, sin)
        k = _apply_rotary(k, cos, sin)
        logits = jnp.einsum('bhld,hdr->bhlr', v, router_w)
        scores = jax.nn.softmax(logits, axis=-1)
        onehot = jax.nn.one_hot(jnp.argmax(scores, axis=-1), RATIO, dtype=scores.dtype)
        masked_scores = scores * onehot
        masked_ind = onehot
        sum_ind = jnp.cumsum(masked_ind, axis=2)
        norm = jnp.where(sum_ind > 0, 1.0 / jnp.maximum(sum_ind, 1.0), 0.0)[..., None]
        q_exp = q[:, :, :, None, :] * masked_scores[..., None] * norm
        k_exp = k[:, :, :, None, :] * masked_ind[..., None]
        q_exp = q_exp.reshape(b, H, l, RATIO * HDK)
        k_exp = k_exp.reshape(b, H, l, RATIO * HDK)
        qk = jnp.einsum('bhld,bhmd->bhlm', q_exp, k_exp) * HDK ** (-0.5)
        mask = jnp.tril(jnp.ones((l, l), dtype=qk.dtype))
        qk = qk * mask
        o = jnp.einsum('bhlm,bhmd->bhld', qk, v)
        o = o.transpose(0, 2, 1, 3)
        mu = jnp.mean(o, axis=-1, keepdims=True)
        var = jnp.var(o, axis=-1, keepdims=True)
        o = (o - mu) / jnp.sqrt(var + EPS)
        out = jax.nn.silu(g) * o.reshape(b, l, d)
        out = out @ Wout
        return jnp.transpose(out, (1, 0, 2))
    x = L0_attn_x
    x = x + _L0_attn_ref(_layernorm(x, axis=-1), L0_attn_z, L0_attn_W_bc, L0_attn_W_dt, L0_attn_b_dt, L0_attn_A_log, L0_attn_D_param)
    x = x + _L0_ffn_ref(_layernorm(x, axis=-1), L0_ffn_conv_w, L0_ffn_Wq, L0_ffn_Wk, L0_ffn_Wv, L0_ffn_Wg, L0_ffn_router_w, L0_ffn_Wout)
    return x

_drawn_inputs = setup_inputs


def setup_inputs(seed=0):
    import zlib

    import numpy as np

    out = dict(_drawn_inputs(seed))
    spreads = {'L0_attn_D_param': (1.0, 0.2)}
    factors = {'L0_ffn_conv_w': 8.0,
     'L0_ffn_Wq': 8.0,
     'L0_ffn_Wk': 8.0,
     'L0_ffn_Wv': 8.0,
     'L0_ffn_Wg': 8.0,
     'L0_ffn_router_w': 8.0,
     'L0_ffn_Wout': 8.0}
    for name, (base, spread) in spreads.items():
        noise = np.random.default_rng([zlib.crc32(name.encode()), seed]).standard_normal(out[name].shape)
        drawn = base * np.exp(spread * noise) if base else spread * noise
        out[name] = jnp.asarray(drawn.astype(out[name].dtype))
    for name, factor in factors.items():
        out[name] = (out[name] * factor).astype(out[name].dtype)
    return out
```

```python
import math
from contextlib import ExitStack

import concourse.bass as bass
from concourse import mybir

F32 = mybir.dt.float32
BF16 = mybir.dt.bfloat16
ALU = mybir.AluOpType
ACT = mybir.ActivationFunctionType
AX = mybir.AxisListType

B, L, D, N, R = 4, 1024, 256, 32, 64
P = 128
EPS = 1e-5
LT = L // P
TC = 32
TS = 16
CHUNKS = L // TC
SUBS = TC // TS
GROUPS = 4
GD = D // GROUPS
DQ, DG = 4, D // 4
UNIT_DG = 4
UNITS = DG // UNIT_DG
STEPS = SUBS * GROUPS
UNITS_PER_STEP = UNITS // STEPS
TERMS = 6
MOVING_PART = (0, 0, 0, 1, 1, 2)
STATION_PART = (0, 1, 2, 0, 1, 0)
ROWS = DQ * TERMS * B
QROWS = TERMS * B
BANK = 512
H, HK, HV = 16, 8, 16
DK = H * HK
COL_K, COL_V, COL_DIFF, COL_Q, COL_G = 0, DK, DK + D, DK + D + H, 2 * DK + D + H
WCOLS = COL_G + D
ROPE_BASE = 10000.0


def sub(t, p0, n, off, *dims, pstep=1):
    a = t[p0:p0 + 1]
    return bass.AP(a.tensor, a.offset + off, [[a.ap[0][0] * pstep, n], *[list(d) for d in dims]])


def dram(t, off, *dims):
    return bass.AP(t.tensor, off, [list(d) for d in dims])


def build(nc, x, W_bc, W_dt, b_dt, A_log, D_param, conv_w, Wq, Wk, Wv, Wg, router_w, Wout, out):
    ctx = ExitStack()
    with ctx:
        def sb(name, shape, dt=F32):
            return ctx.enter_context(nc.sbuf_tensor(name, shape, dt))

        def sem(name):
            return ctx.enter_context(nc.semaphore(name))

        def scratch(name, shape, dt):
            return nc.dram_tensor(name, shape, dt).ap()

        delta_parts_d = scratch("delta_parts", [3, B, DQ, L, DG], BF16)
        du_parts_d = scratch("du_parts", [3, B, L, D], BF16)
        b_terms_d = scratch("b_terms", [TERMS, B, L, N], BF16)
        a_terms_d = scratch("a_terms", [TERMS, D, N], BF16)
        base_d = scratch("base", [B, L, D], F32)
        y_d = scratch("y", [B, L, D], F32)

        SLOT = 1024
        NSLOT = 24
        arena = sb("arena", [P, NSLOT * SLOT])

        def slot(i, n=1):
            return arena[:, i * SLOT:(i + n) * SLOT]

        CHUNK_ELEMS = D * TC
        decay = [arena[:, k * CHUNK_ELEMS:(k + 1) * CHUNK_ELEMS] for k in range(2)]
        state = [arena[:, 2 * CHUNK_ELEMS + k * D * TS:2 * CHUNK_ELEMS + (k + 1) * D * TS] for k in range(2)]

        delta_mov = [sb(f"delta_mov{k}", [P, DQ * TC * DG], BF16) for k in range(2)]
        du_mov = [sb(f"du_mov{k}", [P, (TC // 4) * 4 * D], BF16) for k in range(2)]
        b_sta = [sb(f"b_sta{k}", [P, (TC // 4) * P], BF16) for k in range(2)]
        a_sta = sb("a_sta", [P, DG * P], BF16)
        c_sta = [sb(f"c_sta{k}", [P, TC * 32]) for k in range(2)]
        c_all = sb("c_all", [P, L])
        carry = sb("carry", [P, 4, GD])
        y_rows = [sb(f"y_rows{k}", [P, D]) for k in range(2)]
        ident = sb("ident", [P, P])
        pacer = sb("pacer", [P, 1])
        zeros = sb("zeros", [P, GD])
        own_batch = sb("own_batch", [P, B])

        psum = ctx.enter_context(nc.psum_tensor("psum", [P, 8 * BANK], F32))

        def bank(i, n=1):
            return psum[:, i * BANK:(i + n) * BANK]

        names = """own_made weights_loaded ident_zeroed ident_ready zeros_ready
            wT_psum wT_ready a_exp a_neg a_hi a_res a_mid a_stored a_sta_loaded ones_ready
            stats_done var_done veps_ready rstd_ready xn_ready xnT_psum xnT_ready
            dtr_psum bc_psum dtr_ready c_ready dt_psum sp_abs sp_exp sp_ln delta_ready du_ready
            dhi_ready dres_ready dmid_ready dlo_ready uhi_ready ures_ready umid_ready ulo_ready
            bhi_ready bres_ready bmid_ready blo_ready xd_ready base_ready half_ready
            md_used mu_used args_ready exp_done b_ready carry_ready decay_reset scan_done
            contract_done cpad_ready y_ready y_evac state_zeroed
            fw_loaded rd_ready wvT_psum wvT_ready wvd_psum wvd_ready tables_ready
            f_x1 f_stats f_aggr f_veps f_rstd f_xn f_xnT f_w1 f_conv f_conv0 f_xcT f_proj_qkv f_proj_gr f_q f_k f_v
            f_g f_df f_rope_c f_rope_s f_rope f_ind f_eq f_eqm f_cnt f_rcp f_th f_sm f_wt f_cf1 f_prod f_qk
            f_cf f_av f_sum f_o f_mean f_cen f_sq f_var f_gveps f_grstd f_gn f_gated f_gT_psum f_gT f_outp f_out
            f_wmul""".split()
        S = {n: sem(n) for n in names}
        x_loaded = [sem(f"x_loaded{k}") for k in range(2)]
        stored = [sem(f"stored{k}") for k in range(2)]
        md_loaded = [sem(f"md_loaded{k}") for k in range(2)]
        mu_loaded = [sem(f"mu_loaded{k}") for k in range(2)]
        y_stored = [sem(f"y_stored{k}") for k in range(2)]
        f_loaded = [sem(f"f_loaded{k}") for k in range(2)]
        out_stored = [sem(f"out_stored{k}") for k in range(2)]

        x_t = [slot(0), slot(1)]
        xn = [slot(2), slot(3)]
        xnT = [slot(4), slot(5)]
        dtr = [slot(6)[:, 0:512], slot(6)[:, 512:1024]]
        sp = slot(7)
        delta = [slot(8), slot(9)]
        du = [slot(10), slot(11)]
        dres, ures = slot(12), slot(13)
        base = [slot(14), slot(15)]
        dparts = [slot(16, 3)[:, k * 1536:(k + 1) * 1536].bitcast(BF16) for k in range(2)]
        uparts = [slot(19, 3)[:, k * 1536:(k + 1) * 1536].bitcast(BF16) for k in range(2)]
        misc = slot(22, 2)
        bparts = [misc[:, k * 192:(k + 1) * 192].bitcast(BF16) for k in range(2)]
        bres = misc[:, 384:512]
        w_bcT = misc[:, 512:768]
        w_dtT = misc[0:R, 768:1024]
        d_bc = misc[:, 1024:1280]
        bdt_row = misc[0:1, 1280:1536]
        ones_row = misc[0:1, 1536:1664]
        stats = misc[:, 1664:1664 + 48]
        mv = misc[:, 1712:1728]
        rstd = misc[:, 1728:1736]
        veps = misc[:, 1736:1744]
        half_neg = misc[:, 1744:1748]
        w_bc_n = xn[0][:, 0:256]
        w_dt_n = xn[0][:, 256:384]
        a_log_n = xn[1][:, 0:64]
        a_neg = xn[1][:, 64:128]
        a_res = xn[1][:, 128:192]
        a_parts = xn[1][:, 256:352].bitcast(BF16)


        fy = [slot(0), slot(1)]
        fbase = [slot(2), slot(3)]
        fxn = slot(4)
        fxc = slot(5)
        fxcT = slot(6)
        fqk = [slot(7), slot(8)]
        fv = [slot(9), slot(10)]
        fg = [slot(11), slot(12)]
        frc, frs, fqkr = slot(13), slot(14), slot(15)
        fprod = slot(16, 2)
        ftmp = slot(18)
        fo = slot(19)
        fgt = slot(20)
        fgT = slot(21)
        fout = [slot(22), slot(23)]

        def settle(eng):
            eng.wait_ge(S["weights_loaded"], 16 * 5)

        FP = LT // 2
        fw_t = delta_mov[0][:, :].bitcast(F32)
        fs_t = delta_mov[1][:, :].bitcast(F32)
        w_all = fw_t[:, 0:2 * WCOLS]
        w_out = fw_t[:, 1600:1600 + 2 * D]
        wvT = fw_t[:, 2200:2200 + 2 * D]
        conv = fw_t[:, 2800:2804]
        rt = fw_t[:, 2804:2808]
        rdc = fw_t[:, 2808:2810]
        rd = fw_t[:, 2816:2848]
        cos_t = fw_t[:, 2848:2864]
        sin_t = fw_t[:, 2864:2880]
        causal = fw_t[:, 2880:2896]
        fhalf = fw_t[:, 2896:2960]
        LH = B * H
        PAIR = B * B * H
        fstats = fs_t[:, 0:24]
        fmv = fs_t[:, 24:32]
        fveps = fs_t[:, 32:36]
        frstd = fs_t[:, 36:40]
        fdf = [fs_t[:, 64:128], fs_t[:, 128:192]]
        find = fs_t[:, 192:256]
        fabs = fs_t[:, 256:320]
        fsm = fs_t[:, 320:384]
        fcnt = fs_t[:, 384:448]
        frcp = fs_t[:, 448:512]
        fwt = fs_t[:, 512:576]
        feq = fs_t[:, 576:832]
        fcf = fs_t[:, 832:1088]
        fqkd = fs_t[:, 1088:1344]
        fsum = fs_t[:, 1344:1408]
        fmean = fs_t[:, 1408:1472]
        fgv = fs_t[:, 1472:1536]
        fgr = fs_t[:, 1536:1600]
        SCALE = HK ** -0.5
        FLOADS = 7

        def m_done(eng):
            for k in range(2):
                eng.wait_ge(y_stored[k], 16 * 4 * (CHUNKS // 2))

        def skewed(eng, stage_a, stage_b):
            stage_a(0, 0, 0)
            for lt in range(2):
                stage_a(lt + 1, 1 - lt, lt + 1)
                stage_b(lt, lt, lt)
            with eng.Fori(1, FP - 1) as it:
                for k in range(2):
                    stage_a(2 * it + k + 1, 1 - k, 2)
                    stage_b(2 * it + k, k, 2)
            stage_a(LT - 1, 1, 2)
            stage_b(LT - 2, 0, 2)
            stage_b(LT - 1, 1, 2)

        def dims(t, off, *d):
            return sub(t, 0, P, off, *d)

        def phase_f_sync(eng):
            ld = lambda dst, src: eng.dma_start(dst, src).then_inc(S["fw_loaded"], 16)
            wv = w_all.rearrange("p (h n) -> p h n", h=2)
            for w, o, n in ((Wq, COL_Q, DK), (Wk, COL_K, DK), (Wv, COL_V, D), (Wg, COL_G, D)):
                ld(wv[:, :, o:o + n], w.rearrange("(h p) n -> p h n", p=P))
            ld(w_out.rearrange("p (h n) -> p h n", h=2), Wout.rearrange("(h p) n -> p h n", p=P))
            ld(conv.rearrange("p (h n) -> p h n", h=2), conv_w.rearrange("(h p) n -> p h n", p=P))
            ld(rt.rearrange("p (h n) -> p h n", h=2),
               dram(router_w, 0, (2, P), (2 * P, 2), (1, 2)))

            def load(lt, k):
                eng.dma_start(fy[k].rearrange("p (b d) -> p b d", b=B),
                              dram(y_d, lt * (P * D), (D, P), (L * D, B), (1, D))).then_inc(f_loaded[k], 16)
                eng.dma_start(fbase[k].rearrange("p (b d) -> p b d", b=B),
                              dram(base_d, lt * (P * D), (D, P), (L * D, B), (1, D))).then_inc(f_loaded[k], 16)

            load(0, 0)
            load(1, 1)

            def pair(it, first, last):
                for k in range(2):
                    lt = 2 * it + k
                    settle(eng)
                    eng.wait_ge(S["f_out"], lt + 1)
                    eng.dma_start(dram(out, lt * (P * D), (D, P), (L * D, B), (1, D)),
                                  fout[k].rearrange("p (b d) -> p b d", b=B)).then_inc(out_stored[k], 16)
                    if not last:
                        load(lt + 2, k)

            tiles(eng, FP, pair)
            for k in range(2):
                eng.wait_ge(out_stored[k], 16 * FP)

        def phase_f_pool(pool):
            m_done(pool)
            for l in range(B):
                for i in range(HK // 2):
                    f = l / ROPE_BASE ** (2 * i / HK)
                    o = l * (HK // 2) + i
                    pool.memset(cos_t[:, o:o + 1], math.cos(f))
                    pool.memset(sin_t[:, o:o + 1], math.sin(f))
            pool.memset(causal, 0.0).then_inc(S["tables_ready"], 1)
            pool.wait_ge(S["tables_ready"], 1)
            for l in range(B):
                pool.memset(causal[:, l * B:l * B + l + 1], 1.0)
            pool.memset(fqkd, 0.0)
            pool.memset(fhalf, -0.5).then_inc(S["tables_ready"], 1)
            pool.wait_ge(S["fw_loaded"], 16 * FLOADS)
            pool.tensor_tensor(rdc, dims(fw_t, 2804 + 1, (2, 2)), dims(fw_t, 2804, (2, 2)), ALU.subtract)\
                .then_inc(S["rd_ready"], 1)
            pool.wait_ge(S["rd_ready"], 1)
            pool.tensor_copy(rd.rearrange("p (a h) -> p a h", a=2), dims(fw_t, 2808, (1, 2), (0, H)))\
                .then_inc(S["rd_ready"], 1)
            pool.wait_ge(S["rd_ready"], 2)
            rdv = rd.rearrange("p (a h) -> p a h", a=2)
            pool.affine_select(out=rdv, in_=rdv, compare_op=ALU.is_ge, fill=0.0, base=0,
                               pattern=[[P, 2], [-HV, H]], channel_multiplier=1).then_inc(S["rd_ready"], 1)
            pool.wait_ge(S["rd_ready"], 3)
            pool.affine_select(out=rdv, in_=rdv, compare_op=ALU.is_ge, fill=0.0, base=HV - 1,
                               pattern=[[-P, 2], [HV, H]], channel_multiplier=-1).then_inc(S["rd_ready"], 1)
            pool.wait_ge(S["tables_ready"], 2)

            def stage_a(lt, k, seen):
                pool.wait_ge(f_loaded[k], 32 * f_round(lt, k))
                pool.tensor_tensor(fy[k], fy[k], fbase[k], ALU.add).then_inc(S["f_x1"], 1)
                pool.wait_ge(S["f_veps"], lt + 1)
                pool.tensor_tensor(frstd, fveps, fhalf[:, 0:4], ALU.pow).then_inc(S["f_rstd"], 1)

            def stage_b(lt, k, seen):
                pool.wait_ge(S["f_q"], 4 * lt + 4)
                pool.wait_ge(S["f_df"], 4 * lt + 4)
                if seen:
                    pool.wait_ge(S["f_rope"], 2 * lt)
                for dst, table, name in ((frc, 2848, "f_rope_c"), (frs, 2864, "f_rope_s")):
                    pool.tensor_tensor(dst.rearrange("p (l h i) -> p l h i", l=B, i=HK // 2),
                                       fqk[k].rearrange("p (l h i) -> p l h i", l=B, i=HK // 2),
                                       dims(fw_t, table, (HK // 2, B), (0, 4 * H), (1, HK // 2)), ALU.mult)\
                        .then_inc(S[name], 1)
                pool.wait_ge(S["f_gveps"], lt + 1)
                pool.tensor_tensor(fgr, fgv, fhalf, ALU.pow).then_inc(S["f_grstd"], 1)

            skewed(pool, stage_a, stage_b)

        def f_round(lt, k):
            return (lt - k) // 2 + 1

        def phase_f_pe(pe):
            m_done(pe)
            pe.wait_ge(S["fw_loaded"], 16 * FLOADS)
            for a in range(2):
                for h in range(2):
                    tr = nc.tensor.transpose(bank(6)[:, (a * 2 + h) * P:(a * 2 + h + 1) * P],
                                             w_all[:, h * WCOLS + COL_V + a * P:h * WCOLS + COL_V + (a + 1) * P],
                                             ident[:, :])
            tr.then_inc(S["wvT_psum"], 1)
            pe.wait_ge(S["wvT_ready"], 1)
            pe.wait_ge(S["rd_ready"], 4)
            for h in range(2):
                for a in range(2):
                    mm = nc.tensor.matmul(bank(7)[:, h * H:(h + 1) * H], wvT[:, (a * 2 + h) * P:(a * 2 + h + 1) * P],
                                          rd[:, a * H:(a + 1) * H], start=(a == 0), stop=(a == 1))
            mm.then_inc(S["wvd_psum"], 1)
            pe.wait_ge(S["wvd_ready"], 1)

            def stage_a(lt, k, seen):
                pe.wait_ge(S["f_xn"], lt + 1)
                if seen:
                    pe.wait_ge(S["f_conv"], 2 * lt)
                    pe.wait_ge(S["f_w1"], 2 * lt)
                for h in range(2):
                    for b in range(B):
                        o = (h * B + b) * P
                        tr = nc.tensor.transpose(psum[:, o:o + P], fxn[:, b * D + h * P:b * D + (h + 1) * P],
                                                 ident[:, :])
                    tr.then_inc(S["f_xnT"], 1)
                pe.wait_ge(S["f_xcT"], lt + 1)
                for b in range(B):
                    ba = 2 + 2 * (b % 2)
                    if seen or b >= 2:
                        n = 4 * lt + b - 1
                        pe.wait_ge(S["f_q"], n)
                        pe.wait_ge(S["f_g"], n)
                        pe.wait_ge(S["f_df"], n)
                    for h in range(2):
                        xc = fxcT[:, (h * B + b) * P:(h * B + b + 1) * P]
                        nc.tensor.matmul(bank(ba)[:, 0:COL_Q], xc, w_all[:, h * WCOLS:h * WCOLS + COL_Q],
                                         start=(h == 0), stop=(h == 1))
                        mm = nc.tensor.matmul(bank(ba + 1)[:, 0:WCOLS - COL_Q], xc,
                                              w_all[:, h * WCOLS + COL_Q:(h + 1) * WCOLS],
                                              start=(h == 0), stop=(h == 1))
                    mm.then_inc(S["f_proj_qkv"], 1)

            def stage_b(lt, k, seen):
                pe.wait_ge(S["f_gated"], lt + 1)
                if seen:
                    pe.wait_ge(S["f_out"], lt)
                for h in range(2):
                    for b in range(B):
                        o = 6 * BANK + (h * B + b) * P
                        tr = nc.tensor.transpose(psum[:, o:o + P], fgt[:, b * D + h * P:b * D + (h + 1) * P],
                                                 ident[:, :])
                    tr.then_inc(S["f_gT_psum"], 1)
                pe.wait_ge(S["f_gT"], 2 * lt + 2)
                for b in range(B):
                    for h in range(2):
                        mm = nc.tensor.matmul(psum[:, 6 * BANK + b * D:6 * BANK + (b + 1) * D],
                                              fgT[:, (h * B + b) * P:(h * B + b + 1) * P],
                                              w_out[:, h * D:(h + 1) * D], start=(h == 0), stop=(h == 1))
                mm.then_inc(S["f_outp"], 1)

            skewed(pe, stage_a, stage_b)

        def phase_f_act(act):
            m_done(act)
            act.wait_ge(S["wvT_psum"], 1)
            nc.scalar.copy(wvT, bank(6)).then_inc(S["wvT_ready"], 1)
            act.wait_ge(S["wvd_psum"], 1)
            nc.scalar.copy(dims(fw_t, COL_DIFF, (WCOLS, 2), (1, H)),
                           bank(7)[:, 0:2 * H].rearrange("p (a h) -> p a h", a=2)).then_inc(S["wvd_ready"], 1)

            def stage_a(lt, k, seen):
                for h in range(2):
                    act.wait_ge(S["f_xnT"], 2 * lt + h + 1)
                    nc.scalar.activation(fxc[:, h * BANK:(h + 1) * BANK], bank(h), ACT.Copy,
                                         scale=conv[:, 2 * h + 1:2 * h + 2]).then_inc(S["f_w1"], 1)
                act.wait_ge(S["f_conv"], 2 * lt + 2)
                if seen:
                    act.wait_ge(S["f_proj_qkv"], 4 * lt)
                nc.scalar.activation(fxcT, fxc, ACT.Silu).then_inc(S["f_xcT"], 1)
                for b in range(B):
                    ba = 2 + 2 * (b % 2)
                    act.wait_ge(S["f_proj_qkv"], 4 * lt + b + 1)
                    if b == 0 and seen == 2:
                        act.wait_ge(S["f_rope_s"], lt - 1)
                        act.wait_ge(S["f_gated"], lt - 1)
                    nc.scalar.activation(fqk[k][:, b * D:b * D + DK], bank(ba + 1)[:, 0:DK], ACT.Silu)\
                        .then_inc(S["f_q"], 1)
                    nc.scalar.activation(fg[k][:, b * D:(b + 1) * D], bank(ba + 1)[:, DK:DK + D], ACT.Silu)\
                        .then_inc(S["f_g"], 1)

            def stage_b(lt, k, seen):
                act.wait_ge(S["f_df"], 4 * lt + 4)
                if seen:
                    act.wait_ge(S["f_sm"], lt)
                nc.scalar.activation(fabs, fdf[k], ACT.Abs, scale=0.5).then_inc(S["f_th"], 1)
                act.wait_ge(S["f_th"], 2 * lt + 1)
                nc.scalar.activation(fabs, fabs, ACT.Tanh).then_inc(S["f_th"], 1)
                act.wait_ge(S["f_cen"], lt + 1)
                nc.scalar.activation(ftmp, fo, ACT.Square).then_inc(S["f_sq"], 1)
                for h in range(2):
                    act.wait_ge(S["f_gT_psum"], 2 * lt + h + 1)
                    if seen and h == 0:
                        act.wait_ge(S["f_outp"], lt)
                    nc.scalar.copy(fgT[:, h * BANK:(h + 1) * BANK], bank(6 + h)).then_inc(S["f_gT"], 1)

            skewed(act, stage_a, stage_b)

        def phase_f_dve(dve):
            m_done(dve)
            V = nc.vector

            def stage_a(lt, k, seen):
                dve.wait_ge(S["f_x1"], lt + 1)
                for b in range(B):
                    ins = V.bn_stats(fstats[:, 6 * b:6 * b + 6], fy[k][:, b * D:(b + 1) * D])
                ins.then_inc(S["f_stats"], 1)
                dve.wait_ge(S["f_stats"], lt + 1)
                nc.vector.memset(pacer[:, :], 0.0)
                for b in range(B):
                    ins = V.bn_aggr(fmv[:, 2 * b:2 * b + 2], fstats[:, 6 * b:6 * b + 6])
                ins.then_inc(S["f_aggr"], 1)
                dve.wait_ge(S["f_aggr"], lt + 1)
                V.tensor_scalar(fveps, fmv[:, 1:8:2], EPS, None, ALU.add).then_inc(S["f_veps"], 1)
                dve.wait_ge(S["f_rstd"], lt + 1)
                if seen:
                    dve.wait_ge(S["f_xnT"], 2 * lt)
                for b in range(B):
                    ins = V.tensor_scalar(fxn[:, b * D:(b + 1) * D], fy[k][:, b * D:(b + 1) * D],
                                          fmv[:, 2 * b:2 * b + 1], frstd[:, b:b + 1], ALU.subtract, ALU.mult)
                ins.then_inc(S["f_xn"], 1)
                for h in range(2):
                    dve.wait_ge(S["f_w1"], 2 * lt + h + 1)
                    later = fxc[:, h * BANK + P:(h + 1) * BANK]
                    V.scalar_tensor_tensor(out=later, in0=bank(h)[:, 0:3 * P], scalar=conv[:, 2 * h:2 * h + 1],
                                           in1=later, op0=ALU.mult, op1=ALU.add).then_inc(S["f_conv"], 1)
                for b in range(B):
                    ba = 2 + 2 * (b % 2)
                    dve.wait_ge(S["f_proj_qkv"], 4 * lt + b + 1)
                    if b == 0 and seen == 2:
                        dve.wait_ge(S["f_rope_s"], lt - 1)
                    V.tensor_copy(fqk[k][:, b * D + DK:(b + 1) * D], bank(ba)[:, 0:DK])
                    V.tensor_copy(fv[k][:, b * D:(b + 1) * D], bank(ba)[:, COL_V:COL_V + D])
                    V.tensor_copy(fdf[k][:, b * H:(b + 1) * H], bank(ba)[:, COL_DIFF:COL_DIFF + H])\
                        .then_inc(S["f_df"], 1)

            def stage_b(lt, k, seen):
                def done(ins, name, n=1):
                    ins.then_inc(S[name], 1)
                    dve.wait_ge(S[name], n * lt + n if n == 1 else n)

                dve.wait_ge(S["f_df"], 4 * lt + 4)
                done(V.tensor_scalar(find, fdf[k], 0.0, None, ALU.is_gt), "f_ind")
                eq3 = lambda t: t.rearrange("p (l m h) -> p l m h", l=B, m=B)
                done(V.tensor_tensor(eq3(feq), dims(fs_t, 192, (H, B), (0, B), (1, H)),
                                     dims(fs_t, 192, (0, B), (H, B), (1, H)), ALU.is_equal), "f_eq")
                done(V.tensor_tensor(eq3(feq), eq3(feq), dims(fw_t, 2880, (B, B), (1, B), (0, H)), ALU.mult),
                     "f_eqm")
                done(V.tensor_reduce(fcnt.rearrange("p (l h) -> p l h", l=B),
                                     dims(fs_t, 576, (B * H, B), (1, H), (H, B)), AX.X, ALU.add), "f_cnt")
                done(V.reciprocal(frcp, fcnt), "f_rcp")
                dve.wait_ge(S["f_th"], 2 * lt + 2)
                done(V.tensor_scalar(fsm, fabs, 0.5 * SCALE, 0.5 * SCALE, ALU.mult, ALU.add), "f_sm")
                done(V.tensor_tensor(fwt, fsm, frcp, ALU.mult), "f_wt")
                done(V.tensor_tensor(eq3(feq), eq3(feq), dims(fs_t, 512, (H, B), (0, B), (1, H)), ALU.mult),
                     "f_cf1")
                dve.wait_ge(S["f_rope_s"], lt + 1)
                dve.wait_ge(S["f_rope_c"], lt + 1)
                hk = HK // 2
                half = lambda t, j: t.rearrange("p (h j i) -> p h j i", j=2, i=hk)[:, :, j, :]
                V.tensor_tensor(half(fqkr, 0), half(frc, 0), half(frs, 1), ALU.subtract).then_inc(S["f_rope"], 1)
                V.tensor_tensor(half(fqkr, 1), half(frc, 1), half(frs, 0), ALU.add).then_inc(S["f_rope"], 1)
                dve.wait_ge(S["f_rope"], 2 * lt + 2)
                off = 0
                for l in range(B):
                    n = l + 1
                    ins = V.tensor_tensor(fprod[:, off:off + n * DK].rearrange("p (m c) -> p m c", m=n),
                                          dims(arena, 15 * SLOT + l * D, (0, n), (1, DK)),
                                          dims(arena, 15 * SLOT + DK, (D, n), (1, DK)), ALU.mult)
                    off += n * DK
                ins.then_inc(S["f_prod"], 1)
                dve.wait_ge(S["f_prod"], lt + 1)
                off = 0
                for l in range(B):
                    n = l + 1
                    ins = V.tensor_reduce(fqkd[:, l * B * H:l * B * H + n * H],
                                          fprod[:, off:off + n * DK].rearrange("p (c e) -> p c e", e=HK),
                                          AX.X, ALU.add)
                    off += n * DK
                ins.then_inc(S["f_qk"], 1)
                dve.wait_ge(S["f_qk"], lt + 1)
                done(V.tensor_tensor(fcf, feq, fqkd, ALU.mult), "f_cf")
                for m in range(B):
                    n = B - m
                    dst = fo if m == 0 else ftmp
                    V.tensor_tensor(dims(arena, (19 if m == 0 else 18) * SLOT, (D, n), (HV, H), (1, HV)),
                                    dims(fs_t, 832 + m * B * H + m * H, (B * H, n), (1, H), (0, HV)),
                                    dims(arena, (9 + k) * SLOT + m * D, (0, n), (HV, H), (1, HV)), ALU.mult)\
                        .then_inc(S["f_av"], 1)
                    dve.wait_ge(S["f_av"], 7 * lt + (1 if m == 0 else 2 * m))
                    if m:
                        V.tensor_tensor(fo[:, m * D:], fo[:, m * D:], ftmp[:, 0:n * D], ALU.add)\
                            .then_inc(S["f_av"], 1)
                        dve.wait_ge(S["f_av"], 7 * lt + 2 * m + 1)
                heads = lambda t: t.rearrange("p (c e) -> p c e", e=HV)
                per_head = lambda o: dims(fs_t, o, (1, LH), (0, HV))
                done(V.tensor_reduce(fsum, heads(fo), AX.X, ALU.add), "f_sum")
                done(V.tensor_scalar(fmean, fsum, 1.0 / HV, None, ALU.mult), "f_mean")
                done(V.tensor_tensor(heads(fo), heads(fo), per_head(1408), ALU.subtract), "f_cen")
                dve.wait_ge(S["f_sq"], lt + 1)
                done(V.tensor_reduce(fsum, heads(ftmp), AX.X, ALU.add), "f_var")
                done(V.tensor_scalar(fgv, fsum, 1.0 / HV, EPS, ALU.mult, ALU.add), "f_gveps")
                dve.wait_ge(S["f_grstd"], lt + 1)
                done(V.tensor_tensor(heads(fo), heads(fo), per_head(1536), ALU.mult), "f_gn")
                if seen:
                    dve.wait_ge(S["f_gT_psum"], 2 * lt)
                dve.wait_ge(S["f_g"], 4 * lt + 4)
                V.tensor_tensor(fgt, fo, fg[k], ALU.mult).then_inc(S["f_gated"], 1)
                dve.wait_ge(S["f_outp"], lt + 1)
                if seen == 2:
                    dve.wait_ge(out_stored[k], 16 * f_round(lt - 2, k))
                V.tensor_tensor(fout[k], fy[k], bank(6, 2), ALU.add).then_inc(S["f_out"], 1)

            skewed(dve, stage_a, stage_b)

        block = ctx.enter_context(nc.Block())

        def tiles(eng, count, body):
            body(0, True, False)
            with eng.Fori(1, count - 1) as it:
                body(it, False, False)
            body(count - 1, False, True)

        dp_view = lambda h: dparts[h].rearrange("p (s n) -> p s n", s=3)
        up_view = lambda h: uparts[h].rearrange("p (s n) -> p s n", s=3)
        bp_view = lambda h: bparts[h].rearrange("p (s n) -> p s n", s=3)

        PAIRS = LT // 2
        MD_LOADS = DQ * 3
        MU_LOADS = 4 * (TERMS + B)
        STORES = 3 * B + 3 + TERMS + 1
        ALL_STORED = 16 * STORES * PAIRS

        def p_done(eng):
            for k in range(2):
                eng.wait_ge(stored[k], ALL_STORED)

        @block.sync
        def _(sp_):
            def load_x(lt, k):
                sp_.dma_start(x_t[k].rearrange("p (b d) -> p b d", b=B),
                              dram(x, lt * (P * D), (D, P), (L * D, B), (1, D))).then_inc(x_loaded[k], 16)

            sp_.dma_start(w_bc_n, W_bc[:, :]).then_inc(S["weights_loaded"], 16)
            sp_.dma_start(w_dt_n.rearrange("p (h r) -> p h r", h=2),
                          W_dt.rearrange("(h p) r -> p h r", p=P)).then_inc(S["weights_loaded"], 16)
            sp_.dma_start(a_log_n.rearrange("p (h r) -> p h r", h=2),
                          A_log.rearrange("(h p) r -> p h r", p=P)).then_inc(S["weights_loaded"], 16)
            sp_.dma_start(d_bc, dram(D_param, 0, (0, P), (1, D))).then_inc(S["weights_loaded"], 16)
            sp_.dma_start(bdt_row, dram(b_dt, 0, (0, 1), (1, D))).then_inc(S["weights_loaded"], 16)
            load_x(0, 0)
            load_x(1, 1)

            sp_.wait_ge(S["a_mid"], 2)
            for s in range(TERMS):
                sp_.dma_start(dram(a_terms_d, s * D * N, (N, P), (P * N, 2), (1, N)),
                              a_parts.rearrange("p (s h n) -> p s h n", s=3, h=2)[:, STATION_PART[s]])\
                   .then_inc(S["a_stored"], 16)
            sp_.wait_ge(S["a_stored"], 16 * TERMS)
            sp_.wait_ge(S["zeros_ready"], 2)
            for q in range(DQ):
                for b in range(B):
                    sp_.dma_start(sub(a_sta, q * QROWS + b, TERMS, b * N, (P, DG), (1, N), pstep=B),
                                  dram(a_terms_d, q * DG * N, (D * N, TERMS), (N, DG), (1, N)))\
                       .then_inc(S["a_sta_loaded"], 16)

            def pair(it, first, last):
                for k in range(2):
                    lt = 2 * it + k
                    row = lt * P
                    settle(sp_)
                    sp_.wait_ge(S["base_ready"], lt + 1)
                    sp_.dma_start(dram(base_d, row * D, (D, P), (L * D, B), (1, D)),
                                  base[k].rearrange("p (b d) -> p b d", b=B)).then_inc(stored[k], 16)
                    if not last:
                        settle(sp_)
                        sp_.wait_ge(S["xn_ready"], lt + 1)
                        load_x(lt + 2, k)
                    settle(sp_)
                    sp_.wait_ge(S["blo_ready"], lt + 1)
                    for s in range(TERMS):
                        sp_.dma_start(dram(b_terms_d, s * B * L * N + row * N, (N, P), (L * N, B), (1, N)),
                                      bp_view(k)[:, STATION_PART[s]].rearrange("p (b n) -> p b n", b=B))\
                           .then_inc(stored[k], 16)
                    settle(sp_)
                    sp_.wait_ge(S["dlo_ready"], lt + 1)
                    for s in range(3):
                        for b in range(B):
                            sp_.dma_start(dram(delta_parts_d, (s * B + b) * DQ * L * DG + row * DG,
                                               (DG, P), (L * DG, DQ), (1, DG)),
                                          dp_view(k)[:, s, b * D:(b + 1) * D].rearrange("p (q d) -> p q d", q=DQ))\
                               .then_inc(stored[k], 16)
                    settle(sp_)
                    sp_.wait_ge(S["ulo_ready"], lt + 1)
                    for s in range(3):
                        sp_.dma_start(dram(du_parts_d, s * B * L * D + row * D, (D, P), (L * D, B), (1, D)),
                                      up_view(k)[:, s].rearrange("p (b d) -> p b d", b=B)).then_inc(stored[k], 16)

            tiles(sp_, PAIRS, pair)
            p_done(sp_)

            def load_md(c, k):
                i = 0
                for q in range(DQ):
                    for s0, m in ((0, 3), (3, 2), (5, 1)):
                        part = MOVING_PART[s0]
                        sp_.dma_start(
                            sub(delta_mov[k], q * QROWS + s0 * B, m * B, q * TC * DG, (1, TC * DG)),
                            dram(delta_parts_d, part * B * DQ * L * DG + q * L * DG + c * (TC * DG),
                                 (0, m), (DQ * L * DG, B), (1, TC * DG))).then_inc(md_loaded[k], 16)

            def load_mu(c, k):
                for q in range(4):
                    for s in range(TERMS):
                        sp_.dma_start(
                            sub(du_mov[k], q * QROWS + s * B, B, q * D, (4 * D, TC // 4), (1, D)),
                            dram(du_parts_d, MOVING_PART[s] * B * L * D + q * D + c * (TC * D),
                                 (L * D, B), (4 * D, TC // 4), (1, D))).then_inc(mu_loaded[k], 16)
                    for b in range(B):
                        sp_.dma_start(
                            sub(b_sta[k], q * QROWS + b, TERMS, b * N, (P, TC // 4), (1, N), pstep=B),
                            dram(b_terms_d, b * L * N + q * N + c * (TC * N),
                                 (B * L * N, TERMS), (4 * N, TC // 4), (1, N))).then_inc(mu_loaded[k], 16)

            def store_y(c, k):
                settle(sp_)
                sp_.wait_ge(S["y_evac"], c + 1)
                for j in range(4):
                    sp_.dma_start(dram(y_d, c * (TC * D) + j * D, (4 * D, TC // 4), (L * D, B), (1, D)),
                                  y_rows[k][32 * j:32 * j + 32, :]).then_inc(y_stored[k], 16)

            load_md(0, 0)
            load_mu(0, 0)
            load_md(1, 1)
            load_mu(1, 1)

            def m_pair(it, first, last):
                for k in range(2):
                    c = 2 * it + k
                    if not last:
                        settle(sp_)
                        sp_.wait_ge(S["args_ready"], (c + 1) * UNITS)
                        load_md(c + 2, k)
                    if not (first and k == 0):
                        store_y(c - 1, 1 - k)
                    if not last:
                        settle(sp_)
                        sp_.wait_ge(S["mu_used"], c + 1)
                        load_mu(c + 2, k)

            tiles(sp_, CHUNKS // 2, m_pair)
            store_y(CHUNKS - 1, 1)
            for k in range(2):
                sp_.wait_ge(y_stored[k], 16 * 4 * (CHUNKS // 2))
            phase_f_sync(sp_)

        @block.gpsimd
        def _(pool):
            pool.memset(ident[:, :], 0.0).then_inc(S["ident_zeroed"], 1)
            pool.wait_ge(S["ident_zeroed"], 1)
            pool.affine_select(out=ident[:, :], in_=ident[:, :], compare_op=ALU.not_equal, fill=1.0,
                               base=0, pattern=[[-1, P]], channel_multiplier=1).then_inc(S["ident_ready"], 1)
            pool.memset(zeros[:, :], 0.0)
            pool.memset(own_batch[:, :], 1.0).then_inc(S["own_made"], 1)
            pool.wait_ge(S["own_made"], 1)
            pool.affine_select(out=own_batch[:, :], in_=own_batch[:, :], compare_op=ALU.is_ge, fill=0.0,
                               base=0, pattern=[[-N, B]], channel_multiplier=1).then_inc(S["own_made"], 1)
            pool.wait_ge(S["own_made"], 2)
            pool.affine_select(out=own_batch[:, :], in_=own_batch[:, :], compare_op=ALU.is_ge, fill=0.0,
                               base=N - 1, pattern=[[N, B]], channel_multiplier=-1).then_inc(S["own_made"], 1)
            pool.memset(ones_row, 1.0).then_inc(S["ones_ready"], 1)
            pool.memset(half_neg, -0.5).then_inc(S["half_ready"], 1)
            pool.memset(a_sta[:, :].bitcast(F32), 0.0).then_inc(S["zeros_ready"], 1)
            pool.wait_ge(S["half_ready"], 1)
            pool.wait_ge(S["weights_loaded"], 16 * 5)

            def pair(it, first, last):
                for k in range(2):
                    lt = 2 * it + k
                    pool.wait_ge(S["veps_ready"], lt + 1)
                    pool.tensor_tensor(rstd[:, 4 * k:4 * k + 4], veps[:, 4 * k:4 * k + 4], half_neg, ALU.pow)\
                        .then_inc(S["rstd_ready"], 1)
                    pool.wait_ge(S["xn_ready"], lt + 1)
                    if not first:
                        pool.wait_ge(stored[k], 16 * STORES * it)
                    pool.tensor_tensor(base[k].rearrange("p (b d) -> p b d", b=B),
                                       xn[k].rearrange("p (b d) -> p b d", b=B),
                                       d_bc.unsqueeze(1).to_broadcast([P, B, D]), ALU.mult)\
                        .then_inc(S["xd_ready"], 1)
                    pool.wait_ge(S["xd_ready"], lt + 1)
                    pool.tensor_tensor(base[k], base[k], x_t[k], ALU.add).then_inc(S["base_ready"], 1)
                    pool.wait_ge(S["dhi_ready"], lt + 1)
                    pool.tensor_tensor(dres, delta[k], dp_view(k)[:, 0], ALU.subtract)\
                        .then_inc(S["dres_ready"], 1)
                    pool.wait_ge(S["dmid_ready"], lt + 1)
                    pool.tensor_tensor(dp_view(k)[:, 2], dres, dp_view(k)[:, 1], ALU.subtract)\
                        .then_inc(S["dlo_ready"], 1)

            tiles(pool, PAIRS, pair)

            p_done(pool)
            pool.memset(arena[:, 2 * CHUNK_ELEMS + D * TS:2 * CHUNK_ELEMS + 2 * D * TS], 0.0)\
                .then_inc(S["state_zeroed"], 1)
            pool.wait_ge(S["state_zeroed"], 1)
            pool.wait_ge(S["c_ready"], LT)
            pool.wait_ge(S["own_made"], 3)

            def m_pair(it, first, last):
                for k in range(2):
                    c = 2 * it + k
                    if not first:
                        pool.wait_ge(S["contract_done"], 2 * c - 2)
                    pool.tensor_tensor(
                        sub(c_sta[k], 0, P, 0, (4 * 32 + 4, TC // 4), (32, 4), (1, B)),
                        c_all[:, bass.ds(c * TC, TC)].rearrange("p (q j) -> p q j", j=4)
                        .unsqueeze(3).to_broadcast([P, TC // 4, 4, B]),
                        sub(own_batch, 0, P, 0, (0, TC // 4), (0, 4), (1, B)), ALU.mult)\
                        .then_inc(S["cpad_ready"], 1)
                    for s in range(SUBS):
                        for g in range(GROUPS):
                            G = c * STEPS + s * GROUPS + g
                            early = first and k == 0 and s == 0
                            if s == 0:
                                pool.wait_ge(S["exp_done"], c * UNITS + (g + 1) * (UNITS // GROUPS))
                            if not early:
                                pool.wait_ge(S["scan_done"], G - 3)
                                pool.wait_ge(S["b_ready"], G - 3)
                            seg = decay[k][:, (s * D + g * GD) * TS:(s * D + (g + 1) * GD) * TS]\
                                .rearrange("p (d t) -> p d t", t=TS)
                            before = state[1 - s][:, g * GD * TS:(g + 1) * GD * TS]\
                                .rearrange("p (d t) -> p d t", t=TS)
                            pool.tensor_tensor(carry[:, g, :], seg[:, :, 0], before[:, :, TS - 1], ALU.mult)\
                                .then_inc(S["carry_ready"], 1)
                            pool.wait_ge(S["carry_ready"], G + 1)
                            pool.tensor_tensor(seg[:, :, 0], zeros[:, :], zeros[:, :], ALU.add)\
                                .then_inc(S["decay_reset"], 1)

            tiles(pool, CHUNKS // 2, m_pair)
            phase_f_pool(pool)

        @block.tensor
        def _(pe):
            pe.wait_ge(S["ident_ready"], 1)
            pe.wait_ge(S["weights_loaded"], 16 * 5)
            for h in range(2):
                nc.tensor.transpose(bank(6)[:, h * P:(h + 1) * P], w_bc_n[:, h * P:(h + 1) * P], ident[:, :])
                last = nc.tensor.transpose(bank(6)[0:R, 256 + h * P:256 + (h + 1) * P],
                                           w_dt_n[:, h * R:(h + 1) * R], ident[:, :])
            last.then_inc(S["wT_psum"], 1)
            pe.wait_ge(S["wT_ready"], 2)
            pe.wait_ge(S["ones_ready"], 1)

            def pair(it, first, last):
                for k in range(2):
                    lt = 2 * it + k
                    started = not (first and k == 0)
                    pe.wait_ge(S["xn_ready"], lt + 1)
                    if started:
                        pe.wait_ge(S["xnT_ready"], 2 * lt)
                    for h in range(2):
                        for b in range(B):
                            o = (h * B + b) * P
                            tr = nc.tensor.transpose(psum[:, o:o + P],
                                                     xn[k][:, b * D + h * P:b * D + (h + 1) * P], ident[:, :])
                        tr.then_inc(S["xnT_psum"], 1)
                    xT = xnT[k]
                    pe.wait_ge(S["xnT_ready"], 2 * lt + 2)
                    if started:
                        pe.wait_ge(S["dtr_ready"], lt)
                    for h in range(2):
                        mm = nc.tensor.matmul(bank(2)[0:R, :], w_bcT[:, h * P:h * P + R],
                                              xT[:, h * BANK:(h + 1) * BANK], start=(h == 0), stop=(h == 1))
                    mm.then_inc(S["dtr_psum"], 1)
                    if started:
                        pe.wait_ge(S["c_ready"], lt)
                        pe.wait_ge(S["blo_ready"], lt)
                    for b in range(B):
                        for h in range(2):
                            nc.tensor.matmul(bank(3)[N * b:N * b + N, 0:P],
                                             w_bcT[:, h * P + R + N:h * P + R + 2 * N],
                                             xT[:, h * BANK + b * P:h * BANK + (b + 1) * P],
                                             start=(h == 0), stop=(h == 1))
                    for b in range(B):
                        for h in range(2):
                            mm = nc.tensor.matmul(bank(6)[:, b * N:(b + 1) * N],
                                                  xT[:, h * BANK + b * P:h * BANK + (b + 1) * P],
                                                  w_bcT[:, h * P + R:h * P + R + N],
                                                  start=(h == 0), stop=(h == 1))
                    mm.then_inc(S["bc_psum"], 1)
                    pe.wait_ge(S["dtr_ready"], lt + 1)
                    if started:
                        pe.wait_ge(S["delta_ready"], lt)
                    for b in range(B):
                        o = psum[:, 4 * BANK + b * D:4 * BANK + (b + 1) * D]
                        nc.tensor.matmul(o, dtr[k][0:R, b * P:(b + 1) * P], w_dtT, start=True, stop=False)
                        mm = nc.tensor.matmul(o, ones_row, bdt_row, start=False, stop=True)
                    mm.then_inc(S["dt_psum"], 1)

            tiles(pe, PAIRS, pair)

            pe.wait_ge(S["a_sta_loaded"], 16 * DQ * B)
            p_done(pe)

            def decay_args(c, k, u, started):
                if started:
                    pe.wait_ge(S["exp_done"], c * UNITS + u - 1)
                for i in range(UNIT_DG):
                    dg = u * UNIT_DG + i
                    mm = nc.tensor.matmul(
                        psum[:, (4 + u % 2) * BANK + i * P:(4 + u % 2) * BANK + (i + 1) * P],
                        a_sta[0:ROWS, dg * P:(dg + 1) * P],
                        sub(delta_mov[k], 0, ROWS, dg, (TC * DG, DQ), (DG, TC)), start=True, stop=True)
                mm.then_inc(S["args_ready"], 1)
                return mm

            def contract(c, k, s, quads):
                for qq in quads:
                    for j in range(4):
                        t = s * TS + 4 * qq + j
                        q = t // 4
                        mm = nc.tensor.matmul(
                            psum[32 * j:32 * j + 32, (6 + k) * BANK:(6 + k) * BANK + D],
                            c_sta[k][:, t * 32:(t + 1) * 32],
                            sub(arena, 0, P, (2 * CHUNK_ELEMS + s * D * TS) + 4 * qq + j,
                                (TS, DQ), (DQ * TS, DG)),
                            start=(q == 0), stop=(q == TC // 4 - 1), skip_group_check=True)
                return mm

            pe.wait_ge(md_loaded[0], 16 * MD_LOADS)
            for u in range(UNITS):
                mm = decay_args(0, 0, u, u >= 2)

            def m_pair(it, first, last):
                for k in range(2):
                    c = 2 * it + k
                    pe.wait_ge(mu_loaded[k], 16 * MU_LOADS * (it + 1))
                    if not (last and k == 1):
                        pe.wait_ge(md_loaded[1 - k], 16 * MD_LOADS * (it + 1 + k))
                    for s in range(SUBS):
                        for g in range(GROUPS):
                            step = s * GROUPS + g
                            G = c * STEPS + step
                            pair_bank = 2 * (step % 2)
                            if not (first and k == 0 and step < 2):
                                pe.wait_ge(S["scan_done"], G - 1)
                            for tg in range(TS // 4):
                                for half in range(2):
                                    dg0 = g * (GD // DQ) + half * (GD // DQ // 2)
                                    o = (pair_bank + half) * BANK + tg * 4
                                    mm = nc.tensor.matmul(
                                        sub(psum, 0, P, o, (DQ * TS, GD // DQ // 2), (TS, DQ), (1, 4)),
                                        b_sta[k][0:ROWS, (s * 4 + tg) * P:(s * 4 + tg + 1) * P],
                                        sub(du_mov[k], 0, ROWS, (s * 4 + tg) * 4 * D + dg0,
                                            (1, GD // DQ // 2), (DG, DQ), (D, 4)),
                                        start=(tg == 0), stop=False, skip_group_check=True)
                            if step == STEPS - 1:
                                mm.then_inc(S["mu_used"], 1)
                            if not (last and k == 1):
                                for u in range(step * UNITS_PER_STEP, (step + 1) * UNITS_PER_STEP):
                                    mm = decay_args(c + 1, 1 - k, u, True)
                            if g >= 1 and not (first and k == 0 and s == 0):
                                ps, pk, pc = (0, k, c) if s == 1 else (1, 1 - k, c - 1)
                                if g == 1:
                                    pe.wait_ge(S["scan_done"], G - 1)
                                    if ps == 0:
                                        pe.wait_ge(S["cpad_ready"], c + 1)
                                        if not first:
                                            pe.wait_ge(S["y_evac"], c - 1)
                                mm = contract(pc, pk, ps, [g - 1] if g < 3 else [2, 3])
                                if g == 3:
                                    mm.then_inc(S["contract_done"], 1)
                            pe.wait_ge(S["carry_ready"], G + 1)
                            for half in range(2):
                                mm = nc.tensor.matmul(
                                    sub(psum, 0, P, (pair_bank + half) * BANK, (TS, BANK // TS)), ident[:, :],
                                    carry[:, g, half * (GD // 2):(half + 1) * (GD // 2)],
                                    start=False, stop=True, skip_group_check=True)
                            mm.then_inc(S["b_ready"], 1)

            tiles(pe, CHUNKS // 2, m_pair)
            pe.wait_ge(S["scan_done"], CHUNKS * STEPS)
            contract(CHUNKS - 1, 1, 1, range(4)).then_inc(S["contract_done"], 1)
            phase_f_pe(pe)

        @block.scalar
        def _(act):
            act.wait_ge(S["wT_psum"], 1)
            nc.scalar.copy(w_bcT, bank(6)[:, 0:256]).then_inc(S["wT_ready"], 1)
            nc.scalar.copy(w_dtT, bank(6)[0:R, 256:512]).then_inc(S["wT_ready"], 1)
            nc.scalar.activation(a_neg, a_log_n, ACT.Exp).then_inc(S["a_exp"], 1)

            def pair(it, first, last):
                for k in range(2):
                    lt = 2 * it + k
                    for h in range(2):
                        act.wait_ge(S["xnT_psum"], 2 * lt + h + 1)
                        if not first and h == 0:
                            act.wait_ge(S["bc_psum"], lt - 1)
                        nc.scalar.copy(xnT[k][:, h * BANK:(h + 1) * BANK], bank(h)).then_inc(S["xnT_ready"], 1)
                    act.wait_ge(S["dtr_psum"], lt + 1)
                    if not first:
                        act.wait_ge(S["dt_psum"], lt - 1)
                    nc.scalar.copy(dtr[k][0:R, :], bank(2)[0:R, :]).then_inc(S["dtr_ready"], 1)
                    act.wait_ge(S["bc_psum"], lt + 1)
                    nc.scalar.copy(c_all[:, bass.ds(lt * P, P)], bank(3)[:, 0:P]).then_inc(S["c_ready"], 1)
                    act.wait_ge(S["dt_psum"], lt + 1)
                    if not (first and k == 0):
                        act.wait_ge(S["delta_ready"], lt)
                    nc.scalar.activation(sp, bank(4, 2), ACT.Abs).then_inc(S["sp_abs"], 1)
                    act.wait_ge(S["sp_abs"], lt + 1)
                    nc.scalar.activation(sp, sp, ACT.Exp, scale=-1.0).then_inc(S["sp_exp"], 1)
                    act.wait_ge(S["sp_exp"], lt + 1)
                    nc.scalar.activation(sp, sp, ACT.Ln, bias=1.0).then_inc(S["sp_ln"], 1)
                    act.wait_ge(S["delta_ready"], lt + 1)
                    if not first:
                        act.wait_ge(stored[k], 16 * STORES * it)
                    nc.scalar.copy(dp_view(k)[:, 0], delta[k]).then_inc(S["dhi_ready"], 1)
                    act.wait_ge(S["dres_ready"], lt + 1)
                    nc.scalar.copy(dp_view(k)[:, 1], dres).then_inc(S["dmid_ready"], 1)

            tiles(act, PAIRS, pair)

            p_done(act)

            def exps(c, k, u):
                act.wait_ge(S["args_ready"], c * UNITS + u + 1)
                nc.scalar.activation(
                    sub(arena, 0, P, k * CHUNK_ELEMS + u * 16 * TS, (TS, 16), (D * TS, SUBS), (1, TS)),
                    sub(psum, 0, P, (4 + u % 2) * BANK, (TC, 16), (TS, SUBS), (1, TS)), ACT.Exp)\
                    .then_inc(S["exp_done"], 1)

            for u in range(UNITS):
                exps(0, 0, u)

            def m_pair(it, first, last):
                for k in range(2):
                    c = 2 * it + k
                    for step in range(STEPS):
                        if not (last and k == 1):
                            if step == 0 and not (first and k == 0):
                                act.wait_ge(S["scan_done"], c * STEPS)
                            for u in range(step * UNITS_PER_STEP, (step + 1) * UNITS_PER_STEP):
                                exps(c + 1, 1 - k, u)
                        if step == 4 and not (first and k == 0):
                            act.wait_ge(S["contract_done"], 2 * c)
                            n = it - 1 if k == 0 else it
                            if not (isinstance(n, int) and n <= 0):
                                act.wait_ge(y_stored[1 - k], 64 * n)
                            nc.scalar.copy(y_rows[1 - k][:, :],
                                           bank(7 - k)[:, 0:D])\
                                .then_inc(S["y_evac"], 1)

            m_pair(0, True, False)
            m_pair(1, False, False)
            with act.Fori(2, CHUNKS // 2 - 1) as it:
                m_pair(it, False, False)
            m_pair(CHUNKS // 2 - 1, False, True)
            act.wait_ge(S["contract_done"], 2 * CHUNKS)
            act.wait_ge(y_stored[1], 64 * (CHUNKS // 2 - 1))
            nc.scalar.copy(y_rows[1][:, :], bank(7)[:, 0:D]).then_inc(S["y_evac"], 1)
            phase_f_act(act)

        @block.vector
        def _(dve):
            pv = a_parts.rearrange("p (s n) -> p s n", s=3)
            dve.wait_ge(S["a_exp"], 1)
            nc.vector.tensor_scalar(a_neg, a_neg, -1.0, None, ALU.mult).then_inc(S["a_neg"], 1)
            dve.wait_ge(S["a_neg"], 1)
            nc.vector.tensor_copy(pv[:, 0], a_neg).then_inc(S["a_hi"], 1)
            dve.wait_ge(S["a_hi"], 1)
            nc.vector.tensor_tensor(a_res, a_neg, pv[:, 0], ALU.subtract).then_inc(S["a_res"], 1)
            dve.wait_ge(S["a_res"], 1)
            nc.vector.tensor_copy(pv[:, 1], a_res).then_inc(S["a_mid"], 1)
            dve.wait_ge(S["a_mid"], 1)
            nc.vector.tensor_tensor(pv[:, 2], a_res, pv[:, 1], ALU.subtract).then_inc(S["a_mid"], 1)
            for t in (*delta_mov, *du_mov, *b_sta, *c_sta):
                v = t[:, :] if t in c_sta else t[:, :].bitcast(F32)
                ins = nc.vector.memset(v, 0.0)
            ins.then_inc(S["zeros_ready"], 1)
            dve.wait_ge(S["a_stored"], 16 * TERMS)
            dve.wait_ge(S["wT_psum"], 1)

            def pair(it, first, last):
                for k in range(2):
                    lt = 2 * it + k
                    xv = x_t[k].rearrange("p (b d) -> p b d", b=B)
                    dve.wait_ge(x_loaded[k], 16 * (it + 1))
                    for b in range(B):
                        ins = nc.vector.bn_stats(stats[:, 24 * k + 6 * b:24 * k + 6 * b + 6], xv[:, b, :])
                    ins.then_inc(S["stats_done"], 1)
                    dve.wait_ge(S["stats_done"], lt + 1)
                    nc.vector.memset(pacer[:, :], 0.0)
                    for b in range(B):
                        ins = nc.vector.bn_aggr(mv[:, 8 * k + 2 * b:8 * k + 2 * b + 2],
                                                stats[:, 24 * k + 6 * b:24 * k + 6 * b + 6])
                    ins.then_inc(S["var_done"], 1)
                    dve.wait_ge(S["var_done"], lt + 1)
                    nc.vector.tensor_scalar(veps[:, 4 * k:4 * k + 4], mv[:, 8 * k + 1:8 * k + 8:2], EPS, None,
                                            ALU.add).then_inc(S["veps_ready"], 1)
                    dve.wait_ge(S["rstd_ready"], lt + 1)
                    if not first:
                        dve.wait_ge(S["xnT_psum"], 2 * lt - 2)
                        dve.wait_ge(S["xd_ready"], lt - 1)
                    for b in range(B):
                        ins = nc.vector.tensor_scalar(xn[k][:, b * D:(b + 1) * D], xv[:, b, :],
                                                      mv[:, 8 * k + 2 * b:8 * k + 2 * b + 1],
                                                      rstd[:, 4 * k + b:4 * k + b + 1], ALU.subtract, ALU.mult)
                    ins.then_inc(S["xn_ready"], 1)
                    bpsum = bank(6)[:, 0:P]
                    dve.wait_ge(S["bc_psum"], lt + 1)
                    if not first:
                        dve.wait_ge(stored[k], 16 * STORES * it)
                    nc.vector.tensor_copy(bp_view(k)[:, 0], bpsum).then_inc(S["bhi_ready"], 1)
                    dve.wait_ge(S["bhi_ready"], lt + 1)
                    nc.vector.tensor_tensor(bres, bpsum, bp_view(k)[:, 0], ALU.subtract)\
                        .then_inc(S["bres_ready"], 1)
                    dve.wait_ge(S["bres_ready"], lt + 1)
                    nc.vector.tensor_copy(bp_view(k)[:, 1], bres).then_inc(S["bmid_ready"], 1)
                    dve.wait_ge(S["bmid_ready"], lt + 1)
                    nc.vector.tensor_tensor(bp_view(k)[:, 2], bres, bp_view(k)[:, 1], ALU.subtract)\
                        .then_inc(S["blo_ready"], 1)
                    dve.wait_ge(S["sp_ln"], lt + 1)
                    if not first:
                        dve.wait_ge(S["dres_ready"], lt - 1)
                    nc.vector.scalar_tensor_tensor(out=delta[k], in0=bank(4, 2), scalar=0.0, in1=sp,
                                                   op0=ALU.max, op1=ALU.add).then_inc(S["delta_ready"], 1)
                    dve.wait_ge(S["delta_ready"], lt + 1)
                    nc.vector.tensor_tensor(du[k], delta[k], xn[k], ALU.mult).then_inc(S["du_ready"], 1)
                    dve.wait_ge(S["du_ready"], lt + 1)
                    nc.vector.tensor_copy(up_view(k)[:, 0], du[k]).then_inc(S["uhi_ready"], 1)
                    dve.wait_ge(S["uhi_ready"], lt + 1)
                    nc.vector.tensor_tensor(ures, du[k], up_view(k)[:, 0], ALU.subtract)\
                        .then_inc(S["ures_ready"], 1)
                    dve.wait_ge(S["ures_ready"], lt + 1)
                    nc.vector.tensor_copy(up_view(k)[:, 1], ures).then_inc(S["umid_ready"], 1)
                    dve.wait_ge(S["umid_ready"], lt + 1)
                    nc.vector.tensor_tensor(up_view(k)[:, 2], ures, up_view(k)[:, 1], ALU.subtract)\
                        .then_inc(S["ulo_ready"], 1)

            tiles(dve, PAIRS, pair)

            p_done(dve)

            def m_pair(it, first, last):
                for k in range(2):
                    c = 2 * it + k
                    for s in range(SUBS):
                        for g in range(GROUPS):
                            step = s * GROUPS + g
                            G = c * STEPS + step
                            dve.wait_ge(S["decay_reset"], G + 1)
                            dve.wait_ge(S["b_ready"], G + 1)
                            if g == 0 and not (first and k == 0):
                                dve.wait_ge(S["contract_done"], 2 * c + s - 1)
                            seg = slice(g * GD * TS, (g + 1) * GD * TS)
                            nc.vector.tensor_tensor_scan(
                                state[s][:, seg], decay[k][:, (s * D + g * GD) * TS:(s * D + (g + 1) * GD) * TS],
                                psum[:, 2 * (step % 2) * BANK:(2 * (step % 2) + 2) * BANK], 0.0,
                                ALU.mult, ALU.add).then_inc(S["scan_done"], 1)

            tiles(dve, CHUNKS // 2, m_pair)
            phase_f_dve(dve)


_INS = ["L0_attn_x", "L0_attn_W_bc", "L0_attn_W_dt", "L0_attn_b_dt", "L0_attn_A_log", "L0_attn_D_param",
        "L0_ffn_conv_w", "L0_ffn_Wq", "L0_ffn_Wk", "L0_ffn_Wv", "L0_ffn_Wg", "L0_ffn_router_w", "L0_ffn_Wout"]


def kernel(**inputs):
    import numpy as _np
    import concourse.bacc as _bacc
    from concourse.bass_utils import run_bass_kernel_spmd as _run

    nc = _bacc.Bacc("TRN2", target_bir_lowering=False, num_devices=1)
    arrays, args = {}, []
    for name in _INS:
        a = _np.ascontiguousarray(inputs[name])
        arrays[f"in_{name}"] = a
        args.append(nc.dram_tensor(f"in_{name}", a.shape, F32, kind="ExternalInput").ap())
    out = nc.dram_tensor("out_0", (B, L, D), F32, kind="ExternalOutput").ap()
    build(nc, *args, out)
    r = _run(nc, [arrays], core_ids=[0])
    return r.results[0]["out_0"]
```

```python
import math
from contextlib import ExitStack

import concourse.bass as bass
from concourse import mybir

F32 = mybir.dt.float32
BF16 = mybir.dt.bfloat16
ALU = mybir.AluOpType
ACT = mybir.ActivationFunctionType
AX = mybir.AxisListType

B, L, D, N, R = 4, 1024, 256, 32, 64
P = 128
EPS = 1e-5
LT = L // P
TC = 32
TS = 16
CHUNKS = L // TC
SUBS = TC // TS
GROUPS = 4
GD = D // GROUPS
DQ, DG = 4, D // 4
UNIT_DG = 4
UNITS = DG // UNIT_DG
STEPS = SUBS * GROUPS
UNITS_PER_STEP = UNITS // STEPS
TERMS = 6
MOVING_PART = (0, 0, 0, 1, 1, 2)
STATION_PART = (0, 1, 2, 0, 1, 0)
ROWS = DQ * TERMS * B
QROWS = TERMS * B
BANK = 512
H, HK, HV = 16, 8, 16
DK = H * HK
COL_V, COL_DIFF, COL_K = 0, D, D + H
COL_Q, COL_G = COL_K + DK, COL_K + 2 * DK
WCOLS = COL_G + D
ROPE_BASE = 10000.0


def sub(t, p0, n, off, *dims, pstep=1):
    a = t[p0:p0 + 1]
    return bass.AP(a.tensor, a.offset + off, [[a.ap[0][0] * pstep, n], *[list(d) for d in dims]])


def dram(t, off, *dims):
    return bass.AP(t.tensor, off, [list(d) for d in dims])


def build(nc, x, W_bc, W_dt, b_dt, A_log, D_param, conv_w, Wq, Wk, Wv, Wg, router_w, Wout, out):
    ctx = ExitStack()
    with ctx:
        def sb(name, shape, dt=F32):
            return ctx.enter_context(nc.sbuf_tensor(name, shape, dt))

        def sem(name):
            return ctx.enter_context(nc.semaphore(name))

        def scratch(name, shape, dt):
            return nc.dram_tensor(name, shape, dt).ap()

        delta_terms_d = scratch("delta_terms", [TERMS, B, L, D], BF16)
        du_terms_d = scratch("du_terms", [TERMS, B, L, D], BF16)
        b_terms_d = scratch("b_terms", [TERMS, B, L, P], BF16)
        a_terms_d = scratch("a_terms", [TERMS, D, N], BF16)
        base_d = scratch("base", [B, L, D], F32)
        y_d = scratch("y", [B, L, D], F32)

        SLOT = 1024
        NSLOT = 24
        arena = sb("arena", [P, NSLOT * SLOT])

        def slot(i, n=1):
            return arena[:, i * SLOT:(i + n) * SLOT]

        CHUNK_ELEMS = D * TC
        decay = [arena[:, k * CHUNK_ELEMS:(k + 1) * CHUNK_ELEMS] for k in range(2)]
        state = [arena[:, 2 * CHUNK_ELEMS + k * D * TS:2 * CHUNK_ELEMS + (k + 1) * D * TS] for k in range(2)]

        delta_mov = [sb(f"delta_mov{k}", [P, DQ * TC * DG], BF16) for k in range(2)]
        du_mov = [sb(f"du_mov{k}", [P, (TC // 4) * 4 * D], BF16) for k in range(2)]
        b_sta = [sb(f"b_sta{k}", [P, (TC // 4) * P], BF16) for k in range(2)]
        a_sta = sb("a_sta", [P, DG * P], BF16)
        c_sta = [sb(f"c_sta{k}", [P, TC * 32]) for k in range(2)]
        c_all = sb("c_all", [P, L])
        carry = sb("carry", [P, 4, GD])
        y_rows = [sb(f"y_rows{k}", [P, D]) for k in range(2)]
        ident = sb("ident", [P, P])
        pacer = sb("pacer", [P, 1])
        zeros = sb("zeros", [P, GD])
        own_batch = sb("own_batch", [P, B])

        psum = ctx.enter_context(nc.psum_tensor("psum", [P, 8 * BANK], F32))

        def bank(i, n=1):
            return psum[:, i * BANK:(i + n) * BANK]

        names = """own_made b_filled a_sta_zeroed c_sta_zeroed carried f_seed f_newton f_dx1 weights_loaded ident_zeroed ident_ready zeros_ready
            wT_psum wT_ready a_exp a_neg a_hi a_res a_mid a_stored a_sta_loaded ones_ready
            stats_done var_done veps_ready rstd_ready xn_ready xnT_psum xnT_ready
            dtr_psum bc_psum dtr_ready c_ready dt_psum sp_abs sp_exp sp_ln delta_ready du_ready
            dhi_ready dres_ready dmid_ready dlo_ready uhi_ready ures_ready umid_ready ulo_ready
            bhi_ready bres_ready bmid_ready blo_ready xd_ready base_ready half_ready
            md_used mu_used args_ready exp_done b_ready carry_ready decay_reset scan_done
            contract_done cpad_ready y_ready y_evac state_zeroed
            fw_loaded rd_ready wvT_psum wvT_ready wvd_psum wvd_ready tables_ready
            f_x1 f_stats f_aggr f_veps f_rstd f_xn f_xnT f_w1 f_conv f_conv0 f_xcT f_proj_qkv f_proj_gr f_q f_k f_v
            f_g f_df f_rope_c f_rope_s f_rope f_ind f_eq f_eqm f_cnt f_rcp f_th f_sm f_wt f_cf1 f_prod f_qk
            f_cf f_av f_sum f_o f_mean f_cen f_sq f_var f_gveps f_grstd f_gn f_gated f_gT_psum f_gT f_outp f_out
            f_wmul""".split()
        S = {n: sem(n) for n in names}
        x_loaded = [sem(f"x_loaded{k}") for k in range(2)]
        stored = [sem(f"stored{k}") for k in range(2)]
        md_loaded = [sem(f"md_loaded{k}") for k in range(2)]
        mu_loaded = [sem(f"mu_loaded{k}") for k in range(2)]
        y_stored = [sem(f"y_stored{k}") for k in range(2)]
        f_loaded = [sem(f"f_loaded{k}") for k in range(2)]
        out_stored = [sem(f"out_stored{k}") for k in range(2)]

        x_t = [slot(0), slot(1)]
        xn = [slot(2), slot(3)]
        xnT = [slot(4), slot(5)]
        dtr = [slot(6)[:, 0:512], slot(6)[:, 512:1024]]
        sp = slot(7)
        delta = [slot(8), slot(9)]
        du = [slot(10), slot(11)]
        dres, ures = slot(12), slot(13)
        base = [slot(14), slot(15)]
        dparts = [slot(16, 3)[:, k * 1536:(k + 1) * 1536].bitcast(BF16) for k in range(2)]
        uparts = [slot(19, 3)[:, k * 1536:(k + 1) * 1536].bitcast(BF16) for k in range(2)]
        misc = slot(22, 2)
        bparts = [misc[:, k * 192:(k + 1) * 192].bitcast(BF16) for k in range(2)]
        bres = misc[:, 384:512]
        w_bcT = misc[:, 512:768]
        w_dtT = misc[0:R, 768:1024]
        d_bc = misc[:, 1024:1280]
        bdt_row = misc[0:1, 1280:1536]
        ones_row = misc[0:1, 1536:1664]
        stats = misc[:, 1664:1664 + 48]
        mv = misc[:, 1712:1728]
        rstd = misc[:, 1728:1736]
        veps = misc[:, 1736:1744]
        half_neg = misc[:, 1744:1748]
        w_bc_n = xn[0][:, 0:256]
        w_dt_n = xn[0][:, 256:384]
        a_log_n = xn[1][:, 0:64]
        a_neg = xn[1][:, 64:128]
        a_res = xn[1][:, 128:192]
        a_parts = xn[1][:, 256:352].bitcast(BF16)


        fy = [slot(0), slot(1)]
        f_in = du_mov[0][:, :].bitcast(F32)
        fraw = [f_in[:, k * SLOT:(k + 1) * SLOT] for k in range(2)]
        fbase = [f_in[:, (2 + k) * SLOT:(3 + k) * SLOT] for k in range(2)]
        fxn = slot(4)
        fxc = slot(5)
        fxcT = slot(6)
        fqk = [slot(7), slot(8)]
        fv = [slot(9), slot(10)]
        fg = [slot(11), slot(12)]
        frc, frs, fqkr = slot(13), slot(14), slot(15)
        fprod = slot(16, 2)
        ftmp = slot(18)
        fo = slot(19)
        fgt = slot(20)
        fgT = slot(21)
        fout = [slot(22), slot(23)]

        def before(lt, k):
            return (lt - k) // 2

        def piped(eng, start, step, peeled=1):
            start()
            for lt in range(2 * peeled):
                step(lt, lt % 2, lt, 2)
            with eng.Fori(peeled, LT // 2 - 1) as it:
                for k in range(2):
                    step(2 * it + k, k, 2 * peeled, 2)
            step(LT - 2, 0, 2 * peeled, 1)
            step(LT - 1, 1, 2 * peeled, 0)

        def settle(eng):
            eng.wait_ge(S["weights_loaded"], 16 * 5)

        FP = LT // 2
        fw_t = delta_mov[0][:, :].bitcast(F32)
        fs_t = delta_mov[1][:, :].bitcast(F32)
        w_all = fw_t[:, 0:2 * WCOLS]
        w_out = fw_t[:, 1600:1600 + 2 * D]
        wvT = fw_t[:, 2200:2200 + 2 * D]
        conv = fw_t[:, 2800:2804]
        rt = fw_t[:, 2804:2808]
        rdc = fw_t[:, 2808:2810]
        rd = fw_t[:, 2816:2848]
        cos_t = fw_t[:, 2848:2864]
        sin_t = fw_t[:, 2864:2880]
        causal = fw_t[:, 2880:2896]
        fhalf = fw_t[:, 2896:2960]
        LH = B * H
        PAIR = B * B * H
        fstats = fs_t[:, 0:24]
        fmv = fs_t[:, 24:32]
        fveps = fs_t[:, 32:36]
        frstd = fs_t[:, 36:40]
        fdf = [fs_t[:, 64:128], fs_t[:, 128:192]]
        find = fs_t[:, 192:256]
        fabs = fs_t[:, 256:320]
        fsm = fs_t[:, 320:384]
        fcnt = fs_t[:, 384:448]
        frcp = fs_t[:, 448:512]
        fwt = fs_t[:, 512:576]
        feq = fs_t[:, 576:832]
        fcf = fs_t[:, 832:1088]
        fqkd = fs_t[:, 1088:1344]
        fsum = fs_t[:, 1344:1408]
        fmean = fs_t[:, 1408:1472]
        fgv = fs_t[:, 1472:1536]
        fgr = fs_t[:, 1536:1600]
        SCALE = HK ** -0.5
        NEWTON = 3
        FLOADS = 7

        def m_done(eng):
            for k in range(2):
                eng.wait_ge(y_stored[k], 16 * 4 * (CHUNKS // 2))

        def dims(t, off, *d):
            return sub(t, 0, P, off, *d)

        def phase_f_sync(eng):
            ld = lambda dst, src: eng.dma_start(dst, src).then_inc(S["fw_loaded"], 16)
            wv = w_all.rearrange("p (h n) -> p h n", h=2)
            for w, o, n in ((Wq, COL_Q, DK), (Wk, COL_K, DK), (Wv, COL_V, D), (Wg, COL_G, D)):
                ld(wv[:, :, o:o + n], w.rearrange("(h p) n -> p h n", p=P))
            ld(w_out.rearrange("p (h n) -> p h n", h=2), Wout.rearrange("(h p) n -> p h n", p=P))
            ld(conv.rearrange("p (h n) -> p h n", h=2), conv_w.rearrange("(h p) n -> p h n", p=P))
            ld(rt.rearrange("p (h n) -> p h n", h=2),
               dram(router_w, 0, (2, P), (2 * P, 2), (1, 2)))

            def load(lt, k):
                eng.dma_start(fraw[k].rearrange("p (b d) -> p b d", b=B),
                              dram(y_d, lt * (P * D), (D, P), (L * D, B), (1, D))).then_inc(f_loaded[k], 16)
                eng.dma_start(fbase[k].rearrange("p (b d) -> p b d", b=B),
                              dram(base_d, lt * (P * D), (D, P), (L * D, B), (1, D))).then_inc(f_loaded[k], 16)

            load(0, 0)
            load(1, 1)

            def step(lt, k, seen, more):
                if more == 2:
                    settle(eng)
                    eng.wait_ge(S["f_x1"], lt + 1)
                    load(lt + 2, k)
                settle(eng)
                eng.wait_ge(S["f_out"], lt + 1)
                eng.dma_start(dram(out, lt * (P * D), (D, P), (L * D, B), (1, D)),
                              fout[k].rearrange("p (b d) -> p b d", b=B)).then_inc(out_stored[k], 16)

            piped(eng, lambda: None, step)
            for k in range(2):
                eng.wait_ge(out_stored[k], 16 * FP)

        def phase_f_pool(pool):
            m_done(pool)
            for l in range(B):
                for i in range(HK // 2):
                    f = l / ROPE_BASE ** (2 * i / HK)
                    o = l * (HK // 2) + i
                    pool.memset(cos_t[:, o:o + 1], math.cos(f))
                    pool.memset(sin_t[:, o:o + 1], math.sin(f))
            pool.memset(causal, 0.0).then_inc(S["tables_ready"], 1)
            pool.wait_ge(S["tables_ready"], 1)
            for l in range(B):
                pool.memset(causal[:, l * B:l * B + l + 1], 1.0)
            pool.memset(fqkd, 0.0)
            pool.memset(fhalf, -0.5).then_inc(S["tables_ready"], 1)
            pool.wait_ge(S["fw_loaded"], 16 * FLOADS)
            pool.tensor_tensor(rdc, dims(fw_t, 2804 + 1, (2, 2)), dims(fw_t, 2804, (2, 2)), ALU.subtract)\
                .then_inc(S["rd_ready"], 1)
            pool.wait_ge(S["rd_ready"], 1)
            pool.tensor_copy(rd.rearrange("p (a h) -> p a h", a=2), dims(fw_t, 2808, (1, 2), (0, H)))\
                .then_inc(S["rd_ready"], 1)
            pool.wait_ge(S["rd_ready"], 2)
            rdv = rd.rearrange("p (a h) -> p a h", a=2)
            pool.affine_select(out=rdv, in_=rdv, compare_op=ALU.is_ge, fill=0.0, base=0,
                               pattern=[[P, 2], [-HV, H]], channel_multiplier=1).then_inc(S["rd_ready"], 1)
            pool.wait_ge(S["rd_ready"], 3)
            pool.affine_select(out=rdv, in_=rdv, compare_op=ALU.is_ge, fill=0.0, base=HV - 1,
                               pattern=[[-P, 2], [HV, H]], channel_multiplier=-1).then_inc(S["rd_ready"], 1)
            pool.wait_ge(S["tables_ready"], 2)

            def rstds(lt):
                pool.wait_ge(S["f_veps"], lt + 1)
                pool.tensor_tensor(frstd, fveps, fhalf[:, 0:4], ALU.pow).then_inc(S["f_rstd"], 1)

            def step(lt, k, seen, more):
                def rotate(dst, table, name):
                    pool.tensor_tensor(dst.rearrange("p (l h i) -> p l h i", l=B, i=HK // 2),
                                       fqk[k].rearrange("p (l h i) -> p l h i", l=B, i=HK // 2),
                                       dims(fw_t, table, (HK // 2, B), (0, 4 * H), (1, HK // 2)), ALU.mult)\
                        .then_inc(S[name], 1)

                pool.wait_ge(S["f_q"], 4 * lt + 4)
                if seen:
                    pool.wait_ge(S["f_rope"], 2 * lt)
                rotate(frc, 2848, "f_rope_c")
                rotate(frs, 2864, "f_rope_s")
                if more:
                    rstds(lt + 1)

            piped(pool, lambda: rstds(0), step)

        def phase_f_pe(pe):
            m_done(pe)
            pe.wait_ge(S["fw_loaded"], 16 * FLOADS)
            for a in range(2):
                for h in range(2):
                    tr = nc.tensor.transpose(bank(6)[:, (a * 2 + h) * P:(a * 2 + h + 1) * P],
                                             w_all[:, h * WCOLS + COL_V + a * P:h * WCOLS + COL_V + (a + 1) * P],
                                             ident[:, :])
            tr.then_inc(S["wvT_psum"], 1)
            pe.wait_ge(S["wvT_ready"], 1)
            pe.wait_ge(S["rd_ready"], 4)
            for h in range(2):
                for a in range(2):
                    mm = nc.tensor.matmul(bank(7)[:, h * H:(h + 1) * H], wvT[:, (a * 2 + h) * P:(a * 2 + h + 1) * P],
                                          rd[:, a * H:(a + 1) * H], start=(a == 0), stop=(a == 1))
            mm.then_inc(S["wvd_psum"], 1)
            pe.wait_ge(S["wvd_ready"], 1)

            def transposes(lt, seen):
                pe.wait_ge(S["f_xn"], lt + 1)
                if seen:
                    pe.wait_ge(S["f_conv"], 2 * lt)
                    pe.wait_ge(S["f_w1"], 2 * lt)
                for h in range(2):
                    for b in range(B):
                        o = (h * B + b) * P
                        tr = nc.tensor.transpose(psum[:, o:o + P], fxn[:, b * D + h * P:b * D + (h + 1) * P],
                                                 ident[:, :])
                    tr.then_inc(S["f_xnT"], 1)

            def project(lt, seen, b):
                ba = 2 + 2 * (b % 2)
                if b == 0:
                    pe.wait_ge(S["f_xcT"], lt + 1)
                if seen or b >= 2:
                    n = 4 * lt + b - 1
                    pe.wait_ge(S["f_q"], n)
                    pe.wait_ge(S["f_g"], n)
                    pe.wait_ge(S["f_df"], n)
                for h in range(2):
                    xc = fxcT[:, (h * B + b) * P:(h * B + b + 1) * P]
                    nc.tensor.matmul(bank(ba)[:, 0:COL_K], xc, w_all[:, h * WCOLS:h * WCOLS + COL_K],
                                     start=(h == 0), stop=(h == 1))
                    mm = nc.tensor.matmul(bank(ba + 1), xc, w_all[:, h * WCOLS + COL_K:(h + 1) * WCOLS],
                                          start=(h == 0), stop=(h == 1))
                mm.then_inc(S["f_proj_qkv"], 1)

            def start():
                transposes(0, 0)
                for b in range(B):
                    project(0, 0, b)

            def step(lt, k, seen, more):
                if more:
                    transposes(lt + 1, 1)
                    project(lt + 1, 1, 0)
                    project(lt + 1, 1, 1)
                pe.wait_ge(S["f_gated"], lt + 1)
                if seen:
                    pe.wait_ge(S["f_out"], lt)
                for h in range(2):
                    for b in range(B):
                        o = 6 * BANK + (h * B + b) * P
                        tr = nc.tensor.transpose(psum[:, o:o + P], fgt[:, b * D + h * P:b * D + (h + 1) * P],
                                                 ident[:, :])
                    tr.then_inc(S["f_gT_psum"], 1)
                if more:
                    project(lt + 1, 1, 2)
                pe.wait_ge(S["f_gT"], 2 * lt + 2)
                for b in range(B):
                    for h in range(2):
                        mm = nc.tensor.matmul(psum[:, 6 * BANK + b * D:6 * BANK + (b + 1) * D],
                                              fgT[:, (h * B + b) * P:(h * B + b + 1) * P],
                                              w_out[:, h * D:(h + 1) * D], start=(h == 0), stop=(h == 1))
                mm.then_inc(S["f_outp"], 1)
                if more:
                    project(lt + 1, 1, 3)

            piped(pe, start, step)

        def phase_f_act(act):
            m_done(act)
            act.wait_ge(S["wvT_psum"], 1)
            nc.scalar.copy(wvT, bank(6)).then_inc(S["wvT_ready"], 1)
            act.wait_ge(S["wvd_psum"], 1)
            nc.scalar.copy(dims(fw_t, COL_DIFF, (WCOLS, 2), (1, H)),
                           bank(7)[:, 0:2 * H].rearrange("p (a h) -> p a h", a=2)).then_inc(S["wvd_ready"], 1)

            def taps(lt, seen):
                for h in range(2):
                    act.wait_ge(S["f_xnT"], 2 * lt + h + 1)
                    nc.scalar.activation(fxc[:, h * BANK:(h + 1) * BANK], bank(h), ACT.Copy,
                                         scale=conv[:, 2 * h + 1:2 * h + 2]).then_inc(S["f_w1"], 1)

            def conv_silu(lt, seen):
                act.wait_ge(S["f_conv"], 2 * lt + 2)
                if seen:
                    act.wait_ge(S["f_proj_qkv"], 4 * lt)
                nc.scalar.activation(fxcT, fxc, ACT.Silu).then_inc(S["f_xcT"], 1)

            def q_and_g(lt, k, seen, b):
                ba = 2 + 2 * (b % 2)
                act.wait_ge(S["f_proj_qkv"], 4 * lt + b + 1)
                if b == 0 and seen == 2:
                    act.wait_ge(S["f_rope_s"], lt - 1)
                    act.wait_ge(S["f_gated"], lt - 1)
                nc.scalar.copy(fqk[k][:, b * D + DK:(b + 1) * D], bank(ba + 1)[:, 0:DK])
                nc.scalar.activation(fqk[k][:, b * D:b * D + DK], bank(ba + 1)[:, DK:2 * DK], ACT.Silu)\
                    .then_inc(S["f_q"], 1)
                nc.scalar.activation(fg[k][:, b * D:(b + 1) * D], bank(ba + 1)[:, 2 * DK:BANK], ACT.Silu)\
                    .then_inc(S["f_g"], 1)

            def start():
                taps(0, 0)
                conv_silu(0, 0)
                for b in range(B):
                    q_and_g(0, 0, 0, b)

            def step(lt, k, seen, more):
                ahead = (lt + 1, 1 - k, min(seen + 1, 2))
                act.wait_ge(S["f_df"], 4 * lt + 4)
                if seen:
                    act.wait_ge(S["f_sm"], lt)
                nc.scalar.activation(fabs, fdf[k], ACT.Abs, scale=0.5).then_inc(S["f_th"], 1)
                act.wait_ge(S["f_th"], 2 * lt + 1)
                nc.scalar.activation(fabs, fabs, ACT.Tanh).then_inc(S["f_th"], 1)
                if more:
                    taps(lt + 1, ahead[2])
                    conv_silu(lt + 1, ahead[2])
                    q_and_g(*ahead, 0)
                act.wait_ge(S["f_cen"], lt + 1)
                nc.scalar.activation(ftmp, fo, ACT.Square).then_inc(S["f_sq"], 1)
                if more:
                    q_and_g(*ahead, 1)
                for h in range(2):
                    act.wait_ge(S["f_gT_psum"], 2 * lt + h + 1)
                    if seen and h == 0:
                        act.wait_ge(S["f_outp"], lt)
                    nc.scalar.copy(fgT[:, h * BANK:(h + 1) * BANK], bank(6 + h)).then_inc(S["f_gT"], 1)
                if more:
                    q_and_g(*ahead, 2)
                    q_and_g(*ahead, 3)

            piped(act, start, step)

        def phase_f_dve(dve):
            m_done(dve)
            V = nc.vector

            def normalise(lt, k, seen):
                dve.wait_ge(f_loaded[k], 32 * (before(lt, k) + 1))
                if seen >= 2:
                    dve.wait_ge(S["f_out"], lt - 1)
                V.tensor_tensor(fy[k], fraw[k], fbase[k], ALU.add).then_inc(S["f_x1"], 1)
                dve.wait_ge(S["f_x1"], lt + 1)
                for b in range(B):
                    ins = V.bn_stats(fstats[:, 6 * b:6 * b + 6], fy[k][:, b * D:(b + 1) * D])
                ins.then_inc(S["f_stats"], 1)
                dve.wait_ge(S["f_stats"], lt + 1)
                nc.vector.memset(pacer[:, :], 0.0)
                for b in range(B):
                    ins = V.bn_aggr(fmv[:, 2 * b:2 * b + 2], fstats[:, 6 * b:6 * b + 6])
                ins.then_inc(S["f_aggr"], 1)
                dve.wait_ge(S["f_aggr"], lt + 1)
                V.tensor_scalar(fveps, fmv[:, 1:8:2], EPS, None, ALU.add).then_inc(S["f_veps"], 1)
                dve.wait_ge(S["f_rstd"], lt + 1)
                if seen:
                    dve.wait_ge(S["f_xnT"], 2 * lt)
                for b in range(B):
                    ins = V.tensor_scalar(fxn[:, b * D:(b + 1) * D], fy[k][:, b * D:(b + 1) * D],
                                          fmv[:, 2 * b:2 * b + 1], frstd[:, b:b + 1], ALU.subtract, ALU.mult)
                ins.then_inc(S["f_xn"], 1)

            def conv_taps(lt):
                for h in range(2):
                    dve.wait_ge(S["f_w1"], 2 * lt + h + 1)
                    later = fxc[:, h * BANK + P:(h + 1) * BANK]
                    V.scalar_tensor_tensor(out=later, in0=bank(h)[:, 0:3 * P], scalar=conv[:, 2 * h:2 * h + 1],
                                           in1=later, op0=ALU.mult, op1=ALU.add).then_inc(S["f_conv"], 1)
            def k_and_v(lt, k, seen, b):
                ba = 2 + 2 * (b % 2)
                dve.wait_ge(S["f_proj_qkv"], 4 * lt + b + 1)
                if b == 0 and seen >= 2:
                    dve.wait_ge(S["f_rope_s"], lt - 1)
                V.tensor_copy(fv[k][:, b * D:(b + 1) * D], bank(ba)[:, COL_V:COL_V + D])
                V.tensor_copy(fdf[k][:, b * H:(b + 1) * H], bank(ba)[:, COL_DIFF:COL_DIFF + H])\
                    .then_inc(S["f_df"], 1)

            def residual(lt, k, seen):
                dve.wait_ge(S["f_outp"], lt + 1)
                if seen >= 2:
                    dve.wait_ge(out_stored[k], 16 * before(lt, k))
                V.tensor_tensor(fout[k], fy[k], bank(6, 2), ALU.add).then_inc(S["f_out"], 1)

            def start():
                normalise(0, 0, 0)
                conv_taps(0)
                for b in range(B):
                    k_and_v(0, 0, 0, b)

            def step(lt, k, seen, more):
                ahead = (lt + 1, 1 - k, min(seen + 1, 2))

                def done(ins, name, n=1):
                    ins.then_inc(S[name], 1)
                    dve.wait_ge(S[name], n * lt + n if n == 1 else n)

                dve.wait_ge(S["f_df"], 4 * lt + 4)
                done(V.tensor_scalar(find, fdf[k], 0.0, None, ALU.is_gt), "f_ind")
                eq3 = lambda t: t.rearrange("p (l m h) -> p l m h", l=B, m=B)
                done(V.tensor_tensor(eq3(feq), dims(fs_t, 192, (H, B), (0, B), (1, H)),
                                     dims(fs_t, 192, (0, B), (H, B), (1, H)), ALU.is_equal), "f_eq")
                done(V.tensor_tensor(eq3(feq), eq3(feq), dims(fw_t, 2880, (B, B), (1, B), (0, H)), ALU.mult),
                     "f_eqm")
                done(V.tensor_reduce(fcnt.rearrange("p (l h) -> p l h", l=B),
                                     dims(fs_t, 576, (B * H, B), (1, H), (H, B)), AX.X, ALU.add), "f_cnt")
                done(V.reciprocal(frcp, fcnt), "f_rcp")
                dve.wait_ge(S["f_th"], 2 * lt + 2)
                done(V.tensor_scalar(fsm, fabs, 0.5 * SCALE, 0.5 * SCALE, ALU.mult, ALU.add), "f_sm")
                done(V.tensor_tensor(fwt, fsm, frcp, ALU.mult), "f_wt")
                done(V.tensor_tensor(eq3(feq), eq3(feq), dims(fs_t, 512, (H, B), (0, B), (1, H)), ALU.mult),
                     "f_cf1")
                dve.wait_ge(S["f_rope_s"], lt + 1)
                dve.wait_ge(S["f_rope_c"], lt + 1)
                hk = HK // 2
                half = lambda t, j: t.rearrange("p (h j i) -> p h j i", j=2, i=hk)[:, :, j, :]
                V.tensor_tensor(half(fqkr, 0), half(frc, 0), half(frs, 1), ALU.subtract).then_inc(S["f_rope"], 1)
                V.tensor_tensor(half(fqkr, 1), half(frc, 1), half(frs, 0), ALU.add).then_inc(S["f_rope"], 1)
                dve.wait_ge(S["f_rope"], 2 * lt + 2)
                off = 0
                for l in range(B):
                    n = l + 1
                    ins = V.tensor_tensor(fprod[:, off:off + n * DK].rearrange("p (m c) -> p m c", m=n),
                                          dims(arena, 15 * SLOT + l * D, (0, n), (1, DK)),
                                          dims(arena, 15 * SLOT + DK, (D, n), (1, DK)), ALU.mult)
                    off += n * DK
                ins.then_inc(S["f_prod"], 1)
                dve.wait_ge(S["f_prod"], lt + 1)
                off = 0
                for l in range(B):
                    n = l + 1
                    ins = V.tensor_reduce(fqkd[:, l * B * H:l * B * H + n * H],
                                          fprod[:, off:off + n * DK].rearrange("p (c e) -> p c e", e=HK),
                                          AX.X, ALU.add)
                    off += n * DK
                ins.then_inc(S["f_qk"], 1)
                dve.wait_ge(S["f_qk"], lt + 1)
                done(V.tensor_tensor(fcf, feq, fqkd, ALU.mult), "f_cf")
                if seen:
                    residual(lt - 1, 1 - k, seen - 1)
                if more:
                    normalise(*ahead)
                for m in range(B):
                    n = B - m
                    dst = fo if m == 0 else ftmp
                    V.tensor_tensor(dims(arena, (19 if m == 0 else 18) * SLOT, (D, n), (HV, H), (1, HV)),
                                    dims(fs_t, 832 + m * B * H + m * H, (B * H, n), (1, H), (0, HV)),
                                    dims(arena, (9 + k) * SLOT + m * D, (0, n), (HV, H), (1, HV)), ALU.mult)\
                        .then_inc(S["f_av"], 1)
                    dve.wait_ge(S["f_av"], 7 * lt + (1 if m == 0 else 2 * m))
                    if m:
                        V.tensor_tensor(fo[:, m * D:], fo[:, m * D:], ftmp[:, 0:n * D], ALU.add)\
                            .then_inc(S["f_av"], 1)
                        dve.wait_ge(S["f_av"], 7 * lt + 2 * m + 1)
                if more:
                    conv_taps(lt + 1)
                heads = lambda t: t.rearrange("p (c e) -> p c e", e=HV)
                per_head = lambda o: dims(fs_t, o, (1, LH), (0, HV))
                done(V.tensor_reduce(fsum, heads(fo), AX.X, ALU.add), "f_sum")
                done(V.tensor_scalar(fmean, fsum, 1.0 / HV, None, ALU.mult), "f_mean")
                done(V.tensor_tensor(heads(fo), heads(fo), per_head(1408), ALU.subtract), "f_cen")
                if more:
                    k_and_v(*ahead, 0)
                dve.wait_ge(S["f_sq"], lt + 1)
                done(V.tensor_reduce(fsum, heads(ftmp), AX.X, ALU.add), "f_var")
                done(V.tensor_scalar(fgv, fsum, 1.0 / HV, EPS, ALU.mult, ALU.add), "f_gveps")
                v_bits, y_bits = fgv.bitcast(mybir.dt.int32), fgr.bitcast(mybir.dt.int32)
                V.tensor_scalar(y_bits, v_bits, 1, None, ALU.logical_shift_right).then_inc(S["f_seed"], 1)
                dve.wait_ge(S["f_seed"], 2 * lt + 1)
                V.tensor_scalar(y_bits, y_bits, -1.0, float(0x5F3759DF), ALU.mult, ALU.add)\
                    .then_inc(S["f_seed"], 1)
                dve.wait_ge(S["f_seed"], 2 * lt + 2)
                for n in range(NEWTON):
                    V.tensor_tensor(fsum, fgr, fgr, ALU.mult).then_inc(S["f_newton"], 1)
                    dve.wait_ge(S["f_newton"], 3 * (NEWTON * lt + n) + 1)
                    V.scalar_tensor_tensor(out=fsum, in0=fsum, scalar=-0.5, in1=fgv, op0=ALU.mult, op1=ALU.mult)\
                        .then_inc(S["f_newton"], 1)
                    dve.wait_ge(S["f_newton"], 3 * (NEWTON * lt + n) + 2)
                    V.scalar_tensor_tensor(out=fgr, in0=fsum, scalar=1.5, in1=fgr, op0=ALU.add, op1=ALU.mult)\
                        .then_inc(S["f_newton"], 1)
                    dve.wait_ge(S["f_newton"], 3 * (NEWTON * lt + n) + 3)
                if more:
                    k_and_v(*ahead, 1)
                done(V.tensor_tensor(heads(fo), heads(fo), per_head(1536), ALU.mult), "f_gn")
                if seen:
                    dve.wait_ge(S["f_gT_psum"], 2 * lt)
                dve.wait_ge(S["f_g"], 4 * lt + 4)
                V.tensor_tensor(fgt, fo, fg[k], ALU.mult).then_inc(S["f_gated"], 1)
                if more:
                    k_and_v(*ahead, 2)
                    k_and_v(*ahead, 3)

            piped(dve, start, step, 2)
            residual(LT - 1, 1, 2)

        block = ctx.enter_context(nc.Block())

        def tiles(eng, count, body):
            body(0, True, False)
            with eng.Fori(1, count - 1) as it:
                body(it, False, False)
            body(count - 1, False, True)

        dp_view = lambda h: dparts[h].rearrange("p (s n) -> p s n", s=3)
        up_view = lambda h: uparts[h].rearrange("p (s n) -> p s n", s=3)
        bp_view = lambda h: bparts[h].rearrange("p (s n) -> p s n", s=3)

        PAIRS = LT // 2
        MD_LOADS = DQ
        MU_LOADS = 2 * 4
        STORES = 3 * TERMS + 1
        ALL_STORED = 16 * STORES * PAIRS

        def p_done(eng):
            for k in range(2):
                eng.wait_ge(stored[k], ALL_STORED)

        @block.sync
        def _(sp_):
            def load_x(lt, k):
                sp_.dma_start(x_t[k].rearrange("p (b d) -> p b d", b=B),
                              dram(x, lt * (P * D), (D, P), (L * D, B), (1, D))).then_inc(x_loaded[k], 16)

            sp_.dma_start(w_bc_n, W_bc[:, :]).then_inc(S["weights_loaded"], 16)
            sp_.dma_start(w_dt_n.rearrange("p (h r) -> p h r", h=2),
                          W_dt.rearrange("(h p) r -> p h r", p=P)).then_inc(S["weights_loaded"], 16)
            sp_.dma_start(a_log_n.rearrange("p (h r) -> p h r", h=2),
                          A_log.rearrange("(h p) r -> p h r", p=P)).then_inc(S["weights_loaded"], 16)
            sp_.dma_start(d_bc, dram(D_param, 0, (0, P), (1, D))).then_inc(S["weights_loaded"], 16)
            sp_.dma_start(bdt_row, dram(b_dt, 0, (0, 1), (1, D))).then_inc(S["weights_loaded"], 16)
            load_x(0, 0)
            load_x(1, 1)
            sp_.wait_ge(S["zeros_ready"], 1)
            row_elems = TERMS * B * L * P // P // 6
            for i in range(6):
                sp_.dma_start(dram(b_terms_d, i * P * row_elems, (row_elems, P), (1, row_elems)),
                              delta_mov[0][:, 0:row_elems]).then_inc(S["b_filled"], 16)

            sp_.wait_ge(S["a_mid"], 2)
            for s in range(TERMS):
                sp_.dma_start(dram(a_terms_d, s * D * N, (N, P), (P * N, 2), (1, N)),
                              a_parts.rearrange("p (s h n) -> p s h n", s=3, h=2)[:, STATION_PART[s]])\
                   .then_inc(S["a_stored"], 16)
            sp_.wait_ge(S["a_stored"], 16 * TERMS)
            sp_.wait_ge(S["a_sta_zeroed"], 1)
            for q in range(DQ):
                for b in range(B):
                    sp_.dma_start(sub(a_sta, q * QROWS + b, TERMS, b * N, (P, DG), (1, N), pstep=B),
                                  dram(a_terms_d, q * DG * N, (D * N, TERMS), (N, DG), (1, N)))\
                       .then_inc(S["a_sta_loaded"], 16)

            def store_terms(lt, k, scratch_d, per_term, tile, dst_dims, order):
                for s in range(TERMS):
                    sp_.dma_start(dram(scratch_d, s * per_term + dst_dims[0], *dst_dims[1:]), tile(order[s]))\
                       .then_inc(stored[k], 16)

            def step(lt, k, seen, more):
                row = lt * P
                settle(sp_)
                sp_.wait_ge(S["blo_ready"], lt + 1)
                store_terms(lt, k, b_terms_d, B * L * P,
                            lambda p: bp_view(k)[:, p].rearrange("p (b n) -> p b n", b=B),
                            (row * P, (P, P), (L * P + N, B), (1, N)), STATION_PART)
                settle(sp_)
                sp_.wait_ge(S["base_ready"], lt + 1)
                sp_.dma_start(dram(base_d, row * D, (D, P), (L * D, B), (1, D)),
                              base[k].rearrange("p (b d) -> p b d", b=B)).then_inc(stored[k], 16)
                if more == 2:
                    load_x(lt + 2, k)
                settle(sp_)
                sp_.wait_ge(S["dlo_ready"], lt + 1)
                store_terms(lt, k, delta_terms_d, B * L * D,
                            lambda p: dp_view(k)[:, p].rearrange("p (b d) -> p b d", b=B),
                            (row * D, (D, P), (L * D, B), (1, D)), MOVING_PART)
                settle(sp_)
                sp_.wait_ge(S["ulo_ready"], lt + 1)
                store_terms(lt, k, du_terms_d, B * L * D,
                            lambda p: up_view(k)[:, p].rearrange("p (b d) -> p b d", b=B),
                            (row * D, (D, P), (L * D, B), (1, D)), MOVING_PART)

            sp_.wait_ge(S["b_filled"], 16 * 6)
            piped(sp_, lambda: None, step)
            p_done(sp_)
            sp_.wait_ge(S["zeros_ready"], 4)

            def load_md(c, k):
                for q in range(DQ):
                    sp_.dma_start(sub(delta_mov[k], q * QROWS, QROWS, q * TC * DG, (1, TC * DG)),
                                  dram(delta_terms_d, q * DG + c * (TC * D), (L * D, QROWS), (D, TC), (1, DG)))\
                       .then_inc(md_loaded[k], 16)

            def load_mu(c, k):
                for q in range(4):
                    sp_.dma_start(sub(du_mov[k], q * QROWS, QROWS, q * D, (4 * D, TC // 4), (1, D)),
                                  dram(du_terms_d, q * D + c * (TC * D), (L * D, QROWS), (4 * D, TC // 4), (1, D)))\
                       .then_inc(mu_loaded[k], 16)
                    sp_.dma_start(sub(b_sta[k], q * QROWS, QROWS, 0, (P, TC // 4), (1, P)),
                                  dram(b_terms_d, q * P + c * (TC * P), (L * P, QROWS), (4 * P, TC // 4), (1, P)))\
                       .then_inc(mu_loaded[k], 16)

            def store_y(c, k):
                settle(sp_)
                sp_.wait_ge(S["y_evac"], c + 1)
                for j in range(4):
                    sp_.dma_start(dram(y_d, c * (TC * D) + j * D, (4 * D, TC // 4), (L * D, B), (1, D)),
                                  y_rows[k][32 * j:32 * j + 32, :]).then_inc(y_stored[k], 16)

            load_md(0, 0)
            load_mu(0, 0)
            load_md(1, 1)
            load_mu(1, 1)

            def m_pair(it, first, last):
                for k in range(2):
                    c = 2 * it + k
                    if not last:
                        settle(sp_)
                        sp_.wait_ge(S["args_ready"], (c + 1) * UNITS)
                        load_md(c + 2, k)
                    if not (first and k == 0):
                        store_y(c - 1, 1 - k)
                    if not last:
                        settle(sp_)
                        sp_.wait_ge(S["b_ready"], (c + 1) * STEPS)
                        load_mu(c + 2, k)

            tiles(sp_, CHUNKS // 2, m_pair)
            store_y(CHUNKS - 1, 1)
            for k in range(2):
                sp_.wait_ge(y_stored[k], 16 * 4 * (CHUNKS // 2))
            phase_f_sync(sp_)

        @block.gpsimd
        def _(pool):
            pool.memset(ident[:, :], 0.0).then_inc(S["ident_zeroed"], 1)
            pool.wait_ge(S["ident_zeroed"], 1)
            pool.affine_select(out=ident[:, :], in_=ident[:, :], compare_op=ALU.not_equal, fill=1.0,
                               base=0, pattern=[[-1, P]], channel_multiplier=1).then_inc(S["ident_ready"], 1)
            pool.memset(zeros[:, :], 0.0)
            pool.memset(own_batch[:, :], 1.0).then_inc(S["own_made"], 1)
            pool.wait_ge(S["own_made"], 1)
            pool.affine_select(out=own_batch[:, :], in_=own_batch[:, :], compare_op=ALU.is_ge, fill=0.0,
                               base=0, pattern=[[-N, B]], channel_multiplier=1).then_inc(S["own_made"], 1)
            pool.wait_ge(S["own_made"], 2)
            pool.affine_select(out=own_batch[:, :], in_=own_batch[:, :], compare_op=ALU.is_ge, fill=0.0,
                               base=N - 1, pattern=[[N, B]], channel_multiplier=-1).then_inc(S["own_made"], 1)
            pool.memset(ones_row, 1.0).then_inc(S["ones_ready"], 1)
            pool.memset(half_neg, -0.5).then_inc(S["half_ready"], 1)
            pool.memset(a_sta[:, :].bitcast(F32), 0.0).then_inc(S["a_sta_zeroed"], 1)
            pool.wait_ge(S["half_ready"], 1)
            pool.wait_ge(S["weights_loaded"], 16 * 5)

            def rstds(lt, k):
                pool.wait_ge(S["veps_ready"], lt + 1)
                pool.tensor_tensor(rstd[:, 4 * k:4 * k + 4], veps[:, 4 * k:4 * k + 4], half_neg, ALU.pow)\
                    .then_inc(S["rstd_ready"], 1)

            def bases(lt, k, seen):
                pool.wait_ge(S["xn_ready"], lt + 1)
                if seen == 2:
                    pool.wait_ge(stored[k], 16 * STORES * before(lt, k))
                pool.tensor_tensor(base[k].rearrange("p (b d) -> p b d", b=B),
                                   xn[k].rearrange("p (b d) -> p b d", b=B),
                                   d_bc.unsqueeze(1).to_broadcast([P, B, D]), ALU.mult)\
                    .then_inc(S["xd_ready"], 1)
                pool.wait_ge(S["xd_ready"], lt + 1)
                pool.tensor_tensor(base[k], base[k], x_t[k], ALU.add).then_inc(S["base_ready"], 1)

            def start():
                rstds(0, 0)
                bases(0, 0, 0)

            def step(lt, k, seen, more):
                if more:
                    rstds(lt + 1, 1 - k)
                if seen:
                    pool.wait_ge(S["dlo_ready"], lt)
                pool.wait_ge(S["dhi_ready"], lt + 1)
                pool.tensor_tensor(dres, delta[k], dp_view(k)[:, 0], ALU.subtract)\
                    .then_inc(S["dres_ready"], 1)
                if more:
                    bases(lt + 1, 1 - k, min(seen + 1, 2))
                pool.wait_ge(S["dmid_ready"], lt + 1)
                pool.tensor_tensor(dp_view(k)[:, 2], dres, dp_view(k)[:, 1], ALU.subtract)\
                    .then_inc(S["dlo_ready"], 1)

            piped(pool, start, step)

            for k in range(2):
                pool.memset(c_sta[k][:, :], 0.0).then_inc(S["c_sta_zeroed"], 1)
            p_done(pool)
            pool.wait_ge(S["c_sta_zeroed"], 2)
            pool.memset(arena[:, 2 * CHUNK_ELEMS + D * TS:2 * CHUNK_ELEMS + 2 * D * TS], 0.0)\
                .then_inc(S["state_zeroed"], 1)
            pool.wait_ge(S["state_zeroed"], 1)
            pool.wait_ge(S["c_ready"], LT)
            pool.wait_ge(S["own_made"], 3)

            def m_pair(it, first, last):
                for k in range(2):
                    c = 2 * it + k
                    if not first:
                        pool.wait_ge(S["contract_done"], 2 * c - 2)
                    pool.tensor_tensor(
                        sub(c_sta[k], 0, P, 0, (4 * 32 + 4, TC // 4), (32, 4), (1, B)),
                        c_all[:, bass.ds(c * TC, TC)].rearrange("p (q j) -> p q j", j=4)
                        .unsqueeze(3).to_broadcast([P, TC // 4, 4, B]),
                        sub(own_batch, 0, P, 0, (0, TC // 4), (0, 4), (1, B)), ALU.mult)\
                        .then_inc(S["cpad_ready"], 1)
                    for s in range(SUBS):
                        for g in range(GROUPS):
                            G = c * STEPS + s * GROUPS + g
                            early = first and k == 0 and s == 0
                            if s == 0:
                                pool.wait_ge(S["exp_done"], c * UNITS + (g + 1) * (UNITS // GROUPS))
                            if not early:
                                pool.wait_ge(S["scan_done"], G - 3)
                                pool.wait_ge(S["carried"], G - 3)
                            seg = decay[k][:, (s * D + g * GD) * TS:(s * D + (g + 1) * GD) * TS]\
                                .rearrange("p (d t) -> p d t", t=TS)
                            before = state[1 - s][:, g * GD * TS:(g + 1) * GD * TS]\
                                .rearrange("p (d t) -> p d t", t=TS)
                            pool.tensor_tensor(carry[:, g, :], seg[:, :, 0], before[:, :, TS - 1], ALU.mult)\
                                .then_inc(S["carry_ready"], 1)
                            pool.wait_ge(S["carry_ready"], G + 1)
                            pool.tensor_tensor(seg[:, :, 0], zeros[:, :], zeros[:, :], ALU.add)\
                                .then_inc(S["decay_reset"], 1)

            tiles(pool, CHUNKS // 2, m_pair)
            phase_f_pool(pool)

        @block.tensor
        def _(pe):
            pe.wait_ge(S["ident_ready"], 1)
            pe.wait_ge(S["weights_loaded"], 16 * 5)
            for h in range(2):
                nc.tensor.transpose(bank(6)[:, h * P:(h + 1) * P], w_bc_n[:, h * P:(h + 1) * P], ident[:, :])
                last = nc.tensor.transpose(bank(6)[0:R, 256 + h * P:256 + (h + 1) * P],
                                           w_dt_n[:, h * R:(h + 1) * R], ident[:, :])
            last.then_inc(S["wT_psum"], 1)
            pe.wait_ge(S["wT_ready"], 2)
            pe.wait_ge(S["ones_ready"], 1)

            def pair(it, first, last):
                for k in range(2):
                    lt = 2 * it + k
                    started = not (first and k == 0)
                    pe.wait_ge(S["xn_ready"], lt + 1)
                    if started:
                        pe.wait_ge(S["xnT_ready"], 2 * lt)
                    for h in range(2):
                        for b in range(B):
                            o = (h * B + b) * P
                            tr = nc.tensor.transpose(psum[:, o:o + P],
                                                     xn[k][:, b * D + h * P:b * D + (h + 1) * P], ident[:, :])
                        tr.then_inc(S["xnT_psum"], 1)
                    xT = xnT[k]
                    pe.wait_ge(S["xnT_ready"], 2 * lt + 2)
                    if started:
                        pe.wait_ge(S["dtr_ready"], lt)
                    for h in range(2):
                        mm = nc.tensor.matmul(bank(2)[0:R, :], w_bcT[:, h * P:h * P + R],
                                              xT[:, h * BANK:(h + 1) * BANK], start=(h == 0), stop=(h == 1))
                    mm.then_inc(S["dtr_psum"], 1)
                    if started:
                        pe.wait_ge(S["c_ready"], lt)
                        pe.wait_ge(S["blo_ready"], lt)
                    for b in range(B):
                        for h in range(2):
                            nc.tensor.matmul(bank(3)[N * b:N * b + N, 0:P],
                                             w_bcT[:, h * P + R + N:h * P + R + 2 * N],
                                             xT[:, h * BANK + b * P:h * BANK + (b + 1) * P],
                                             start=(h == 0), stop=(h == 1))
                    for b in range(B):
                        for h in range(2):
                            mm = nc.tensor.matmul(bank(6)[:, b * N:(b + 1) * N],
                                                  xT[:, h * BANK + b * P:h * BANK + (b + 1) * P],
                                                  w_bcT[:, h * P + R:h * P + R + N],
                                                  start=(h == 0), stop=(h == 1))
                    mm.then_inc(S["bc_psum"], 1)
                    pe.wait_ge(S["dtr_ready"], lt + 1)
                    if started:
                        pe.wait_ge(S["delta_ready"], lt)
                    for b in range(B):
                        o = psum[:, 4 * BANK + b * D:4 * BANK + (b + 1) * D]
                        nc.tensor.matmul(o, dtr[k][0:R, b * P:(b + 1) * P], w_dtT, start=True, stop=False)
                        mm = nc.tensor.matmul(o, ones_row, bdt_row, start=False, stop=True)
                    mm.then_inc(S["dt_psum"], 1)

            tiles(pe, PAIRS, pair)

            pe.wait_ge(S["a_sta_loaded"], 16 * DQ * B)
            p_done(pe)

            def decay_args(c, k, u, started):
                if started:
                    pe.wait_ge(S["exp_done"], c * UNITS + u - 1)
                for i in range(UNIT_DG):
                    dg = u * UNIT_DG + i
                    mm = nc.tensor.matmul(
                        psum[:, (4 + u % 2) * BANK + i * P:(4 + u % 2) * BANK + (i + 1) * P],
                        a_sta[0:ROWS, dg * P:(dg + 1) * P],
                        sub(delta_mov[k], 0, ROWS, dg, (TC * DG, DQ), (DG, TC)), start=True, stop=True)
                mm.then_inc(S["args_ready"], 1)
                return mm

            def contract(c, k, s, quads):
                for qq in quads:
                    for j in range(4):
                        t = s * TS + 4 * qq + j
                        q = t // 4
                        mm = nc.tensor.matmul(
                            psum[32 * j:32 * j + 32, (6 + k) * BANK:(6 + k) * BANK + D],
                            c_sta[k][:, t * 32:(t + 1) * 32],
                            sub(arena, 0, P, (2 * CHUNK_ELEMS + s * D * TS) + 4 * qq + j,
                                (TS, DQ), (DQ * TS, DG)),
                            start=(q == 0), stop=(q == TC // 4 - 1), skip_group_check=True)
                return mm

            pe.wait_ge(md_loaded[0], 16 * MD_LOADS)
            for u in range(UNITS):
                mm = decay_args(0, 0, u, u >= 2)

            def m_pair(it, first, last):
                for k in range(2):
                    c = 2 * it + k
                    pe.wait_ge(mu_loaded[k], 16 * MU_LOADS * (it + 1))
                    if not (last and k == 1):
                        pe.wait_ge(md_loaded[1 - k], 16 * MD_LOADS * (it + 1 + k))
                    for s in range(SUBS):
                        for g in range(GROUPS):
                            step = s * GROUPS + g
                            G = c * STEPS + step
                            pair_bank = 2 * (step % 2)
                            if not (first and k == 0 and step < 2):
                                pe.wait_ge(S["scan_done"], G - 1)
                            for tg in range(TS // 4):
                                for half in range(2):
                                    dg0 = g * (GD // DQ) + half * (GD // DQ // 2)
                                    o = (pair_bank + half) * BANK + tg * 4
                                    mm = nc.tensor.matmul(
                                        sub(psum, 0, P, o, (DQ * TS, GD // DQ // 2), (TS, DQ), (1, 4)),
                                        b_sta[k][0:ROWS, (s * 4 + tg) * P:(s * 4 + tg + 1) * P],
                                        sub(du_mov[k], 0, ROWS, (s * 4 + tg) * 4 * D + dg0,
                                            (1, GD // DQ // 2), (DG, DQ), (D, 4)),
                                        start=True, stop=True)
                            mm.then_inc(S["b_ready"], 1)
                            if not (last and k == 1):
                                for u in range(step * UNITS_PER_STEP, (step + 1) * UNITS_PER_STEP):
                                    mm = decay_args(c + 1, 1 - k, u, True)
                            if g >= 1 and not (first and k == 0 and s == 0):
                                ps, pk, pc = (0, k, c) if s == 1 else (1, 1 - k, c - 1)
                                if g == 1:
                                    pe.wait_ge(S["scan_done"], G - 1)
                                    if ps == 0:
                                        pe.wait_ge(S["cpad_ready"], c + 1)
                                        if not first:
                                            pe.wait_ge(S["y_evac"], c - 1)
                                mm = contract(pc, pk, ps, [g - 1] if g < 3 else [2, 3])
                                if g == 3:
                                    mm.then_inc(S["contract_done"], 1)
            tiles(pe, CHUNKS // 2, m_pair)
            pe.wait_ge(S["scan_done"], CHUNKS * STEPS)
            contract(CHUNKS - 1, 1, 1, range(4)).then_inc(S["contract_done"], 1)
            phase_f_pe(pe)

        @block.scalar
        def _(act):
            act.wait_ge(S["wT_psum"], 1)
            nc.scalar.copy(w_bcT, bank(6)[:, 0:256]).then_inc(S["wT_ready"], 1)
            nc.scalar.copy(w_dtT, bank(6)[0:R, 256:512]).then_inc(S["wT_ready"], 1)
            nc.scalar.activation(a_neg, a_log_n, ACT.Exp).then_inc(S["a_exp"], 1)

            def xnTs(lt, k, seen):
                for h in range(2):
                    act.wait_ge(S["xnT_psum"], 2 * lt + h + 1)
                    if seen == 2 and h == 0:
                        act.wait_ge(S["bc_psum"], lt - 1)
                    nc.scalar.copy(xnT[k][:, h * BANK:(h + 1) * BANK], bank(h)).then_inc(S["xnT_ready"], 1)

            def projections(lt, k, seen):
                act.wait_ge(S["dtr_psum"], lt + 1)
                if seen == 2:
                    act.wait_ge(S["dt_psum"], lt - 1)
                nc.scalar.copy(dtr[k][0:R, :], bank(2)[0:R, :]).then_inc(S["dtr_ready"], 1)
                act.wait_ge(S["bc_psum"], lt + 1)
                nc.scalar.copy(c_all[:, bass.ds(lt * P, P)], bank(3)[:, 0:P]).then_inc(S["c_ready"], 1)

            def start():
                xnTs(0, 0, 0)
                projections(0, 0, 0)

            def step(lt, k, seen, more):
                act.wait_ge(S["dt_psum"], lt + 1)
                if seen:
                    act.wait_ge(S["delta_ready"], lt)
                nc.scalar.activation(sp, bank(4, 2), ACT.Abs).then_inc(S["sp_abs"], 1)
                act.wait_ge(S["sp_abs"], lt + 1)
                nc.scalar.activation(sp, sp, ACT.Exp, scale=-1.0).then_inc(S["sp_exp"], 1)
                act.wait_ge(S["sp_exp"], lt + 1)
                nc.scalar.activation(sp, sp, ACT.Ln, bias=1.0).then_inc(S["sp_ln"], 1)
                if more:
                    xnTs(lt + 1, 1 - k, min(seen + 1, 2))
                act.wait_ge(S["delta_ready"], lt + 1)
                if seen == 2:
                    act.wait_ge(stored[k], 16 * STORES * before(lt, k))
                nc.scalar.copy(dp_view(k)[:, 0], delta[k]).then_inc(S["dhi_ready"], 1)
                if more:
                    projections(lt + 1, 1 - k, min(seen + 1, 2))
                act.wait_ge(S["dres_ready"], lt + 1)
                nc.scalar.copy(dp_view(k)[:, 1], dres).then_inc(S["dmid_ready"], 1)

            piped(act, start, step)

            p_done(act)

            def exps(c, k, u):
                act.wait_ge(S["args_ready"], c * UNITS + u + 1)
                nc.scalar.activation(
                    sub(arena, 0, P, k * CHUNK_ELEMS + u * 16 * TS, (TS, 16), (D * TS, SUBS), (1, TS)),
                    sub(psum, 0, P, (4 + u % 2) * BANK, (TC, 16), (TS, SUBS), (1, TS)), ACT.Exp)\
                    .then_inc(S["exp_done"], 1)

            for u in range(UNITS):
                exps(0, 0, u)

            def m_pair(it, first, last):
                for k in range(2):
                    c = 2 * it + k
                    for step in range(STEPS):
                        if not (last and k == 1):
                            if step == 0 and not (first and k == 0):
                                act.wait_ge(S["scan_done"], c * STEPS)
                            for u in range(step * UNITS_PER_STEP, (step + 1) * UNITS_PER_STEP):
                                exps(c + 1, 1 - k, u)
                        if step == 4 and not (first and k == 0):
                            act.wait_ge(S["contract_done"], 2 * c)
                            n = it - 1 if k == 0 else it
                            if not (isinstance(n, int) and n <= 0):
                                act.wait_ge(y_stored[1 - k], 64 * n)
                            nc.scalar.copy(y_rows[1 - k][:, :],
                                           bank(7 - k)[:, 0:D])\
                                .then_inc(S["y_evac"], 1)

            m_pair(0, True, False)
            m_pair(1, False, False)
            with act.Fori(2, CHUNKS // 2 - 1) as it:
                m_pair(it, False, False)
            m_pair(CHUNKS // 2 - 1, False, True)
            act.wait_ge(S["contract_done"], 2 * CHUNKS)
            act.wait_ge(y_stored[1], 64 * (CHUNKS // 2 - 1))
            nc.scalar.copy(y_rows[1][:, :], bank(7)[:, 0:D]).then_inc(S["y_evac"], 1)
            phase_f_act(act)

        @block.vector
        def _(dve):
            def zero(t):
                nc.vector.memset(t[:, :].bitcast(F32), 0.0).then_inc(S["zeros_ready"], 1)

            zero(delta_mov[0])
            pv = a_parts.rearrange("p (s n) -> p s n", s=3)
            dve.wait_ge(S["a_exp"], 1)
            nc.vector.tensor_scalar(a_neg, a_neg, -1.0, None, ALU.mult).then_inc(S["a_neg"], 1)
            dve.wait_ge(S["a_neg"], 1)
            nc.vector.tensor_copy(pv[:, 0], a_neg).then_inc(S["a_hi"], 1)
            dve.wait_ge(S["a_hi"], 1)
            nc.vector.tensor_tensor(a_res, a_neg, pv[:, 0], ALU.subtract).then_inc(S["a_res"], 1)
            dve.wait_ge(S["a_res"], 1)
            nc.vector.tensor_copy(pv[:, 1], a_res).then_inc(S["a_mid"], 1)
            dve.wait_ge(S["a_mid"], 1)
            nc.vector.tensor_tensor(pv[:, 2], a_res, pv[:, 1], ALU.subtract).then_inc(S["a_mid"], 1)
            dve.wait_ge(S["a_stored"], 16 * TERMS)
            dve.wait_ge(S["wT_psum"], 1)

            def normalise(lt, k, seen):
                xv = x_t[k].rearrange("p (b d) -> p b d", b=B)
                dve.wait_ge(x_loaded[k], 16 * (before(lt, k) + 1))
                for b in range(B):
                    ins = nc.vector.bn_stats(stats[:, 24 * k + 6 * b:24 * k + 6 * b + 6], xv[:, b, :])
                ins.then_inc(S["stats_done"], 1)
                dve.wait_ge(S["stats_done"], lt + 1)
                nc.vector.memset(pacer[:, :], 0.0)
                for b in range(B):
                    ins = nc.vector.bn_aggr(mv[:, 8 * k + 2 * b:8 * k + 2 * b + 2],
                                            stats[:, 24 * k + 6 * b:24 * k + 6 * b + 6])
                ins.then_inc(S["var_done"], 1)
                dve.wait_ge(S["var_done"], lt + 1)
                nc.vector.tensor_scalar(veps[:, 4 * k:4 * k + 4], mv[:, 8 * k + 1:8 * k + 8:2], EPS, None,
                                        ALU.add).then_inc(S["veps_ready"], 1)
                dve.wait_ge(S["rstd_ready"], lt + 1)
                if seen == 2:
                    dve.wait_ge(S["xnT_psum"], 2 * lt - 2)
                    dve.wait_ge(S["xd_ready"], lt - 1)
                for b in range(B):
                    ins = nc.vector.tensor_scalar(xn[k][:, b * D:(b + 1) * D], xv[:, b, :],
                                                  mv[:, 8 * k + 2 * b:8 * k + 2 * b + 1],
                                                  rstd[:, 4 * k + b:4 * k + b + 1], ALU.subtract, ALU.mult)
                ins.then_inc(S["xn_ready"], 1)

            def b_split(lt, k, seen):
                bpsum = bank(6)[:, 0:P]
                dve.wait_ge(S["bc_psum"], lt + 1)
                if seen == 2:
                    dve.wait_ge(stored[k], 16 * STORES * before(lt, k))
                nc.vector.tensor_copy(bp_view(k)[:, 0], bpsum).then_inc(S["bhi_ready"], 1)
                dve.wait_ge(S["bhi_ready"], lt + 1)
                nc.vector.tensor_tensor(bres, bpsum, bp_view(k)[:, 0], ALU.subtract)\
                    .then_inc(S["bres_ready"], 1)
                dve.wait_ge(S["bres_ready"], lt + 1)
                nc.vector.tensor_copy(bp_view(k)[:, 1], bres).then_inc(S["bmid_ready"], 1)
                dve.wait_ge(S["bmid_ready"], lt + 1)
                nc.vector.tensor_tensor(bp_view(k)[:, 2], bres, bp_view(k)[:, 1], ALU.subtract)\
                    .then_inc(S["blo_ready"], 1)

            def start():
                normalise(0, 0, 0)
                b_split(0, 0, 0)

            def step(lt, k, seen, more):
                if more:
                    normalise(lt + 1, 1 - k, min(seen + 1, 2))
                dve.wait_ge(S["sp_ln"], lt + 1)
                if seen == 2:
                    dve.wait_ge(S["dlo_ready"], lt - 1)
                nc.vector.scalar_tensor_tensor(out=delta[k], in0=bank(4, 2), scalar=0.0, in1=sp,
                                               op0=ALU.max, op1=ALU.add).then_inc(S["delta_ready"], 1)
                dve.wait_ge(S["delta_ready"], lt + 1)
                nc.vector.tensor_tensor(du[k], delta[k], xn[k], ALU.mult).then_inc(S["du_ready"], 1)
                dve.wait_ge(S["du_ready"], lt + 1)
                if seen == 2:
                    dve.wait_ge(stored[k], 16 * STORES * before(lt, k))
                nc.vector.tensor_copy(up_view(k)[:, 0], du[k]).then_inc(S["uhi_ready"], 1)
                dve.wait_ge(S["uhi_ready"], lt + 1)
                nc.vector.tensor_tensor(ures, du[k], up_view(k)[:, 0], ALU.subtract)\
                    .then_inc(S["ures_ready"], 1)
                dve.wait_ge(S["ures_ready"], lt + 1)
                nc.vector.tensor_copy(up_view(k)[:, 1], ures).then_inc(S["umid_ready"], 1)
                dve.wait_ge(S["umid_ready"], lt + 1)
                nc.vector.tensor_tensor(up_view(k)[:, 2], ures, up_view(k)[:, 1], ALU.subtract)\
                    .then_inc(S["ulo_ready"], 1)
                if more:
                    b_split(lt + 1, 1 - k, min(seen + 1, 2))
                if seen < 2:
                    zero((delta_mov[1], du_mov[0])[seen])
                elif more == 1:
                    zero(du_mov[1])

            piped(dve, start, step)

            p_done(dve)

            def m_pair(it, first, last):
                for k in range(2):
                    c = 2 * it + k
                    for s in range(SUBS):
                        for g in range(GROUPS):
                            step = s * GROUPS + g
                            G = c * STEPS + step
                            dve.wait_ge(S["decay_reset"], G + 1)
                            dve.wait_ge(S["b_ready"], G + 1)
                            if g == 0 and not (first and k == 0):
                                dve.wait_ge(S["contract_done"], 2 * c + s - 1)
                            seg = slice(g * GD * TS, (g + 1) * GD * TS)
                            firsts = sub(psum, 0, P, 2 * (step % 2) * BANK, (TS, GD))
                            nc.vector.tensor_tensor(firsts, firsts, carry[:, g, :], ALU.add)\
                                .then_inc(S["carried"], 1)
                            dve.wait_ge(S["carried"], G + 1)
                            nc.vector.tensor_tensor_scan(
                                state[s][:, seg], decay[k][:, (s * D + g * GD) * TS:(s * D + (g + 1) * GD) * TS],
                                psum[:, 2 * (step % 2) * BANK:(2 * (step % 2) + 2) * BANK], 0.0,
                                ALU.mult, ALU.add).then_inc(S["scan_done"], 1)

            tiles(dve, CHUNKS // 2, m_pair)
            phase_f_dve(dve)


_INS = ["L0_attn_x", "L0_attn_W_bc", "L0_attn_W_dt", "L0_attn_b_dt", "L0_attn_A_log", "L0_attn_D_param",
        "L0_ffn_conv_w", "L0_ffn_Wq", "L0_ffn_Wk", "L0_ffn_Wv", "L0_ffn_Wg", "L0_ffn_router_w", "L0_ffn_Wout"]


def kernel(**inputs):
    import numpy as _np
    import concourse.bacc as _bacc
    from concourse.bass_utils import run_bass_kernel_spmd as _run

    nc = _bacc.Bacc("TRN2", target_bir_lowering=False, num_devices=1)
    arrays, args = {}, []
    for name in _INS:
        a = _np.ascontiguousarray(inputs[name])
        arrays[f"in_{name}"] = a
        args.append(nc.dram_tensor(f"in_{name}", a.shape, F32, kind="ExternalInput").ap())
    out = nc.dram_tensor("out_0", (B, L, D), F32, kind="ExternalOutput").ap()
    build(nc, *args, out)
    r = _run(nc, [arrays], core_ids=[0])
    return r.results[0]["out_0"]
```

```python
import math
from contextlib import ExitStack

import concourse.bass as bass
from concourse import mybir

F32 = mybir.dt.float32
BF16 = mybir.dt.bfloat16
ALU = mybir.AluOpType
ACT = mybir.ActivationFunctionType
AX = mybir.AxisListType

B, L, D, N, R = 4, 1024, 256, 32, 64
P = 128
EPS = 1e-5
LT = L // P
TC = 32
TS = 16
CHUNKS = L // TC
SUBS = TC // TS
GROUPS = 4
GD = D // GROUPS
DQ, DG = 4, D // 4
UNIT_DG = 4
UNITS = DG // UNIT_DG
STEPS = SUBS * GROUPS
UNITS_PER_STEP = UNITS // STEPS
TERMS = 6
MOVING_PART = (0, 0, 0, 1, 1, 2)
STATION_PART = (0, 1, 2, 0, 1, 0)
ROWS = DQ * TERMS * B
QROWS = TERMS * B
DU_COLS = TC // 4 * D
BANK = 512
H, HK, HV = 16, 8, 16
DK = H * HK
COL_V, COL_DIFF, COL_K = 0, D, D + H
COL_Q, COL_G = COL_K + DK, COL_K + 2 * DK
WCOLS = COL_G + D
ROPE_BASE = 10000.0


def sub(t, p0, n, off, *dims, pstep=1):
    a = t[p0:p0 + 1]
    return bass.AP(a.tensor, a.offset + off, [[a.ap[0][0] * pstep, n], *[list(d) for d in dims]])


def dram(t, off, *dims):
    return bass.AP(t.tensor, off, [list(d) for d in dims])


def build(nc, x, W_bc, W_dt, b_dt, A_log, D_param, conv_w, Wq, Wk, Wv, Wg, router_w, Wout, out):
    ctx = ExitStack()
    with ctx:
        def sb(name, shape, dt=F32):
            return ctx.enter_context(nc.sbuf_tensor(name, shape, dt))

        def sem(name):
            return ctx.enter_context(nc.semaphore(name))

        def scratch(name, shape, dt):
            return nc.dram_tensor(name, shape, dt).ap()

        delta_terms_d = scratch("delta_terms", [TERMS, B, L, D], BF16)
        du_terms_d = scratch("du_terms", [TERMS, B, L, D], BF16)
        b_terms_d = scratch("b_terms", [TERMS, B, L, P], BF16)
        a_terms_d = scratch("a_terms", [TERMS, D, N], BF16)
        base_d = scratch("base", [B, L, D], F32)
        y_d = scratch("y", [B, L, D], F32)

        SLOT = 1024
        NSLOT = 24
        arena = sb("arena", [P, NSLOT * SLOT])

        def slot(i, n=1):
            return arena[:, i * SLOT:(i + n) * SLOT]

        CHUNK_ELEMS = D * TC
        decay = [arena[:, k * CHUNK_ELEMS:(k + 1) * CHUNK_ELEMS] for k in range(2)]
        state = [arena[:, 2 * CHUNK_ELEMS + k * D * TS:2 * CHUNK_ELEMS + (k + 1) * D * TS] for k in range(2)]

        delta_mov = [sb(f"delta_mov{k}", [P, DQ * TC * DG], BF16) for k in range(2)]
        du_mov = [sb(f"du_mov{k}", [P, (TC // 4) * 4 * D], BF16) for k in range(2)]
        b_sta = [sb(f"b_sta{k}", [P, (TC // 4) * P], BF16) for k in range(2)]
        a_sta = sb("a_sta", [P, DG * P], BF16)
        c_sta = [sb(f"c_sta{k}", [P, TC * 32]) for k in range(2)]
        c_all = sb("c_all", [P, L])
        carry = sb("carry", [P, 4, GD])
        y_rows = [sb(f"y_rows{k}", [P, D]) for k in range(2)]
        ident = sb("ident", [P, P])
        pacer = sb("pacer", [P, 1])
        zeros = sb("zeros", [P, GD])
        own_batch = sb("own_batch", [P, B])

        psum = ctx.enter_context(nc.psum_tensor("psum", [P, 8 * BANK], F32))

        def bank(i, n=1):
            return psum[:, i * BANK:(i + n) * BANK]

        names = """own_made b_filled a_sta_zeroed c_sta_zeroed carried f_seed f_newton f_keep wv_sum wv_mean
            wv_centred weights_loaded ident_zeroed ident_ready zeros_ready wT_psum wT_ready a_exp a_neg a_hi
            a_res a_mid a_stored a_sta_loaded ones_ready stats_done var_done veps_ready rstd_ready xn_ready
            xnT_psum xnT_ready dtr_psum bc_psum dtr_ready c_ready dt_psum sp_abs sp_exp sp_ln delta_ready
            du_ready dhi_ready dres_ready dmid_ready dlo_ready uhi_ready ures_ready umid_ready ulo_ready
            bhi_ready bres_ready bmid_ready blo_ready xd_ready base_ready half_ready args_ready exp_done
            b_ready carry_ready decay_reset scan_done contract_done cpad_ready y_evac fw_loaded
            rd_ready wvT_psum wvT_ready wvd_psum wvd_ready tables_ready f_x1 f_stats f_aggr f_veps f_rstd
            f_xn f_xnT f_w1 f_conv f_xcT f_proj_qkv f_q f_g f_df f_rope_c f_rope_s f_rope f_ind f_eq f_eqm
            f_cnt f_rcp f_th f_sm f_wt f_prod f_qk f_cf f_av f_sq f_var f_gveps f_gn f_gated f_gT_psum
            f_gT f_outp f_out""".split()
        S = {n: sem(n) for n in names}
        x_loaded = [sem(f"x_loaded{k}") for k in range(2)]
        b_stored = [sem(f"b_stored{k}") for k in range(2)]
        base_stored = [sem(f"base_stored{k}") for k in range(2)]
        delta_stored = [sem(f"delta_stored{k}") for k in range(2)]
        du_stored = [sem(f"du_stored{k}") for k in range(2)]
        md_loaded = [sem(f"md_loaded{k}") for k in range(2)]
        mu_loaded = [sem(f"mu_loaded{k}") for k in range(2)]
        y_stored = [sem(f"y_stored{k}") for k in range(2)]
        f_loaded = [sem(f"f_loaded{k}") for k in range(2)]
        out_stored = [sem(f"out_stored{k}") for k in range(2)]

        x_t = [slot(0), slot(1)]
        xn = [slot(2), slot(3)]
        xnT = [slot(4), slot(5)]
        dtr = [slot(6)[:, 0:512], slot(6)[:, 512:1024]]
        sp = slot(7)
        delta = [slot(8), slot(9)]
        du = [slot(10), slot(11)]
        dres, ures = slot(12), slot(13)
        base = [slot(14), slot(15)]
        dparts = [slot(16, 3)[:, k * 1536:(k + 1) * 1536].bitcast(BF16) for k in range(2)]
        uparts = [slot(19, 3)[:, k * 1536:(k + 1) * 1536].bitcast(BF16) for k in range(2)]
        misc = slot(22, 2)
        bparts = [misc[:, k * 192:(k + 1) * 192].bitcast(BF16) for k in range(2)]
        bres = misc[:, 384:512]
        w_bcT = misc[:, 512:768]
        w_dtT = misc[0:R, 768:1024]
        w_dtT_b = misc[0:R + 1, 768:1024]
        d_bc = misc[:, 1024:1280]
        bdt_row = misc[R:R + 1, 768:1024]
        stats = misc[:, 1664:1664 + 48]
        mv = misc[:, 1712:1728]
        rstd = misc[:, 1728:1736]
        veps = misc[:, 1736:1744]
        half_neg = misc[:, 1744:1748]
        w_bc_n = ures[:, 0:256]
        w_dt_n = ures[:, 256:384]
        a_log_n = dres[:, 0:64]
        a_neg = dres[:, 64:128]
        a_res = dres[:, 128:192]
        a_parts = dres[:, 256:352].bitcast(BF16)


        fy = [slot(0), slot(1)]
        f_in = du_mov[0][:, :].bitcast(F32)
        fraw = [f_in[:, k * SLOT:(k + 1) * SLOT] for k in range(2)]
        fbase = [f_in[:, (2 + k) * SLOT:(3 + k) * SLOT] for k in range(2)]
        fxn = slot(4)
        fxc = slot(5)
        fxcT = slot(6)
        fqk = [slot(7), slot(8)]
        fv = [slot(9), slot(10)]
        fg = [slot(11), slot(12)]
        frc, frs, fqkr = slot(13), slot(14), slot(15)
        fprod = slot(16, 2)
        ftmp = slot(18)
        AV_TMP = (None, 18, 3, 16)
        fo = slot(19)
        fgt = slot(20)
        fgT = slot(21)
        fout = [slot(22), slot(23)]

        def before(lt, k):
            return (lt - k) // 2

        def piped(eng, start, step, peeled=1, tail=2):
            start()
            for lt in range(2 * peeled):
                step(lt, lt % 2, lt, tail)
            with eng.Fori(peeled, (LT - tail) // 2) as it:
                for k in range(2):
                    step(2 * it + k, k, 2 * peeled, tail)
            for lt in range(LT - tail, LT):
                step(lt, lt % 2, 2 * peeled, LT - 1 - lt)

        def settle(eng):
            eng.wait_ge(S["weights_loaded"], 16 * 5)

        FP = LT // 2
        fw_t = delta_mov[0][:, :].bitcast(F32)
        fs_t = delta_mov[1][:, :].bitcast(F32)
        LH = B * H
        O_IND, O_WT, O_EQ, O_CF, O_SUM, O_RSTD = 192, 512, 576, 832, 1344, 1536
        O_CONV, O_ROUTE, O_ROUTE_DIFF, O_COS, O_SIN, O_CAUSAL = 2800, 2804, 2808, 2848, 2864, 2880
        w_all = fw_t[:, 0:2 * WCOLS]
        w_out = fw_t[:, 1600:1600 + 2 * D]
        wvT = fw_t[:, 2200:2200 + 2 * D]
        conv = fw_t[:, O_CONV:O_CONV + 4]
        rt = fw_t[:, O_ROUTE:O_ROUTE + 4]
        rdc = fw_t[:, O_ROUTE_DIFF:O_ROUTE_DIFF + 2]
        rd = fw_t[:, 2816:2848]
        cos_t = fw_t[:, O_COS:O_COS + 16]
        sin_t = fw_t[:, O_SIN:O_SIN + 16]
        causal = fw_t[:, O_CAUSAL:O_CAUSAL + B * B]
        fhalf = fw_t[:, 2896:2960]
        fstats = fs_t[:, 0:24]
        fmv = fs_t[:, 24:32]
        fveps = fs_t[:, 32:36]
        frstd = fs_t[:, 36:40]
        fdf = [fs_t[:, 64:128], fs_t[:, 128:192]]
        find = fs_t[:, O_IND:O_IND + LH]
        fabs = fs_t[:, 256:320]
        fsm = fs_t[:, 320:384]
        fcnt = fs_t[:, 384:448]
        frcp = fs_t[:, 448:512]
        fwt = fs_t[:, O_WT:O_WT + LH]
        feq = fs_t[:, O_EQ:O_EQ + B * LH]
        fcf = fs_t[:, O_CF:O_CF + B * LH]
        fqkd = fs_t[:, 1088:1344]
        fsum = fs_t[:, O_SUM:O_SUM + LH]
        fgv = fs_t[:, 1472:1536]
        fgr = fs_t[:, O_RSTD:O_RSTD + LH]
        SCALE = HK ** -0.5
        NEWTON = 3
        FLOADS = 7

        def m_done(eng):
            for k in range(2):
                eng.wait_ge(y_stored[k], 16 * 4 * (CHUNKS // 2))

        def dims(t, off, *d):
            return sub(t, 0, P, off, *d)

        def load_f_weights(eng):
            ld = lambda dst, src: eng.dma_start(dst, src).then_inc(S["fw_loaded"], 16)
            wv = w_all.rearrange("p (h n) -> p h n", h=2)
            for w, o, n in ((Wq, COL_Q, DK), (Wk, COL_K, DK), (Wv, COL_V, D), (Wg, COL_G, D)):
                ld(wv[:, :, o:o + n], w.rearrange("(h p) n -> p h n", p=P))
            ld(w_out.rearrange("p (h n) -> p h n", h=2), Wout.rearrange("(h p) n -> p h n", p=P))
            ld(conv.rearrange("p (h n) -> p h n", h=2), conv_w.rearrange("(h p) n -> p h n", p=P))
            ld(rt.rearrange("p (h n) -> p h n", h=2),
               dram(router_w, 0, (2, P), (2 * P, 2), (1, 2)))

        def f_load(eng, lt, k):
            for tile, source in ((fraw[k], y_d), (fbase[k], base_d)):
                eng.dma_start(tile.rearrange("p (b d) -> p b d", b=B),
                              dram(source, lt * (P * D), (D, P), (L * D, B), (1, D))).then_inc(f_loaded[k], 16)

        def phase_f_sync(eng):
            load = lambda lt, k: f_load(eng, lt, k)

            def start():
                eng.wait_ge(S["f_x1"], 1)
                load(2, 0)
                m_done(eng)

            def step(lt, k, seen, more):
                if more >= 3:
                    settle(eng)
                    eng.wait_ge(S["f_x1"], lt + 2)
                    load(lt + 3, 1 - k)
                settle(eng)
                eng.wait_ge(S["f_out"], lt + 1)
                eng.dma_start(dram(out, lt * (P * D), (D, P), (L * D, B), (1, D)),
                              fout[k].rearrange("p (b d) -> p b d", b=B)).then_inc(out_stored[k], 16)

            piped(eng, start, step, 1, 4)
            for k in range(2):
                eng.wait_ge(out_stored[k], 16 * FP)

        def rope_table(pool, l):
            for i in range(HK // 2):
                f = l / ROPE_BASE ** (2 * i / HK)
                o = l * (HK // 2) + i
                pool.memset(cos_t[:, o:o + 1], math.cos(f))
                pool.memset(sin_t[:, o:o + 1], math.sin(f))

        def causal_mask(pool):
            pool.memset(causal, 0.0).then_inc(S["tables_ready"], 1)
            pool.wait_ge(S["tables_ready"], 1)
            for l in range(B):
                pool.memset(causal[:, l * B:l * B + l + 1], 1.0)
            pool.memset(fhalf, -0.5).then_inc(S["tables_ready"], 1)

        def routing_weights(pool):
            pool.memset(fqkd, 0.0).then_inc(S["tables_ready"], 1)
            pool.wait_ge(S["fw_loaded"], 16 * FLOADS)
            pool.tensor_tensor(rdc, dims(fw_t, O_ROUTE + 1, (2, 2)), dims(fw_t, O_ROUTE, (2, 2)), ALU.subtract)\
                .then_inc(S["rd_ready"], 1)
            pool.wait_ge(S["rd_ready"], 1)
            pool.tensor_copy(rd.rearrange("p (a h) -> p a h", a=2), dims(fw_t, O_ROUTE_DIFF, (1, 2), (0, H)))\
                .then_inc(S["rd_ready"], 1)
            pool.wait_ge(S["rd_ready"], 2)
            rdv = rd.rearrange("p (a h) -> p a h", a=2)
            pool.affine_select(out=rdv, in_=rdv, compare_op=ALU.is_ge, fill=0.0, base=0,
                               pattern=[[P, 2], [-HV, H]], channel_multiplier=1).then_inc(S["rd_ready"], 1)
            pool.wait_ge(S["rd_ready"], 3)
            pool.affine_select(out=rdv, in_=rdv, compare_op=ALU.is_ge, fill=0.0, base=HV - 1,
                               pattern=[[-P, 2], [HV, H]], channel_multiplier=-1).then_inc(S["rd_ready"], 1)

        def phase_f_pool(pool):
            pool.wait_ge(S["tables_ready"], 3)

            def x1(lt, k, seen):
                pool.wait_ge(f_loaded[k], 32 * (before(lt, k) + 1))
                if seen >= 2:
                    pool.wait_ge(S["f_xn"], lt - 1)
                    pool.wait_ge(S["f_keep"], lt - 1)
                pool.tensor_tensor(fy[k], fraw[k], fbase[k], ALU.add).then_inc(S["f_x1"], 1)

            def rstds(lt):
                pool.wait_ge(S["f_veps"], lt + 1)
                pool.tensor_tensor(frstd, fveps, fhalf[:, 0:4], ALU.pow).then_inc(S["f_rstd"], 1)

            def gate(lt, k, seen):
                pool.wait_ge(S["f_newton"], 3 * NEWTON * (lt + 1))
                pool.tensor_tensor(fo.rearrange("p (c e) -> p c e", e=HV), fo.rearrange("p (c e) -> p c e", e=HV),
                                   dims(fs_t, O_RSTD, (1, LH), (0, HV)), ALU.mult).then_inc(S["f_gn"], 1)
                pool.wait_ge(S["f_g"], 4 * lt + 4)
                pool.wait_ge(S["f_gn"], lt + 1)
                if seen:
                    pool.wait_ge(S["f_gT_psum"], 2 * lt)
                pool.tensor_tensor(fgt, fo, fg[k], ALU.mult).then_inc(S["f_gated"], 1)

            def start():
                x1(0, 0, 0)
                x1(1, 1, 0)
                rstds(0)
                rstds(1)

            def step(lt, k, seen, more):
                def rotate(dst, table, name):
                    pool.tensor_tensor(dst.rearrange("p (l h i) -> p l h i", l=B, i=HK // 2),
                                       fqk[k].rearrange("p (l h i) -> p l h i", l=B, i=HK // 2),
                                       dims(fw_t, table, (HK // 2, B), (0, 4 * H), (1, HK // 2)), ALU.mult)\
                        .then_inc(S[name], 1)

                pool.wait_ge(S["f_q"], 4 * lt + 4)
                if seen:
                    pool.wait_ge(S["f_rope"], 2 * lt)
                rotate(frc, O_COS, "f_rope_c")
                rotate(frs, O_SIN, "f_rope_s")
                if seen:
                    gate(lt - 1, 1 - k, seen - 1)
                if more == 2:
                    x1(lt + 2, k, 2)
                    rstds(lt + 2)

            piped(pool, start, step, 1)
            gate(LT - 1, 1, 2)

        def routing_columns(pe):
            pe.wait_ge(S["fw_loaded"], 16 * FLOADS)
            pe.wait_ge(S["exp_done"], CHUNKS * UNITS)
            for a in range(2):
                for h in range(2):
                    tr = nc.tensor.transpose(bank(4)[:, (a * 2 + h) * P:(a * 2 + h + 1) * P],
                                             w_all[:, h * WCOLS + COL_V + a * P:h * WCOLS + COL_V + (a + 1) * P],
                                             ident[:, :])
            tr.then_inc(S["wvT_psum"], 1)
            pe.wait_ge(S["wvT_ready"], 1)
            pe.wait_ge(S["rd_ready"], 4)
            for h in range(2):
                for a in range(2):
                    mm = nc.tensor.matmul(bank(5)[:, h * H:(h + 1) * H], wvT[:, (a * 2 + h) * P:(a * 2 + h + 1) * P],
                                          rd[:, a * H:(a + 1) * H], start=(a == 0), stop=(a == 1))
            mm.then_inc(S["wvd_psum"], 1)

        def phase_f_pe(pe):
            def transposes(lt, seen):
                pe.wait_ge(S["f_xn"], lt + 1)
                if seen:
                    pe.wait_ge(S["f_conv"], 2 * lt)
                    pe.wait_ge(S["f_w1"], 2 * lt)
                for h in range(2):
                    for b in range(B):
                        o = (h * B + b) * P
                        tr = nc.tensor.transpose(psum[:, o:o + P], fxn[:, b * D + h * P:b * D + (h + 1) * P],
                                                 ident[:, :])
                    tr.then_inc(S["f_xnT"], 1)

            def project(lt, seen, b):
                ba = 2 + 2 * (b % 2)
                if b == 0:
                    pe.wait_ge(S["f_xcT"], lt + 1)
                if seen or b >= 2:
                    n = 4 * lt + b - 1
                    pe.wait_ge(S["f_df"], n)
                for h in range(2):
                    xc = fxcT[:, (h * B + b) * P:(h * B + b + 1) * P]
                    nc.tensor.matmul(bank(ba)[:, 0:COL_K], xc, w_all[:, h * WCOLS:h * WCOLS + COL_K],
                                     start=(h == 0), stop=(h == 1))
                    mm = nc.tensor.matmul(bank(ba + 1), xc, w_all[:, h * WCOLS + COL_K:(h + 1) * WCOLS],
                                          start=(h == 0), stop=(h == 1))
                mm.then_inc(S["f_proj_qkv"], 1)

            def start():
                transposes(0, 0)
                pe.wait_ge(S["wvd_ready"], 1)
                pe.wait_ge(S["wv_centred"], 1)
                for b in range(B):
                    project(0, 0, b)
                transposes(1, 1)
                pe.wait_ge(S["y_evac"], CHUNKS)

            def gate_transposes(lt, seen):
                pe.wait_ge(S["f_gated"], lt + 1)
                if seen:
                    pe.wait_ge(S["f_out"], lt)
                for h in range(2):
                    for b in range(B):
                        o = 6 * BANK + (h * B + b) * P
                        tr = nc.tensor.transpose(psum[:, o:o + P], fgt[:, b * D + h * P:b * D + (h + 1) * P],
                                                 ident[:, :])
                    tr.then_inc(S["f_gT_psum"], 1)

            def output(lt):
                pe.wait_ge(S["f_gT"], 2 * lt + 2)
                for b in range(B):
                    for h in range(2):
                        mm = nc.tensor.matmul(psum[:, 6 * BANK + b * D:6 * BANK + (b + 1) * D],
                                              fgT[:, (h * B + b) * P:(h * B + b + 1) * P],
                                              w_out[:, h * D:(h + 1) * D], start=(h == 0), stop=(h == 1))
                mm.then_inc(S["f_outp"], 1)

            def step(lt, k, seen, more):
                if more:
                    project(lt + 1, 1, 0)
                if seen:
                    gate_transposes(lt - 1, seen - 1)
                if more:
                    project(lt + 1, 1, 1)
                if seen:
                    output(lt - 1)
                if more:
                    project(lt + 1, 1, 2)
                    project(lt + 1, 1, 3)
                if more == 2:
                    transposes(lt + 2, 1)

            piped(pe, start, step, 1)
            gate_transposes(LT - 1, 1)
            output(LT - 1)

        def copy_routing_columns(act):
            act.wait_ge(S["wvT_psum"], 1)
            nc.scalar.copy(wvT, bank(4)).then_inc(S["wvT_ready"], 1)
            act.wait_ge(S["wvd_psum"], 1)
            nc.scalar.copy(dims(fw_t, COL_DIFF, (WCOLS, 2), (1, H)),
                           bank(5)[:, 0:2 * H].rearrange("p (a h) -> p a h", a=2)).then_inc(S["wvd_ready"], 1)

        def phase_f_act(act):
            def taps(lt, seen):
                for h in range(2):
                    act.wait_ge(S["f_xnT"], 2 * lt + h + 1)
                    nc.scalar.activation(fxc[:, h * BANK:(h + 1) * BANK], bank(h), ACT.Copy,
                                         scale=conv[:, 2 * h + 1:2 * h + 2]).then_inc(S["f_w1"], 1)

            def conv_silu(lt, seen):
                act.wait_ge(S["f_conv"], 2 * lt + 2)
                if seen:
                    act.wait_ge(S["f_proj_qkv"], 4 * lt)
                nc.scalar.activation(fxcT, fxc, ACT.Silu).then_inc(S["f_xcT"], 1)

            def evacuate(lt, k, seen, b):
                ba = 2 + 2 * (b % 2)
                act.wait_ge(S["f_proj_qkv"], 4 * lt + b + 1)
                if b == 0 and seen == 2:
                    act.wait_ge(S["f_gated"], lt - 1)
                nc.scalar.copy(fqk[k][:, b * D + DK:(b + 1) * D], bank(ba + 1)[:, 0:DK])
                nc.scalar.activation(fqk[k][:, b * D:b * D + DK], bank(ba + 1)[:, DK:2 * DK], ACT.Silu)\
                    .then_inc(S["f_q"], 1)
                nc.scalar.activation(fg[k][:, b * D:(b + 1) * D], bank(ba + 1)[:, 2 * DK:BANK], ACT.Silu)\
                    .then_inc(S["f_g"], 1)
                nc.scalar.copy(fv[k][:, b * D:(b + 1) * D], bank(ba)[:, COL_V:COL_V + D])
                nc.scalar.copy(fdf[k][:, b * H:(b + 1) * H], bank(ba)[:, COL_DIFF:COL_DIFF + H])\
                    .then_inc(S["f_df"], 1)

            def keep(lt, k, seen):
                if seen == 0:
                    act.wait_ge(S["f_x1"], lt + 1)
                if seen == 2:
                    act.wait_ge(out_stored[k], 16 * before(lt, k))
                nc.scalar.copy(fout[k], fy[k]).then_inc(S["f_keep"], 1)

            def gT_copies(lt, seen):
                for h in range(2):
                    act.wait_ge(S["f_gT_psum"], 2 * lt + h + 1)
                    if seen and h == 0:
                        act.wait_ge(S["f_outp"], lt)
                    nc.scalar.copy(fgT[:, h * BANK:(h + 1) * BANK], bank(6 + h)).then_inc(S["f_gT"], 1)

            def start():
                taps(0, 0)
                conv_silu(0, 0)
                for b in range(B):
                    evacuate(0, 0, 0, b)
                taps(1, 1)
                conv_silu(1, 1)

            def step(lt, k, seen, more):
                ahead = (lt + 1, 1 - k, min(seen + 1, 2))
                act.wait_ge(S["f_df"], 4 * lt + 4)
                if seen:
                    act.wait_ge(S["f_sm"], lt)
                nc.scalar.activation(fabs, fdf[k], ACT.Abs, scale=0.5).then_inc(S["f_th"], 1)
                act.wait_ge(S["f_th"], 2 * lt + 1)
                nc.scalar.activation(fabs, fabs, ACT.Tanh).then_inc(S["f_th"], 1)
                keep(lt, k, seen)
                if more:
                    evacuate(*ahead, 0)
                if seen:
                    gT_copies(lt - 1, seen - 1)
                if more:
                    evacuate(*ahead, 1)
                act.wait_ge(S["f_av"], 7 * lt + 7)
                nc.scalar.activation(ftmp, fo, ACT.Square).then_inc(S["f_sq"], 1)
                if more:
                    evacuate(*ahead, 2)
                    evacuate(*ahead, 3)
                if more == 2:
                    taps(lt + 2, 2)
                    conv_silu(lt + 2, 2)

            piped(act, start, step, 1)
            gT_copies(LT - 1, 1)

        def phase_f_dve(dve):
            V = nc.vector

            def centre_v_columns():
                dve.wait_ge(S["fw_loaded"], 16 * FLOADS)
                dve.wait_ge(S["wvT_psum"], 1)
                wv_heads = dims(fw_t, COL_V, (WCOLS, 2), (HV, H), (1, HV))
                head_means = dims(fs_t, O_SUM, (H, 2), (1, H), (0, HV))
                V.tensor_reduce(fsum[:, 0:2 * H].rearrange("p (a h) -> p a h", a=2), wv_heads, AX.X, ALU.add)\
                    .then_inc(S["wv_sum"], 1)
                dve.wait_ge(S["wv_sum"], 1)
                V.tensor_scalar(fsum[:, 0:2 * H], fsum[:, 0:2 * H], 1.0 / HV, None, ALU.mult).then_inc(S["wv_mean"], 1)
                dve.wait_ge(S["wv_mean"], 1)
                V.tensor_tensor(wv_heads, wv_heads, head_means, ALU.subtract).then_inc(S["wv_centred"], 1)

            def statistics(lt, k):
                dve.wait_ge(S["f_x1"], lt + 1)
                for b in range(B):
                    ins = V.bn_stats(fstats[:, 6 * b:6 * b + 6], fy[k][:, b * D:(b + 1) * D])
                ins.then_inc(S["f_stats"], 1)
                dve.wait_ge(S["f_stats"], lt + 1)
                nc.vector.memset(pacer[:, :], 0.0)
                for b in range(B):
                    ins = V.bn_aggr(fmv[:, 2 * b:2 * b + 2], fstats[:, 6 * b:6 * b + 6])
                ins.then_inc(S["f_aggr"], 1)
                dve.wait_ge(S["f_aggr"], lt + 1)
                V.tensor_scalar(fveps, fmv[:, 1:8:2], EPS, None, ALU.add).then_inc(S["f_veps"], 1)

            def normalise(lt, k, seen, rows=range(B)):
                if 0 in rows:
                    dve.wait_ge(S["f_rstd"], lt + 1)
                    if seen:
                        dve.wait_ge(S["f_xnT"], 2 * lt)
                for b in rows:
                    ins = V.tensor_scalar(fxn[:, b * D:(b + 1) * D], fy[k][:, b * D:(b + 1) * D],
                                          fmv[:, 2 * b:2 * b + 1], frstd[:, b:b + 1], ALU.subtract, ALU.mult)
                if B - 1 in rows:
                    ins.then_inc(S["f_xn"], 1)

            def conv_taps(lt):
                for h in range(2):
                    dve.wait_ge(S["f_w1"], 2 * lt + h + 1)
                    later = fxc[:, h * BANK + P:(h + 1) * BANK]
                    V.scalar_tensor_tensor(out=later, in0=bank(h)[:, 0:3 * P], scalar=conv[:, 2 * h:2 * h + 1],
                                           in1=later, op0=ALU.mult, op1=ALU.add).then_inc(S["f_conv"], 1)

            def residual(lt, k):
                dve.wait_ge(S["f_outp"], lt + 1)
                dve.wait_ge(S["f_keep"], lt + 1)
                V.tensor_tensor(fout[k], fout[k], bank(6, 2), ALU.add).then_inc(S["f_out"], 1)

            def start():
                statistics(0, 0)
                normalise(0, 0, 0)
                centre_v_columns()
                dve.wait_ge(S["f_xn"], 1)
                statistics(1, 1)
                conv_taps(0)
                normalise(1, 1, 1)
                conv_taps(1)

            def step(lt, k, seen, more):
                def done(ins, name, n=1):
                    ins.then_inc(S[name], 1)
                    dve.wait_ge(S[name], n * lt + n if n == 1 else n)

                dve.wait_ge(S["f_df"], 4 * lt + 4)
                hk = HK // 2
                half = lambda t, j: t.rearrange("p (h j i) -> p h j i", j=2, i=hk)[:, :, j, :]
                eq3 = lambda t: t.rearrange("p (l m h) -> p l m h", l=B, m=B)

                def qk_product(l):
                    n = l + 1
                    off = (l * n // 2) * DK
                    return V.tensor_tensor(fprod[:, off:off + n * DK].rearrange("p (m c) -> p m c", m=n),
                                           dims(arena, 15 * SLOT + l * D, (0, n), (1, DK)),
                                           dims(arena, 15 * SLOT + DK, (D, n), (1, DK)), ALU.mult)

                V.tensor_scalar(find, fdf[k], 0.0, None, ALU.is_gt).then_inc(S["f_ind"], 1)
                dve.wait_ge(S["f_rope_s"], lt + 1)
                dve.wait_ge(S["f_rope_c"], lt + 1)
                V.tensor_tensor(half(fqkr, 0), half(frc, 0), half(frs, 1), ALU.subtract).then_inc(S["f_rope"], 1)
                dve.wait_ge(S["f_ind"], lt + 1)
                V.tensor_tensor(eq3(feq), dims(fs_t, O_IND, (H, B), (0, B), (1, H)),
                                dims(fs_t, O_IND, (0, B), (H, B), (1, H)), ALU.is_equal).then_inc(S["f_eq"], 1)
                V.tensor_tensor(half(fqkr, 1), half(frc, 1), half(frs, 0), ALU.add).then_inc(S["f_rope"], 1)
                dve.wait_ge(S["f_eq"], lt + 1)
                V.tensor_tensor(eq3(feq), eq3(feq), dims(fw_t, O_CAUSAL, (B, B), (1, B), (0, H)), ALU.mult)\
                    .then_inc(S["f_eqm"], 1)
                dve.wait_ge(S["f_th"], 2 * lt + 2)
                V.tensor_scalar(fsm, fabs, 0.5 * SCALE, 0.5 * SCALE, ALU.mult, ALU.add).then_inc(S["f_sm"], 1)
                dve.wait_ge(S["f_eqm"], lt + 1)
                V.tensor_reduce(fcnt.rearrange("p (l h) -> p l h", l=B),
                                dims(fs_t, O_EQ, (B * H, B), (1, H), (H, B)), AX.X, ALU.add).then_inc(S["f_cnt"], 1)
                dve.wait_ge(S["f_rope"], 2 * lt + 2)
                qk_product(0)
                dve.wait_ge(S["f_cnt"], lt + 1)
                V.reciprocal(frcp, fcnt).then_inc(S["f_rcp"], 1)
                qk_product(1)
                dve.wait_ge(S["f_rcp"], lt + 1)
                V.tensor_tensor(fwt, fsm, frcp, ALU.mult).then_inc(S["f_wt"], 1)
                qk_product(2)
                dve.wait_ge(S["f_wt"], lt + 1)
                V.tensor_tensor(eq3(feq), eq3(feq), dims(fs_t, O_WT, (H, B), (0, B), (1, H)), ALU.mult)
                ins = qk_product(3)
                ins.then_inc(S["f_prod"], 1)
                dve.wait_ge(S["f_prod"], lt + 1)
                off = 0
                for l in range(B):
                    n = l + 1
                    ins = V.tensor_reduce(fqkd[:, l * B * H:l * B * H + n * H],
                                          fprod[:, off:off + n * DK].rearrange("p (c e) -> p c e", e=HK),
                                          AX.X, ALU.add)
                    off += n * DK
                ins.then_inc(S["f_qk"], 1)
                dve.wait_ge(S["f_qk"], lt + 1)
                done(V.tensor_tensor(fcf, feq, fqkd, ALU.mult), "f_cf")
                if seen:
                    dve.wait_ge(S["f_gated"], lt)
                for m in range(B):
                    n = B - m
                    V.tensor_tensor(dims(arena, (AV_TMP[m] if m else 19) * SLOT, (D, n), (HV, H), (1, HV)),
                                    dims(fs_t, O_CF + m * B * H + m * H, (B * H, n), (1, H), (0, HV)),
                                    dims(arena, (9 + k) * SLOT + m * D, (0, n), (HV, H), (1, HV)), ALU.mult)\
                        .then_inc(S["f_av"], 1)
                for m in range(1, B):
                    dve.wait_ge(S["f_av"], 7 * lt + (2 if m == 1 else 3 + m))
                    V.tensor_tensor(fo[:, m * D:], fo[:, m * D:],
                                    arena[:, AV_TMP[m] * SLOT:AV_TMP[m] * SLOT + (B - m) * D], ALU.add)\
                        .then_inc(S["f_av"], 1)
                if more == 2:
                    statistics(lt + 2, k)
                heads = lambda t: t.rearrange("p (c e) -> p c e", e=HV)
                dve.wait_ge(S["f_sq"], lt + 1)
                done(V.tensor_reduce(fsum, heads(ftmp), AX.X, ALU.add), "f_var")
                done(V.tensor_scalar(fgv, fsum, 1.0 / HV, EPS, ALU.mult, ALU.add), "f_gveps")
                def beside(i):
                    if i < B and more == 2:
                        normalise(lt + 2, k, 2, [i])
                    if i == B and seen:
                        residual(lt - 1, 1 - k)

                v_bits, y_bits = fgv.bitcast(mybir.dt.int32), fgr.bitcast(mybir.dt.int32)
                V.tensor_scalar(y_bits, v_bits, 1, None, ALU.logical_shift_right).then_inc(S["f_seed"], 1)
                beside(0)
                dve.wait_ge(S["f_seed"], 2 * lt + 1)
                V.tensor_scalar(y_bits, y_bits, -1.0, float(0x5F3759DF), ALU.mult, ALU.add)\
                    .then_inc(S["f_seed"], 1)
                beside(1)
                dve.wait_ge(S["f_seed"], 2 * lt + 2)
                for n in range(NEWTON):
                    V.tensor_tensor(fsum, fgr, fgr, ALU.mult).then_inc(S["f_newton"], 1)
                    beside(2 + n)
                    dve.wait_ge(S["f_newton"], 3 * (NEWTON * lt + n) + 1)
                    V.scalar_tensor_tensor(out=fsum, in0=fsum, scalar=-0.5, in1=fgv, op0=ALU.mult, op1=ALU.mult)\
                        .then_inc(S["f_newton"], 1)
                    dve.wait_ge(S["f_newton"], 3 * (NEWTON * lt + n) + 2)
                    V.scalar_tensor_tensor(out=fgr, in0=fsum, scalar=1.5, in1=fgr, op0=ALU.add, op1=ALU.mult)\
                        .then_inc(S["f_newton"], 1)
                    dve.wait_ge(S["f_newton"], 3 * (NEWTON * lt + n) + 3)
                if more == 2:
                    conv_taps(lt + 2)

            piped(dve, start, step, 1)
            residual(LT - 1, 1)

        block = ctx.enter_context(nc.Block())

        def tiles(eng, count, body):
            body(0, True, False)
            with eng.Fori(1, count - 1) as it:
                body(it, False, False)
            body(count - 1, False, True)

        dp_view = lambda h: dparts[h].rearrange("p (s n) -> p s n", s=3)
        up_view = lambda h: uparts[h].rearrange("p (s n) -> p s n", s=3)
        bp_view = lambda h: bparts[h].rearrange("p (s n) -> p s n", s=3)

        PAIRS = LT // 2
        MD_LOADS = DQ
        MU_LOADS = 4 + SUBS

        def p_done(eng):
            for k in range(2):
                for terms in (b_stored, delta_stored, du_stored):
                    eng.wait_ge(terms[k], 16 * TERMS * PAIRS)
                eng.wait_ge(base_stored[k], 16 * PAIRS)

        @block.sync
        def _(sp_):
            def load_x(lt, k):
                sp_.dma_start(x_t[k].rearrange("p (b d) -> p b d", b=B),
                              dram(x, lt * (P * D), (D, P), (L * D, B), (1, D))).then_inc(x_loaded[k], 16)

            load_x(0, 0)
            sp_.dma_start(w_bc_n, W_bc[:, :]).then_inc(S["weights_loaded"], 16)
            sp_.dma_start(w_dt_n.rearrange("p (h r) -> p h r", h=2),
                          W_dt.rearrange("(h p) r -> p h r", p=P)).then_inc(S["weights_loaded"], 16)
            sp_.dma_start(a_log_n.rearrange("p (h r) -> p h r", h=2),
                          A_log.rearrange("(h p) r -> p h r", p=P)).then_inc(S["weights_loaded"], 16)
            sp_.dma_start(d_bc, dram(D_param, 0, (0, P), (1, D))).then_inc(S["weights_loaded"], 16)
            sp_.dma_start(bdt_row, dram(b_dt, 0, (0, 1), (1, D))).then_inc(S["weights_loaded"], 16)
            load_x(1, 1)
            sp_.wait_ge(S["zeros_ready"], 1)
            row_elems = TERMS * B * L * P // P // 6
            for i in range(6):
                sp_.dma_start(dram(b_terms_d, i * P * row_elems, (row_elems, P), (1, row_elems)),
                              delta_mov[0][:, 0:row_elems]).then_inc(S["b_filled"], 16)

            sp_.wait_ge(S["a_mid"], 2)
            for s in range(TERMS):
                sp_.dma_start(dram(a_terms_d, s * D * N, (N, P), (P * N, 2), (1, N)),
                              a_parts.rearrange("p (s h n) -> p s h n", s=3, h=2)[:, STATION_PART[s]])\
                   .then_inc(S["a_stored"], 16)

            def load_a_sta(q):
                sp_.wait_ge(S["a_stored"], 16 * TERMS)
                sp_.wait_ge(S["a_sta_zeroed"], 1)
                for b in range(B):
                    sp_.dma_start(sub(a_sta, q * QROWS + b, TERMS, b * N, (P, DG), (1, N), pstep=B),
                                  dram(a_terms_d, q * DG * N, (D * N, TERMS), (N, DG), (1, N)))\
                       .then_inc(S["a_sta_loaded"], 16)

            def store_terms(scratch_d, per_term, part, offset, dims_, order, count):
                for s in range(TERMS):
                    sp_.dma_start(dram(scratch_d, s * per_term + offset, *dims_), part(order[s]))\
                       .then_inc(count, 16)

            def store_base(lt, k):
                settle(sp_)
                sp_.wait_ge(S["base_ready"], lt + 1)
                sp_.dma_start(dram(base_d, lt * (P * D), (D, P), (L * D, B), (1, D)),
                              base[k].rearrange("p (b d) -> p b d", b=B)).then_inc(base_stored[k], 16)

            def store_b(lt, k):
                settle(sp_)
                sp_.wait_ge(S["blo_ready"], lt + 1)
                store_terms(b_terms_d, B * L * P, lambda p: bp_view(k)[:, p].rearrange("p (b n) -> p b n", b=B),
                            lt * (P * P), ((P, P), (L * P + N, B), (1, N)), STATION_PART, b_stored[k])

            def load_md(c, k):
                for q in range(DQ):
                    sp_.dma_start(sub(delta_mov[k], q * QROWS, QROWS, q * TC * DG, (1, TC * DG)),
                                  dram(delta_terms_d, q * DG + c * (TC * D), (L * D, QROWS), (D, TC), (1, DG)))\
                       .then_inc(md_loaded[k], 16)

            def load_mu(c, k):
                for j in range(4):
                    sp_.dma_start(sub(du_mov[k], j * QROWS, QROWS, j * DU_COLS, (4 * D, SUBS), (1, 4 * D)),
                                  dram(du_terms_d, j * 4 * D + c * (TC * D), (L * D, QROWS), (TS * D, SUBS),
                                       (1, 4 * D))).then_inc(mu_loaded[k], 16)
                for s in range(SUBS):
                    sp_.dma_start(sub(b_sta[k], 0, ROWS, s * 4 * P, (1, 4 * P)),
                                  dram(b_terms_d, s * TS * P + c * (TC * P), (4 * P, 4), (L * P, QROWS),
                                       (1, 4 * P))).then_inc(mu_loaded[k], 16)

            def step(lt, k, seen, more):
                if more:
                    store_base(lt + 1, 1 - k)
                if more >= 3:
                    load_x(lt + 3, 1 - k)
                if more:
                    store_b(lt + 1, 1 - k)
                if seen < 2:
                    load_a_sta(seen)
                elif 2 <= more < 4:
                    load_a_sta(more)
                if more == 1:
                    load_md(0, 0)
                    sp_.wait_ge(S["zeros_ready"], 3)
                    load_mu(0, 0)
                    load_md(1, 1)
                settle(sp_)
                sp_.wait_ge(S["dlo_ready"], lt + 1)
                store_terms(delta_terms_d, B * L * D,
                            lambda p: dp_view(k)[:, p].rearrange("p (b d) -> p b d", b=B),
                            lt * (P * D), ((D, P), (L * D, B), (1, D)), MOVING_PART, delta_stored[k])
                settle(sp_)
                sp_.wait_ge(S["ulo_ready"], lt + 1)
                store_terms(du_terms_d, B * L * D,
                            lambda p: up_view(k)[:, p].rearrange("p (b d) -> p b d", b=B),
                            lt * (P * D), ((D, P), (L * D, B), (1, D)), MOVING_PART, du_stored[k])

            def start():
                store_base(0, 0)
                load_x(2, 0)
                sp_.wait_ge(S["b_filled"], 16 * 6)
                store_b(0, 0)

            piped(sp_, start, step, 1, 4)

            def store_y(c, k):
                settle(sp_)
                sp_.wait_ge(S["y_evac"], c + 1)
                for j in range(4):
                    sp_.dma_start(dram(y_d, c * (TC * D) + j * D, (4 * D, TC // 4), (L * D, B), (1, D)),
                                  y_rows[k][32 * j:32 * j + 32, :]).then_inc(y_stored[k], 16)

            sp_.wait_ge(S["zeros_ready"], 4)
            load_mu(1, 1)

            def m_pair(it, first, last):
                for k in range(2):
                    c = 2 * it + k
                    if not last:
                        settle(sp_)
                        sp_.wait_ge(S["args_ready"], (c + 1) * UNITS)
                        load_md(c + 2, k)
                    if last and k == 0:
                        sp_.wait_ge(S["args_ready"], (c + 1) * UNITS)
                        load_f_weights(sp_)
                    if last and k == 1:
                        sp_.wait_ge(S["b_ready"], c * STEPS)
                        f_load(sp_, 0, 0)
                        f_load(sp_, 1, 1)
                    if not (first and k == 0):
                        store_y(c - 1, 1 - k)
                    if not last:
                        settle(sp_)
                        sp_.wait_ge(S["b_ready"], (c + 1) * STEPS)
                        load_mu(c + 2, k)

            tiles(sp_, CHUNKS // 2, m_pair)
            store_y(CHUNKS - 1, 1)
            phase_f_sync(sp_)

        @block.gpsimd
        def _(pool):
            pool.memset(ident[:, :], 0.0).then_inc(S["ident_zeroed"], 1)
            pool.wait_ge(S["ident_zeroed"], 1)
            pool.affine_select(out=ident[:, :], in_=ident[:, :], compare_op=ALU.not_equal, fill=1.0,
                               base=0, pattern=[[-1, P]], channel_multiplier=1).then_inc(S["ident_ready"], 1)
            pool.memset(zeros[:, :], 0.0)
            pool.memset(own_batch[:, :], 1.0).then_inc(S["own_made"], 1)
            pool.wait_ge(S["own_made"], 1)
            pool.affine_select(out=own_batch[:, :], in_=own_batch[:, :], compare_op=ALU.is_ge, fill=0.0,
                               base=0, pattern=[[-N, B]], channel_multiplier=1).then_inc(S["own_made"], 1)
            pool.wait_ge(S["own_made"], 2)
            pool.affine_select(out=own_batch[:, :], in_=own_batch[:, :], compare_op=ALU.is_ge, fill=0.0,
                               base=N - 1, pattern=[[N, B]], channel_multiplier=-1).then_inc(S["own_made"], 1)
            pool.memset(slot(6), 1.0).then_inc(S["ones_ready"], 1)
            pool.memset(half_neg, -0.5).then_inc(S["half_ready"], 1)
            pool.memset(a_sta[:, :].bitcast(F32), 0.0).then_inc(S["a_sta_zeroed"], 1)
            pool.wait_ge(S["half_ready"], 1)
            pool.wait_ge(S["weights_loaded"], 16 * 5)

            def rstds(lt, k):
                pool.wait_ge(S["veps_ready"], lt + 1)
                pool.tensor_tensor(rstd[:, 4 * k:4 * k + 4], veps[:, 4 * k:4 * k + 4], half_neg, ALU.pow)\
                    .then_inc(S["rstd_ready"], 1)

            def bases(lt, k, seen):
                pool.wait_ge(S["xn_ready"], lt + 1)
                if seen == 2:
                    pool.wait_ge(base_stored[k], 16 * before(lt, k))
                pool.tensor_tensor(base[k].rearrange("p (b d) -> p b d", b=B),
                                   xn[k].rearrange("p (b d) -> p b d", b=B),
                                   d_bc.unsqueeze(1).to_broadcast([P, B, D]), ALU.mult)\
                    .then_inc(S["xd_ready"], 1)
                pool.wait_ge(S["xd_ready"], lt + 1)
                pool.tensor_tensor(base[k], base[k], x_t[k], ALU.add).then_inc(S["base_ready"], 1)

            def start():
                rstds(0, 0)
                rstds(1, 1)
                bases(0, 0, 0)

            def step(lt, k, seen, more):
                if more:
                    bases(lt + 1, 1 - k, min(seen + 1, 2))
                if more == 2:
                    rstds(lt + 2, k)
                if seen == 0:
                    pool.wait_ge(S["a_stored"], 16 * TERMS)
                if seen:
                    pool.wait_ge(S["dlo_ready"], lt)
                pool.wait_ge(S["dhi_ready"], lt + 1)
                pool.tensor_tensor(dres, delta[k], dp_view(k)[:, 0], ALU.subtract)\
                    .then_inc(S["dres_ready"], 1)
                pool.wait_ge(S["dmid_ready"], lt + 1)
                pool.tensor_tensor(dp_view(k)[:, 2], dres, dp_view(k)[:, 1], ALU.subtract)\
                    .then_inc(S["dlo_ready"], 1)

            piped(pool, start, step)

            for k in range(2):
                pool.memset(c_sta[k][:, :], 0.0).then_inc(S["c_sta_zeroed"], 1)
            pool.wait_ge(S["c_sta_zeroed"], 2)
            pool.wait_ge(S["c_ready"], LT)
            pool.wait_ge(S["own_made"], 3)

            def m_pair(it, first, last):
                for k in range(2):
                    c = 2 * it + k
                    if not first:
                        pool.wait_ge(S["contract_done"], 2 * c - 2)
                    pool.tensor_tensor(
                        sub(c_sta[k], 0, P, 0, (4 * 32 + 4, TC // 4), (32, 4), (1, B)),
                        c_all[:, bass.ds(c * TC, TC)].rearrange("p (q j) -> p q j", j=4)
                        .unsqueeze(3).to_broadcast([P, TC // 4, 4, B]),
                        sub(own_batch, 0, P, 0, (0, TC // 4), (0, 4), (1, B)), ALU.mult)\
                        .then_inc(S["cpad_ready"], 1)
                    for s in range(SUBS):
                        for g in range(GROUPS):
                            G = c * STEPS + s * GROUPS + g
                            early = first and k == 0 and s == 0
                            if s == 0:
                                pool.wait_ge(S["exp_done"], c * UNITS + (g + 1) * (UNITS // GROUPS))
                            if not early:
                                pool.wait_ge(S["scan_done"], G - 3)
                                pool.wait_ge(S["carried"], G - 3)
                            seg = decay[k][:, (s * D + g * GD) * TS:(s * D + (g + 1) * GD) * TS]\
                                .rearrange("p (d t) -> p d t", t=TS)
                            before = state[1 - s][:, g * GD * TS:(g + 1) * GD * TS]\
                                .rearrange("p (d t) -> p d t", t=TS)
                            if early:
                                ins = pool.tensor_tensor(carry[:, g, :], zeros[:, :], zeros[:, :], ALU.add)
                            else:
                                ins = pool.tensor_tensor(carry[:, g, :], seg[:, :, 0], before[:, :, TS - 1], ALU.mult)
                            ins.then_inc(S["carry_ready"], 1)
                            pool.wait_ge(S["carry_ready"], G + 1)
                            pool.tensor_tensor(seg[:, :, 0], zeros[:, :], zeros[:, :], ALU.add)\
                                .then_inc(S["decay_reset"], 1)
                            if last and k == 0 and s == 0:
                                if g == 0:
                                    pool.wait_ge(S["args_ready"], (c + 1) * UNITS)
                                rope_table(pool, g)
                            if last and k == 0 and (s, g) == (1, 0):
                                causal_mask(pool)
                            if last and k == 1 and (s, g) == (0, 0):
                                pool.wait_ge(S["args_ready"], CHUNKS * UNITS)
                                routing_weights(pool)

            tiles(pool, CHUNKS // 2, m_pair)
            phase_f_pool(pool)

        @block.tensor
        def _(pe):
            pe.wait_ge(S["ident_ready"], 1)
            pe.wait_ge(S["weights_loaded"], 16 * 5)
            for h in range(2):
                nc.tensor.transpose(bank(6)[:, h * P:(h + 1) * P], w_bc_n[:, h * P:(h + 1) * P], ident[:, :])
                last = nc.tensor.transpose(bank(6)[0:R, 256 + h * P:256 + (h + 1) * P],
                                           w_dt_n[:, h * R:(h + 1) * R], ident[:, :])
            last.then_inc(S["wT_psum"], 1)
            pe.wait_ge(S["wT_ready"], 2)
            pe.wait_ge(S["ones_ready"], 1)

            def pair(it, first, last):
                for k in range(2):
                    lt = 2 * it + k
                    started = not (first and k == 0)
                    pe.wait_ge(S["xn_ready"], lt + 1)
                    if started:
                        pe.wait_ge(S["xnT_ready"], 2 * lt)
                    for h in range(2):
                        for b in range(B):
                            o = (h * B + b) * P
                            tr = nc.tensor.transpose(psum[:, o:o + P],
                                                     xn[k][:, b * D + h * P:b * D + (h + 1) * P], ident[:, :])
                        tr.then_inc(S["xnT_psum"], 1)
                    xT = xnT[k]
                    pe.wait_ge(S["xnT_ready"], 2 * lt + 2)
                    if started:
                        pe.wait_ge(S["dtr_ready"], lt)
                    for h in range(2):
                        mm = nc.tensor.matmul(bank(2)[0:R, :], w_bcT[:, h * P:h * P + R],
                                              xT[:, h * BANK:(h + 1) * BANK], start=(h == 0), stop=(h == 1))
                    mm.then_inc(S["dtr_psum"], 1)
                    if started:
                        pe.wait_ge(S["c_ready"], lt)
                        pe.wait_ge(S["blo_ready"], lt)
                    for b in range(B):
                        for h in range(2):
                            nc.tensor.matmul(bank(3)[N * b:N * b + N, 0:P],
                                             w_bcT[:, h * P + R + N:h * P + R + 2 * N],
                                             xT[:, h * BANK + b * P:h * BANK + (b + 1) * P],
                                             start=(h == 0), stop=(h == 1))
                    for b in range(B):
                        for h in range(2):
                            mm = nc.tensor.matmul(bank(6)[:, b * N:(b + 1) * N],
                                                  xT[:, h * BANK + b * P:h * BANK + (b + 1) * P],
                                                  w_bcT[:, h * P + R:h * P + R + N],
                                                  start=(h == 0), stop=(h == 1))
                    mm.then_inc(S["bc_psum"], 1)
                    pe.wait_ge(S["dtr_ready"], lt + 1)
                    if started:
                        pe.wait_ge(S["delta_ready"], lt)
                    for b in range(B):
                        o = psum[:, 4 * BANK + b * D:4 * BANK + (b + 1) * D]
                        mm = nc.tensor.matmul(o, dtr[k][0:R + 1, b * P:(b + 1) * P], w_dtT_b, start=True, stop=True)
                    mm.then_inc(S["dt_psum"], 1)

            tiles(pe, PAIRS, pair)

            pe.wait_ge(S["a_sta_loaded"], 16 * DQ * B)
            pe.wait_ge(S["delta_ready"], LT)

            def decay_args(c, k, u, started):
                if started:
                    pe.wait_ge(S["exp_done"], c * UNITS + u - 1)
                for i in range(UNIT_DG):
                    dg = u * UNIT_DG + i
                    mm = nc.tensor.matmul(
                        psum[:, (4 + u % 2) * BANK + i * P:(4 + u % 2) * BANK + (i + 1) * P],
                        a_sta[0:ROWS, dg * P:(dg + 1) * P],
                        sub(delta_mov[k], 0, ROWS, dg, (TC * DG, DQ), (DG, TC)), start=True, stop=True)
                mm.then_inc(S["args_ready"], 1)
                return mm

            def contract(c, k, s, quads):
                for qq in quads:
                    for j in range(4):
                        t = s * TS + 4 * qq + j
                        q = t // 4
                        mm = nc.tensor.matmul(
                            psum[32 * j:32 * j + 32, (6 + k) * BANK:(6 + k) * BANK + D],
                            c_sta[k][:, t * 32:(t + 1) * 32],
                            sub(arena, 0, P, (2 * CHUNK_ELEMS + s * D * TS) + 4 * qq + j,
                                (TS, DQ), (DQ * TS, DG)),
                            start=(q == 0), stop=(q == TC // 4 - 1), skip_group_check=True)
                return mm

            pe.wait_ge(md_loaded[0], 16 * MD_LOADS)
            for u in range(UNITS):
                mm = decay_args(0, 0, u, u >= 2)
            pe.wait_ge(S["c_ready"], LT)
            pe.wait_ge(S["blo_ready"], LT)

            def m_pair(it, first, last):
                for k in range(2):
                    c = 2 * it + k
                    pe.wait_ge(mu_loaded[k], 16 * MU_LOADS * (it + 1))
                    if not (last and k == 1):
                        pe.wait_ge(md_loaded[1 - k], 16 * MD_LOADS * (it + 1 + k))
                    for s in range(SUBS):
                        for g in range(GROUPS):
                            step = s * GROUPS + g
                            G = c * STEPS + step
                            pair_bank = 2 * (step % 2)
                            if not (first and k == 0 and step < 2):
                                pe.wait_ge(S["scan_done"], G - 1)
                            for tg in range(TS // 4):
                                for half in range(2):
                                    dg0 = g * (GD // DQ) + half * (GD // DQ // 2)
                                    o = (pair_bank + half) * BANK + tg
                                    mm = nc.tensor.matmul(
                                        sub(psum, 0, P, o, (DQ * TS, GD // DQ // 2), (TS, DQ), (4, 4)),
                                        b_sta[k][0:ROWS, (s * 4 + tg) * P:(s * 4 + tg + 1) * P],
                                        sub(du_mov[k], 0, ROWS, (s * 4 + tg) * D + dg0,
                                            (1, GD // DQ // 2), (DG, DQ), (DU_COLS, 4)),
                                        start=True, stop=True)
                            mm.then_inc(S["b_ready"], 1)
                            if not (last and k == 1):
                                for u in range(step * UNITS_PER_STEP, (step + 1) * UNITS_PER_STEP):
                                    mm = decay_args(c + 1, 1 - k, u, True)
                            if not (first and k == 0 and s == 0):
                                ps, pk, pc = (0, k, c) if s == 1 else (1, 1 - k, c - 1)
                                if g == 0:
                                    pe.wait_ge(S["scan_done"], G)
                                    if ps == 0:
                                        pe.wait_ge(S["cpad_ready"], c + 1)
                                        if not first:
                                            pe.wait_ge(S["y_evac"], c - 1)
                                mm = contract(pc, pk, ps, [g])
                                if g == 3:
                                    mm.then_inc(S["contract_done"], 1)
            tiles(pe, CHUNKS // 2, m_pair)
            routing_columns(pe)
            pe.wait_ge(S["scan_done"], CHUNKS * STEPS)
            contract(CHUNKS - 1, 1, 1, range(4)).then_inc(S["contract_done"], 1)
            phase_f_pe(pe)

        @block.scalar
        def _(act):
            act.wait_ge(S["wT_psum"], 1)
            nc.scalar.copy(w_bcT, bank(6)[:, 0:256]).then_inc(S["wT_ready"], 1)
            nc.scalar.copy(w_dtT, bank(6)[0:R, 256:512]).then_inc(S["wT_ready"], 1)
            nc.scalar.activation(a_neg, a_log_n, ACT.Exp).then_inc(S["a_exp"], 1)

            def xnTs(lt, k, seen):
                for h in range(2):
                    act.wait_ge(S["xnT_psum"], 2 * lt + h + 1)
                    if seen == 2 and h == 0:
                        act.wait_ge(S["bc_psum"], lt - 1)
                    nc.scalar.copy(xnT[k][:, h * BANK:(h + 1) * BANK], bank(h)).then_inc(S["xnT_ready"], 1)

            def projections(lt, k, seen):
                act.wait_ge(S["dtr_psum"], lt + 1)
                if seen == 2:
                    act.wait_ge(S["dt_psum"], lt - 1)
                nc.scalar.copy(dtr[k][0:R, :], bank(2)[0:R, :]).then_inc(S["dtr_ready"], 1)
                act.wait_ge(S["bc_psum"], lt + 1)
                nc.scalar.copy(c_all[:, bass.ds(lt * P, P)], bank(3)[:, 0:P]).then_inc(S["c_ready"], 1)

            def start():
                xnTs(0, 0, 0)
                act.wait_ge(S["ones_ready"], 1)
                projections(0, 0, 0)

            def step(lt, k, seen, more):
                act.wait_ge(S["dt_psum"], lt + 1)
                if seen:
                    act.wait_ge(S["delta_ready"], lt)
                nc.scalar.activation(sp, bank(4, 2), ACT.Abs).then_inc(S["sp_abs"], 1)
                act.wait_ge(S["sp_abs"], lt + 1)
                nc.scalar.activation(sp, sp, ACT.Exp, scale=-1.0).then_inc(S["sp_exp"], 1)
                if more:
                    xnTs(lt + 1, 1 - k, min(seen + 1, 2))
                act.wait_ge(S["sp_exp"], lt + 1)
                nc.scalar.activation(sp, sp, ACT.Ln, bias=1.0).then_inc(S["sp_ln"], 1)
                act.wait_ge(S["delta_ready"], lt + 1)
                if seen == 2:
                    act.wait_ge(delta_stored[k], 16 * TERMS * before(lt, k))
                nc.scalar.copy(dp_view(k)[:, 0], delta[k]).then_inc(S["dhi_ready"], 1)
                if more:
                    projections(lt + 1, 1 - k, min(seen + 1, 2))
                act.wait_ge(S["dres_ready"], lt + 1)
                nc.scalar.copy(dp_view(k)[:, 1], dres).then_inc(S["dmid_ready"], 1)

            piped(act, start, step)

            act.wait_ge(S["du_ready"], LT)
            act.wait_ge(S["base_ready"], LT)

            def exps(c, k, u):
                act.wait_ge(S["args_ready"], c * UNITS + u + 1)
                nc.scalar.activation(
                    sub(arena, 0, P, k * CHUNK_ELEMS + u * 16 * TS, (TS, 16), (D * TS, SUBS), (1, TS)),
                    sub(psum, 0, P, (4 + u % 2) * BANK, (TC, 16), (TS, SUBS), (1, TS)), ACT.Exp)\
                    .then_inc(S["exp_done"], 1)

            for u in range(UNITS):
                exps(0, 0, u)
            act.wait_ge(S["dlo_ready"], LT)
            act.wait_ge(S["ulo_ready"], LT)
            for k in range(2):
                act.wait_ge(base_stored[k], 16 * PAIRS)

            def m_pair(it, first, last):
                for k in range(2):
                    c = 2 * it + k
                    for step in range(STEPS):
                        if not (last and k == 1):
                            if step == 0 and not (first and k == 0):
                                act.wait_ge(S["scan_done"], c * STEPS)
                            for u in range(step * UNITS_PER_STEP, (step + 1) * UNITS_PER_STEP):
                                exps(c + 1, 1 - k, u)
                        if step == 4 and not (first and k == 0):
                            act.wait_ge(S["contract_done"], 2 * c)
                            n = it - 1 if k == 0 else it
                            if not (isinstance(n, int) and n <= 0):
                                act.wait_ge(y_stored[1 - k], 64 * n)
                            nc.scalar.copy(y_rows[1 - k][:, :],
                                           bank(7 - k)[:, 0:D])\
                                .then_inc(S["y_evac"], 1)

            m_pair(0, True, False)
            m_pair(1, False, False)
            with act.Fori(2, CHUNKS // 2 - 1) as it:
                m_pair(it, False, False)
            m_pair(CHUNKS // 2 - 1, False, True)
            copy_routing_columns(act)
            act.wait_ge(S["contract_done"], 2 * CHUNKS)
            act.wait_ge(y_stored[1], 64 * (CHUNKS // 2 - 1))
            nc.scalar.copy(y_rows[1][:, :], bank(7)[:, 0:D]).then_inc(S["y_evac"], 1)
            phase_f_act(act)

        @block.vector
        def _(dve):
            def zero(t):
                nc.vector.memset(t[:, :].bitcast(F32), 0.0).then_inc(S["zeros_ready"], 1)

            zero(delta_mov[0])
            ZERO_AT = {3: du_mov[0], 2: delta_mov[1], 1: du_mov[1]}
            def statistics(lt, k):
                xv = x_t[k].rearrange("p (b d) -> p b d", b=B)
                dve.wait_ge(x_loaded[k], 16 * (before(lt, k) + 1))
                for b in range(B):
                    ins = nc.vector.bn_stats(stats[:, 24 * k + 6 * b:24 * k + 6 * b + 6], xv[:, b, :])
                ins.then_inc(S["stats_done"], 1)
                dve.wait_ge(S["stats_done"], lt + 1)
                nc.vector.memset(pacer[:, :], 0.0)
                for b in range(B):
                    ins = nc.vector.bn_aggr(mv[:, 8 * k + 2 * b:8 * k + 2 * b + 2],
                                            stats[:, 24 * k + 6 * b:24 * k + 6 * b + 6])
                ins.then_inc(S["var_done"], 1)
                dve.wait_ge(S["var_done"], lt + 1)
                nc.vector.tensor_scalar(veps[:, 4 * k:4 * k + 4], mv[:, 8 * k + 1:8 * k + 8:2], EPS, None,
                                        ALU.add).then_inc(S["veps_ready"], 1)

            def normalise(lt, k, seen):
                xv = x_t[k].rearrange("p (b d) -> p b d", b=B)
                dve.wait_ge(S["rstd_ready"], lt + 1)
                if seen == 2:
                    dve.wait_ge(S["xnT_psum"], 2 * lt - 2)
                    dve.wait_ge(S["xd_ready"], lt - 1)
                for b in range(B):
                    ins = nc.vector.tensor_scalar(xn[k][:, b * D:(b + 1) * D], xv[:, b, :],
                                                  mv[:, 8 * k + 2 * b:8 * k + 2 * b + 1],
                                                  rstd[:, 4 * k + b:4 * k + b + 1], ALU.subtract, ALU.mult)
                ins.then_inc(S["xn_ready"], 1)

            def b_split(lt, k, seen):
                bpsum = bank(6)[:, 0:P]
                dve.wait_ge(S["bc_psum"], lt + 1)
                if seen == 2:
                    dve.wait_ge(b_stored[k], 16 * TERMS * before(lt, k))
                nc.vector.tensor_copy(bp_view(k)[:, 0], bpsum).then_inc(S["bhi_ready"], 1)
                dve.wait_ge(S["bhi_ready"], lt + 1)
                nc.vector.tensor_tensor(bres, bpsum, bp_view(k)[:, 0], ALU.subtract)\
                    .then_inc(S["bres_ready"], 1)
                dve.wait_ge(S["bres_ready"], lt + 1)
                nc.vector.tensor_copy(bp_view(k)[:, 1], bres).then_inc(S["bmid_ready"], 1)
                dve.wait_ge(S["bmid_ready"], lt + 1)
                nc.vector.tensor_tensor(bp_view(k)[:, 2], bres, bp_view(k)[:, 1], ALU.subtract)\
                    .then_inc(S["blo_ready"], 1)

            def split_a():
                pv = a_parts.rearrange("p (s n) -> p s n", s=3)
                dve.wait_ge(S["a_exp"], 1)
                nc.vector.tensor_scalar(a_neg, a_neg, -1.0, None, ALU.mult).then_inc(S["a_neg"], 1)
                dve.wait_ge(S["a_neg"], 1)
                nc.vector.tensor_copy(pv[:, 0], a_neg).then_inc(S["a_hi"], 1)
                dve.wait_ge(S["a_hi"], 1)
                nc.vector.tensor_tensor(a_res, a_neg, pv[:, 0], ALU.subtract).then_inc(S["a_res"], 1)
                dve.wait_ge(S["a_res"], 1)
                nc.vector.tensor_copy(pv[:, 1], a_res).then_inc(S["a_mid"], 1)
                dve.wait_ge(S["a_mid"], 1)
                nc.vector.tensor_tensor(pv[:, 2], a_res, pv[:, 1], ALU.subtract).then_inc(S["a_mid"], 1)

            def start():
                statistics(0, 0)
                split_a()
                normalise(0, 0, 0)
                statistics(1, 1)
                normalise(1, 1, 0)
                b_split(0, 0, 0)

            def step(lt, k, seen, more):
                if more >= 2 and seen:
                    statistics(lt + 2, k)
                dve.wait_ge(S["sp_ln"], lt + 1)
                if seen == 2:
                    dve.wait_ge(S["dlo_ready"], lt - 1)
                nc.vector.scalar_tensor_tensor(out=delta[k], in0=bank(4, 2), scalar=0.0, in1=sp,
                                               op0=ALU.max, op1=ALU.add).then_inc(S["delta_ready"], 1)
                dve.wait_ge(S["delta_ready"], lt + 1)
                nc.vector.tensor_tensor(du[k], delta[k], xn[k], ALU.mult).then_inc(S["du_ready"], 1)
                dve.wait_ge(S["du_ready"], lt + 1)
                if seen == 0:
                    statistics(2, 0)
                if more >= 2:
                    normalise(lt + 2, k, 2)
                if seen == 2:
                    dve.wait_ge(du_stored[k], 16 * TERMS * before(lt, k))
                nc.vector.tensor_copy(up_view(k)[:, 0], du[k]).then_inc(S["uhi_ready"], 1)
                dve.wait_ge(S["uhi_ready"], lt + 1)
                nc.vector.tensor_tensor(ures, du[k], up_view(k)[:, 0], ALU.subtract)\
                    .then_inc(S["ures_ready"], 1)
                dve.wait_ge(S["ures_ready"], lt + 1)
                nc.vector.tensor_copy(up_view(k)[:, 1], ures).then_inc(S["umid_ready"], 1)
                dve.wait_ge(S["umid_ready"], lt + 1)
                nc.vector.tensor_tensor(up_view(k)[:, 2], ures, up_view(k)[:, 1], ALU.subtract)\
                    .then_inc(S["ulo_ready"], 1)
                if more:
                    b_split(lt + 1, 1 - k, min(seen + 1, 2))
                if more in ZERO_AT:
                    zero(ZERO_AT[more])

            piped(dve, start, step, 1, 4)

            for k in range(2):
                dve.wait_ge(delta_stored[k], 16 * TERMS * PAIRS)
            dve.wait_ge(du_stored[0], 16 * TERMS * PAIRS)

            def m_pair(it, first, last):
                for k in range(2):
                    c = 2 * it + k
                    for s in range(SUBS):
                        if first and k == 0 and s == 1:
                            p_done(dve)
                        for g in range(GROUPS):
                            step = s * GROUPS + g
                            G = c * STEPS + step
                            dve.wait_ge(S["decay_reset"], G + 1)
                            dve.wait_ge(S["b_ready"], G + 1)
                            if g == 0 and not (first and k == 0):
                                dve.wait_ge(S["contract_done"], 2 * c + s - 1)
                            seg = slice(g * GD * TS, (g + 1) * GD * TS)
                            firsts = sub(psum, 0, P, 2 * (step % 2) * BANK, (TS, GD))
                            nc.vector.tensor_tensor(firsts, firsts, carry[:, g, :], ALU.add)\
                                .then_inc(S["carried"], 1)
                            dve.wait_ge(S["carried"], G + 1)
                            nc.vector.tensor_tensor_scan(
                                state[s][:, seg], decay[k][:, (s * D + g * GD) * TS:(s * D + (g + 1) * GD) * TS],
                                psum[:, 2 * (step % 2) * BANK:(2 * (step % 2) + 2) * BANK], 0.0,
                                ALU.mult, ALU.add).then_inc(S["scan_done"], 1)

            tiles(dve, CHUNKS // 2, m_pair)
            phase_f_dve(dve)


_INS = ["L0_attn_x", "L0_attn_W_bc", "L0_attn_W_dt", "L0_attn_b_dt", "L0_attn_A_log", "L0_attn_D_param",
        "L0_ffn_conv_w", "L0_ffn_Wq", "L0_ffn_Wk", "L0_ffn_Wv", "L0_ffn_Wg", "L0_ffn_router_w", "L0_ffn_Wout"]


def kernel(**inputs):
    import numpy as _np
    import concourse.bacc as _bacc
    from concourse.bass_utils import run_bass_kernel_spmd as _run

    nc = _bacc.Bacc("TRN2", target_bir_lowering=False, num_devices=1)
    arrays, args = {}, []
    for name in _INS:
        a = _np.ascontiguousarray(inputs[name])
        arrays[f"in_{name}"] = a
        args.append(nc.dram_tensor(f"in_{name}", a.shape, F32, kind="ExternalInput").ap())
    out = nc.dram_tensor("out_0", (B, L, D), F32, kind="ExternalOutput").ap()
    build(nc, *args, out)
    r = _run(nc, [arrays], core_ids=[0])
    return r.results[0]["out_0"]
```
